# Optimizing a Trainium2 kernel written in Bass

```python
import numpy as np
import jax
import jax.numpy as jnp

def _softmax(x, axis=-1):
    return jax.nn.softmax(x, axis=axis)

def _gelu(x):
    return jax.nn.gelu(x, approximate=True)

def _silu(x):
    return jax.nn.silu(x)

def _sigmoid(x):
    return jax.nn.sigmoid(x)

def _layernorm(x, axis=-1, eps=1e-05):
    m = jnp.mean(x, axis=axis, keepdims=True)
    v = jnp.var(x, axis=axis, keepdims=True)
    return (x - m) / jnp.sqrt(v + eps)

def _scatter_add(tgt, idx, src, axis=0):
    return tgt.at[idx].add(src)

def _segment_sum(src, seg, n):
    return jax.ops.segment_sum(src, seg, n)
kernel_name = 'mk_conv_seq_d2_conv_nchw96_r2_7472c2'

def setup_inputs(seed: int=0):
    np.random.seed(seed)
    _w = jnp.asarray

    def _rec_inputs():
        import jax
        import jax.numpy as jnp
        _gk = jax.random.key(seed)
        x = -0.0001667 + 0.9999 * jax.random.normal(jax.random.fold_in(_gk, 1), (8, 48, 96, 96), jnp.float32)
        return x
    x = _rec_inputs()

    def _L0_conv_setup():
        import jax, jax.numpy as jnp
        import numpy as np
        from jax import lax
        B, C, H, W = (8, 48, 96, 96)
        HC = 48
        EPS = 1e-05

        def _convlstm_scan(x_rows, w_mid, b, reverse):
            hc = w_mid.shape[0] // 4
            dn = ('NCH', 'OIH', 'NCH')

            def step(carry, xr):
                h, c = carry
                inp = jnp.concatenate([xr, h], axis=1)
                gates = lax.conv_general_dilated(inp, w_mid, (1,), 'SAME', dimension_numbers=dn) + b[None, :, None]
                i, f, g, o = jnp.split(gates, 4, axis=1)
                c2 = jax.nn.sigmoid(f) * c + jax.nn.sigmoid(i) * jnp.tanh(g)
                h2 = jax.nn.sigmoid(o) * jnp.tanh(c2)
                return ((h2, c2), h2)
            z = jnp.zeros((x_rows.shape[1], hc, x_rows.shape[3]), x_rows.dtype)
            _, hs = lax.scan(step, (z, z), x_rows, reverse=reverse)
            return hs
        key = jax.random.key(seed)
        ks = jax.random.split(key, 6)
        s = 0.05
        x = jax.random.normal(ks[0], (B, C, H, W), jnp.float32)
        w_f = jax.random.normal(ks[1], (4 * HC, C + HC, 3, 3), jnp.float32) * s
        b_f = jnp.zeros((4 * HC,), jnp.float32)
        w_b = jax.random.normal(ks[2], (4 * HC, C + HC, 3, 3), jnp.float32) * s
        b_b = jnp.zeros((4 * HC,), jnp.float32)
        w_proj = jax.random.normal(ks[3], (C, 2 * HC), jnp.float32) * s
        gamma = jnp.ones((C,), jnp.float32)
        beta = jnp.zeros((C,), jnp.float32)
        return {'x': x, 'w_f': w_f, 'b_f': b_f, 'w_b': w_b, 'b_b': b_b, 'w_proj': w_proj, 'gamma': gamma, 'beta': beta}
    _L0_conv_all = _L0_conv_setup()
    _L0_conv_in = {k: v for k, v in _L0_conv_all.items() if k in ('w_f', 'b_f', 'w_b', 'b_b', 'w_proj', 'gamma', 'beta')}
    del _L0_conv_all

    def _L1_conv_setup():
        import jax, jax.numpy as jnp
        import numpy as np
        from jax import lax
        INP, HID, OUP = (48, 288, 48)
        BUDGET = 0.5
        EPS = 1e-05

        def _bn(x, g, b, m, v):
            scale = (g / jnp.sqrt(v + EPS))[None, :, None, None]
            return x * scale + (b - m * g / jnp.sqrt(v + EPS))[None, :, None, None]

        def _conv1x1(x, w):
            return jnp.einsum('oi,bihw->bohw', w, x)

        def _dwconv3x3(x, w):
            c = x.shape[1]
            return lax.conv_general_dilated(x, w, window_strides=(1, 1), padding='SAME', dimension_numbers=('NCHW', 'OIHW', 'NCHW'), feature_group_count=c)

        def _maxpool3x3(m):
            return lax.reduce_window(m, -jnp.inf, lax.max, (1, 1, 3, 3), (1, 1, 1, 1), 'SAME')
        key = jax.random.key(seed)
        ks = jax.random.split(key, 16)
        d = {}
        d['x'] = jax.random.normal(ks[0], (16, INP, 56, 56), jnp.float32)
        d['w_pw1'] = jax.random.normal(ks[1], (HID, INP), jnp.float32) * 0.1
        d['bn1_g'] = jax.random.uniform(ks[2], (HID,), jnp.float32)
        d['bn1_b'] = jax.random.normal(ks[3], (HID,), jnp.float32) * 0.1
        d['bn1_m'] = jax.random.normal(ks[4], (HID,), jnp.float32) * 0.1
        d['bn1_v'] = jax.random.uniform(ks[5], (HID,), jnp.float32) + 0.5
        d['w_dw'] = jax.random.normal(ks[6], (HID, 1, 3, 3), jnp.float32) * 0.2
        d['bnd_g'] = jax.random.uniform(ks[7], (HID,), jnp.float32)
        d['bnd_b'] = jax.random.normal(ks[8], (HID,), jnp.float32) * 0.1
        d['bnd_m'] = jax.random.normal(ks[9], (HID,), jnp.float32) * 0.1
        d['bnd_v'] = jax.random.uniform(ks[10], (HID,), jnp.float32) + 0.5
        d['w_pw2'] = jax.random.normal(ks[11], (OUP, HID), jnp.float32) * 0.05
        d['bn2_g'] = jax.random.uniform(ks[12], (OUP,), jnp.float32)
        d['bn2_b'] = jax.random.normal(ks[13], (OUP,), jnp.float32) * 0.1
        d['bn2_m'] = jax.random.normal(ks[14], (OUP,), jnp.float32) * 0.1
        d['bn2_v'] = jax.random.uniform(ks[15], (OUP,), jnp.float32) + 0.5
        k2 = jax.random.split(jax.random.fold_in(key, 1), 2)
        d['w_mask'] = jax.random.normal(k2[0], (1, INP), jnp.float32) * 0.3
        d['b_mask'] = jnp.zeros((1,), jnp.float32)
        d['w_sal'] = jax.random.normal(k2[1], (HID, INP), jnp.float32) * 0.3
        d['b_sal'] = jnp.zeros((HID,), jnp.float32)
        return d
    _L1_conv_all = _L1_conv_setup()
    _L1_conv_in = {k: v for k, v in _L1_conv_all.items() if k in ('w_pw1', 'bn1_g', 'bn1_b', 'bn1_m', 'bn1_v', 'w_dw', 'bnd_g', 'bnd_b', 'bnd_m', 'bnd_v', 'w_pw2', 'bn2_g', 'bn2_b', 'bn2_m', 'bn2_v', 'w_mask', 'b_mask', 'w_sal', 'b_sal')}
    del _L1_conv_all
    return {'x': x, 'L0_conv_w_f': _L0_conv_in['w_f'], 'L0_conv_b_f': _L0_conv_in['b_f'], 'L0_conv_w_b': _L0_conv_in['w_b'], 'L0_conv_b_b': _L0_conv_in['b_b'], 'L0_conv_w_proj': _L0_conv_in['w_proj'], 'L0_conv_gamma': _L0_conv_in['gamma'], 'L0_conv_beta': _L0_conv_in['beta'], 'L1_conv_w_pw1': _L1_conv_in['w_pw1'], 'L1_conv_bn1_g': _L1_conv_in['bn1_g'], 'L1_conv_bn1_b': _L1_conv_in['bn1_b'], 'L1_conv_bn1_m': _L1_conv_in['bn1_m'], 'L1_conv_bn1_v': _L1_conv_in['bn1_v'], 'L1_conv_w_dw': _L1_conv_in['w_dw'], 'L1_conv_bnd_g': _L1_conv_in['bnd_g'], 'L1_conv_bnd_b': _L1_conv_in['bnd_b'], 'L1_conv_bnd_m': _L1_conv_in['bnd_m'], 'L1_conv_bnd_v': _L1_conv_in['bnd_v'], 'L1_conv_w_pw2': _L1_conv_in['w_pw2'], 'L1_conv_bn2_g': _L1_conv_in['bn2_g'], 'L1_conv_bn2_b': _L1_conv_in['bn2_b'], 'L1_conv_bn2_m': _L1_conv_in['bn2_m'], 'L1_conv_bn2_v': _L1_conv_in['bn2_v'], 'L1_conv_w_mask': _L1_conv_in['w_mask'], 'L1_conv_b_mask': _L1_conv_in['b_mask'], 'L1_conv_w_sal': _L1_conv_in['w_sal'], 'L1_conv_b_sal': _L1_conv_in['b_sal']}

def reference(x, L0_conv_w_f, L0_conv_b_f, L0_conv_w_b, L0_conv_b_b, L0_conv_w_proj, L0_conv_gamma, L0_conv_beta, L1_conv_w_pw1, L1_conv_bn1_g, L1_conv_bn1_b, L1_conv_bn1_m, L1_conv_bn1_v, L1_conv_w_dw, L1_conv_bnd_g, L1_conv_bnd_b, L1_conv_bnd_m, L1_conv_bnd_v, L1_conv_w_pw2, L1_conv_bn2_g, L1_conv_bn2_b, L1_conv_bn2_m, L1_conv_bn2_v, L1_conv_w_mask, L1_conv_b_mask, L1_conv_w_sal, L1_conv_b_sal):
    import jax
    import jax.numpy as jnp

    def _L0_conv_ref(x, w_f, b_f, w_b, b_b, w_proj, gamma, beta):
        import jax, jax.numpy as jnp
        import numpy as np
        from jax import lax
        B, C, H, W = (8, 48, 96, 96)
        HC = 48
        EPS = 1e-05

        def _convlstm_scan(x_rows, w_mid, b, reverse):
            hc = w_mid.shape[0] // 4
            dn = ('NCH', 'OIH', 'NCH')

            def step(carry, xr):
                h, c = carry
                inp = jnp.concatenate([xr, h], axis=1)
                gates = lax.conv_general_dilated(inp, w_mid, (1,), 'SAME', dimension_numbers=dn) + b[None, :, None]
                i, f, g, o = jnp.split(gates, 4, axis=1)
                c2 = jax.nn.sigmoid(f) * c + jax.nn.sigmoid(i) * jnp.tanh(g)
                h2 = jax.nn.sigmoid(o) * jnp.tanh(c2)
                return ((h2, c2), h2)
            z = jnp.zeros((x_rows.shape[1], hc, x_rows.shape[3]), x_rows.dtype)
            _, hs = lax.scan(step, (z, z), x_rows, reverse=reverse)
            return hs
        xr = jnp.transpose(x, (2, 0, 1, 3))
        hs_f = _convlstm_scan(xr, w_f[:, :, 1, :], b_f, reverse=False)
        hs_b = _convlstm_scan(xr, w_b[:, :, 1, :], b_b, reverse=True)
        feats = jnp.concatenate([hs_f, hs_b], axis=2)
        feats = jnp.transpose(feats, (1, 2, 0, 3))
        y = jnp.einsum('oc,bchw->bohw', w_proj, feats)
        mu = jnp.mean(y, axis=(0, 2, 3))
        var = jnp.var(y, axis=(0, 2, 3))
        yn = (y - mu[None, :, None, None]) * lax.rsqrt(var + EPS)[None, :, None, None]
        y = gamma[None, :, None, None] * yn + beta[None, :, None, None]
        return jax.nn.relu(y) + x

    def _L1_conv_ref(x, w_pw1, bn1_g, bn1_b, bn1_m, bn1_v, w_dw, bnd_g, bnd_b, bnd_m, bnd_v, w_pw2, bn2_g, bn2_b, bn2_m, bn2_v, w_mask, b_mask, w_sal, b_sal):
        import jax, jax.numpy as jnp
        import numpy as np
        from jax import lax
        INP, HID, OUP = (48, 288, 48)
        BUDGET = 0.5
        EPS = 1e-05

        def _bn(x, g, b, m, v):
            scale = (g / jnp.sqrt(v + EPS))[None, :, None, None]
            return x * scale + (b - m * g / jnp.sqrt(v + EPS))[None, :, None, None]

        def _conv1x1(x, w):
            return jnp.einsum('oi,bihw->bohw', w, x)

        def _dwconv3x3(x, w):
            c = x.shape[1]
            return lax.conv_general_dilated(x, w, window_strides=(1, 1), padding='SAME', dimension_numbers=('NCHW', 'OIHW', 'NCHW'), feature_group_count=c)

        def _maxpool3x3(m):
            return lax.reduce_window(m, -jnp.inf, lax.max, (1, 1, 3, 3), (1, 1, 1, 1), 'SAME')
        logits = _conv1x1(x, w_mask) + b_mask[None, :, None, None]
        mask = (logits >= 0).astype(x.dtype)
        mask_dilate = _maxpool3x3(mask)
        pooled = jnp.mean(x, axis=(2, 3))
        s = jax.nn.sigmoid(pooled @ w_sal.T + b_sal)
        k = int(round(BUDGET * HID))
        thr = lax.top_k(s, k)[0][:, -1:]
        vector = (s >= thr).astype(x.dtype)
        h = jax.nn.relu(_bn(_conv1x1(x, w_pw1), bn1_g, bn1_b, bn1_m, bn1_v)) * mask_dilate
        h = h * vector[:, :, None, None]
        h = jax.nn.relu(_bn(_dwconv3x3(h, w_dw), bnd_g, bnd_b, bnd_m, bnd_v)) * mask
        h = h * vector[:, :, None, None]
        h = _bn(_conv1x1(h, w_pw2), bn2_g, bn2_b, bn2_m, bn2_v) * mask
        return x + h

    def _gn(v, G=32, eps=1e-05):
        B_, C_, H_, W_ = v.shape
        g = v.reshape(B_, G, C_ // G, H_, W_)
        m = jnp.mean(g, axis=(2, 3, 4), keepdims=True)
        s = jnp.var(g, axis=(2, 3, 4), keepdims=True)
        return ((g - m) / jnp.sqrt(s + eps)).reshape(v.shape)

    def _ln_c(v, eps=1e-06):
        m = jnp.mean(v, axis=1, keepdims=True)
        s = jnp.var(v, axis=1, keepdims=True)
        return (v - m) / jnp.sqrt(s + eps)

    def _ln_t(v, eps=1e-05):
        m = jnp.mean(v, axis=-1, keepdims=True)
        s = jnp.var(v, axis=-1, keepdims=True)
        return (v - m) / jnp.sqrt(s + eps)

    def _to_tokens(v):
        B_, C_, H_, W_ = v.shape
        return v.reshape(B_, C_, H_ * W_).transpose(0, 2, 1)

    def _from_tokens(t, like):
        B_, C_, H_, W_ = like.shape
        return t.transpose(0, 2, 1).reshape(B_, C_, H_, W_)
    x = _L0_conv_ref(x, L0_conv_w_f, L0_conv_b_f, L0_conv_w_b, L0_conv_b_b, L0_conv_w_proj, L0_conv_gamma, L0_conv_beta)
    x = _L1_conv_ref(x, L1_conv_w_pw1, L1_conv_bn1_g, L1_conv_bn1_b, L1_conv_bn1_m, L1_conv_bn1_v, L1_conv_w_dw, L1_conv_bnd_g, L1_conv_bnd_b, L1_conv_bnd_m, L1_conv_bnd_v, L1_conv_w_pw2, L1_conv_bn2_g, L1_conv_bn2_b, L1_conv_bn2_m, L1_conv_bn2_v, L1_conv_w_mask, L1_conv_b_mask, L1_conv_w_sal, L1_conv_b_sal)
    return x

_drawn_inputs = setup_inputs


def setup_inputs(seed=0):
    import zlib

    import numpy as np

    out = dict(_drawn_inputs(seed))
    spreads = {'L0_conv_b_f': (0.0, 0.1),
     'L0_conv_b_b': (0.0, 0.1),
     'L0_conv_gamma': (1.0, 0.2),
     'L0_conv_beta': (0.0, 0.1),
     'L1_conv_b_sal': (0.0, 0.8)}
    factors = {'L1_conv_w_pw1': 3.386,
     'L1_conv_bn1_g': 3.775,
     'L1_conv_bn1_b': 8.0,
     'L1_conv_bn1_m': 8.0,
     'L1_conv_bn1_v': 8.0,
     'L1_conv_bnd_g': 4.882,
     'L1_conv_bnd_b': 3.637,
     'L1_conv_bnd_m': 6.275,
     'L1_conv_bnd_v': 8.0,
     'L1_conv_bn2_g': 2.881,
     'L1_conv_bn2_v': 8.0,
     'L1_conv_w_sal': 3.112}
    for name, (base, spread) in spreads.items():
        noise = np.random.default_rng([zlib.crc32(name.encode()), seed]).standard_normal(out[name].shape)
        drawn = base * np.exp(spread * noise) if base else spread * noise
        out[name] = jnp.asarray(drawn.astype(out[name].dtype))
    for name, factor in factors.items():
        out[name] = (out[name] * factor).astype(out[name].dtype)
    return out
```

```python
from contextlib import ExitStack

import numpy as np

import concourse.bass as bass
from concourse import mybir

F32 = mybir.dt.float32
F32R = mybir.dt.float32r
I32 = mybir.dt.int32
ACT = mybir.ActivationFunctionType
ALU = mybir.AluOpType
AX = mybir.AxisListType

B, C, H, W = 8, 48, 96, 96
HB = B // 2
HC = 48
HID = 288
P = 128
LO, HI = 0, 64
PX = H * W
NH = HB * W
WP = W + 2
HG = 96
NG = HID // HG
TOPK = 144
EPS = 1e-5
S1, T1, TAP, SD, TD, W2, NPAR = 0, 1, 2, 11, 12, 13, 64
UNITS = 3
UC = 64
PE_TAPS = [0, 1]
ACT_TAPS = [2, 3]
DVE_TAPS = [4, 5, 6, 7, 8]
CH = 8
CPX = CH * W
NCH = H // CH
PKR = 2 * UNITS * P
PKF = UNITS * P + UNITS * len(PE_TAPS) * P + UNITS * 13 + 2
PK_DIAG = UNITS * P
PK_PAR = PK_DIAG + UNITS * len(PE_TAPS) * P
PK_S2 = PK_PAR + UNITS * 13


def at_least(eng, sem, value):
    if not isinstance(value, int) or value > 0:
        eng.wait_ge(sem, value)


def recurrence(nc, x_rows, w_gates, h_rows):
    STEPS = H
    with ExitStack() as ctx:
        def sb(name, shape, dt=F32):
            return ctx.enter_context(nc.sbuf_tensor(name, shape, dt))

        def sem(name):
            return ctx.enter_context(nc.semaphore(name))

        w_raw = sb("w_raw", [P, 12, P])
        w_hi = sb("w_hi", [P, 12, P], F32R)
        w_lo = sb("w_lo", [P, 12, P], F32R)
        top = [[sb(f"top{d}{e}", [P, B, WP], F32R) for e in range(2)] for d in range(2)]
        rest = [[sb(f"rest{d}{e}", [P, B, WP], F32R) for e in range(2)] for d in range(2)]
        x_raw = [[sb(f"x_raw{d}{e}", [P, B, W]) for e in range(2)] for d in range(2)]
        sig_if = [sb(f"sig_if{g}", [P, HB, W]) for g in range(4)]
        tanh_g = [sb(f"tanh_g{g}", [P, HB, W]) for g in range(4)]
        sig_o = [sb(f"sig_o{g}", [P, HB, W]) for g in range(4)]
        i_g = [sb(f"i_g{g}", [P, HB, W]) for g in range(4)]
        f_c = [sb(f"f_c{g}", [P, HB, W]) for g in range(4)]
        cell = [sb(f"cell{g}", [P, HB, W]) for g in range(4)]
        tanh_c = [sb(f"tanh_c{g}", [P, HB, W]) for g in range(4)]
        h_new = [[sb(f"h_new{g}{e}", [P, HB, W]) for e in range(2)] for g in range(4)]
        gates = [ctx.enter_context(nc.psum_tensor(f"gates{k}", [P, 2, 512], F32)) for k in range(2)]

        w_loaded, w_split = sem("w_loaded"), sem("w_split")
        x_loaded = [[sem(f"x_loaded{d}{e}") for e in range(2)] for d in range(2)]
        h_stored = [[sem(f"h_stored{g}{e}") for e in range(2)] for g in range(4)]
        zeroed, cells_zero = sem("zeroed"), sem("cells_zero")
        x_high, x_low = sem("x_high"), sem("x_low")
        if_summed, go_summed = sem("if_summed"), sem("go_summed")
        sif_ready, tg_ready, so_ready, tc_ready = (sem(n) for n in ("sif_ready", "tg_ready", "so_ready", "tc_ready"))
        ig_fc_ready = sem("ig_fc_ready")
        cell_ready, h_ready, hi_ready, lo_ready = (sem(n) for n in ("cell_ready", "h_ready", "hi_ready", "lo_ready"))

        def halves(g):
            return slice(HB * (g // 2), HB * (g // 2) + HB)

        def row(d, t):
            return t if d == 0 else t * -1 + (H - 1)

        block = ctx.enter_context(nc.Block())

        def turns(eng, body):
            body(0, True, False)
            with eng.Fori(1, STEPS // 2 - 1) as i:
                body(i, False, False)
            body(STEPS // 2 - 1, False, True)

        @block.sync
        def _(sp):
            sp.dma_start(w_raw[:], w_gates).then_inc(w_loaded, 16)
            for t in range(2):
                for d in range(2):
                    sp.dma_start(x_raw[d][t][HI:HI + C], x_rows[row(d, t)]).then_inc(x_loaded[d][t], 16)

            def store(t, e, g):
                sp.wait_ge(h_ready, 4 * t + g + 1)
                sp.dma_start(h_rows[row(g % 2, t), g % 2, :, halves(g), :],
                             h_new[g][e][0:HC]).then_inc(h_stored[g][e], 16)

            def body(i, first, last):
                for e in range(2):
                    t = 2 * i + e
                    if not last:
                        for d in range(2):
                            sp.wait_ge(x_low, 2 * t + d + 1)
                            sp.dma_start(x_raw[d][e][HI:HI + C],
                                         x_rows[row(d, t + 2)]).then_inc(x_loaded[d][e], 16)
                    for g in range(4):
                        store(t, e, g)

            turns(sp, body)
            for g in range(4):
                for e in range(2):
                    sp.wait_ge(h_stored[g][e], 16 * STEPS // 2)

        @block.tensor
        def _(pe):
            pe.wait_ge(w_split, 2)
            pe.wait_ge(zeroed, 1)

            def body(i, first, last):
                for k in range(8):
                    e, g = k // 4, k % 4
                    d = g % 2
                    t, s = 2 * i + e, 8 * i + k
                    pe.wait_ge(x_low, 2 * t + d + 1)
                    at_least(pe, hi_ready, s - 3)
                    at_least(pe, lo_ready, s - 3)
                    at_least(pe, so_ready, s - 1)
                    for m in range(2):
                        n = 0
                        for tap in range(3):
                            at = (d * 3 + tap) * 2 + m
                            a = top[d][e][0:112, halves(g), tap:tap + W]
                            b = rest[d][e][0:112, halves(g), tap:tap + W]
                            for w, v in ((w_hi, a), (w_lo, a), (w_hi, b)):
                                mm = nc.tensor.matmul(gates[k % 2][:, m, 0:NH], w[0:112, at, :], v,
                                                      start=(n == 0), stop=(n == 8))
                                n += 1
                        mm.then_inc(go_summed if m else if_summed, 1)

            turns(pe, body)

        @block.scalar
        def _(act):
            def gates_in(s, k):
                act.wait_ge(if_summed, s + 1)
                nc.scalar.activation(sig_if[k % 4][:], gates[k % 2][:, 0, 0:NH], ACT.Sigmoid).then_inc(sif_ready, 1)

            def gates_out(s, k):
                act.wait_ge(go_summed, s + 1)
                nc.scalar.activation(tanh_g[k % 4][0:HC], gates[k % 2][0:HC, 1, 0:NH], ACT.Tanh).then_inc(tg_ready, 1)
                nc.scalar.activation(sig_o[k % 4][HI:HI + HC], gates[k % 2][HI:HI + HC, 1, 0:NH],
                                     ACT.Sigmoid).then_inc(so_ready, 1)

            def cell_out(s, k):
                act.wait_ge(cell_ready, s + 1)
                nc.scalar.activation(tanh_c[k % 4][HI:HI + HC], cell[k % 4][HI:HI + HC], ACT.Tanh).then_inc(tc_ready, 1)

            def body(i, first, last):
                for k in range(8):
                    s = 8 * i + k
                    gates_in(s, k)
                    if not (first and k == 0):
                        cell_out(s - 1, k + 7)
                    gates_out(s, k)

            turns(act, body)
            cell_out(4 * STEPS - 1, 7)

        @block.vector
        def _(dve):
            dve.wait_ge(w_loaded, 16)
            nc.vector.tensor_copy(w_hi[:], w_raw[:]).then_inc(w_split, 1)
            dve.wait_ge(w_split, 1)
            nc.vector.tensor_tensor(w_lo[:], w_raw[:], w_hi[:], ALU.subtract).then_inc(w_split, 1)
            for g in range(4):
                clear = nc.vector.memset(cell[g][HI:HI + HC], 0.0)
            clear.then_inc(cells_zero, 1)
            dve.wait_ge(cells_zero, 1)

            def new_cell(s, k, first):
                g = k % 4
                dve.wait_ge(sif_ready, s + 1)
                at_least(dve, cell_ready, s - 3)
                nc.vector.tensor_tensor(f_c[g][HI:HI + HC], sig_if[g][HI:HI + HC], cell[g][HI:HI + HC],
                                        ALU.mult).then_inc(ig_fc_ready, 1)
                dve.wait_ge(tg_ready, s + 1)
                nc.vector.tensor_tensor(i_g[g][HI:HI + HC], sig_if[g][0:HC], tanh_g[g][0:HC],
                                        ALU.mult).then_inc(ig_fc_ready, 1)
                dve.wait_ge(ig_fc_ready, 2 * s + 2)
                nc.vector.tensor_tensor(cell[g][HI:HI + HC], f_c[g][HI:HI + HC], i_g[g][HI:HI + HC],
                                        ALU.add).then_inc(cell_ready, 1)

            def new_h(s, k, stored):
                g, e = k % 4, k // 4
                dve.wait_ge(tc_ready, s + 1)
                dve.wait_ge(so_ready, s + 1)
                at_least(dve, h_stored[g][e], stored)
                at_least(dve, lo_ready, s - 7)
                nc.vector.tensor_tensor(h_new[g][e][0:HC], sig_o[g][HI:HI + HC], tanh_c[g][HI:HI + HC],
                                        ALU.mult).then_inc(h_ready, 1)
                dve.wait_ge(h_ready, s + 1)
                nc.vector.tensor_copy(top[g % 2][1 - e][0:HC, halves(g), 1:1 + W],
                                      h_new[g][e][0:HC]).then_inc(hi_ready, 1)

            def high_x(t, e, d, loaded):
                dve.wait_ge(x_loaded[d][e], loaded)
                at_least(dve, go_summed, 4 * t - 5 + d)
                nc.vector.tensor_copy(top[d][e][HI:HI + C, :, 1:1 + W], x_raw[d][e][HI:HI + C]).then_inc(x_high, 1)

            dve.wait_ge(zeroed, 1)
            for d in range(2):
                high_x(0, 0, d, 16)

            def body(i, first, last):
                for k in range(8):
                    s, e = 8 * i + k, k // 4
                    if k > 0:
                        new_h(s - 1, k - 1, 16 * i)
                    elif not first:
                        new_h(s - 1, 7, 16 * (i - 1))
                    new_cell(s, k, first)
                    if k % 4 < 2 and not (last and e == 1):
                        high_x(2 * i + e + 1, 1 - e, k % 4, 16 * (i + 1 + e))

            turns(dve, body)
            new_h(4 * STEPS - 1, 7, 16 * (STEPS // 2 - 1))

        @block.gpsimd
        def _(pool):
            def done(n):
                pool.wait_ge(cleared, n)

            cleared = sem("cleared")
            for d in range(2):
                for e in range(2):
                    nc.gpsimd.memset(top[d][e][:].bitcast(F32), 0.0).then_inc(cleared, 1)
                    nc.gpsimd.memset(rest[d][e][:].bitcast(F32), 0.0).then_inc(cleared, 1)
            done(8)
            for n in range(4):
                nc.gpsimd.memset(top[n // 2][n % 2][32:64].bitcast(F32), 1.0).then_inc(cleared, 1)
            done(12)
            for n in range(4):
                nc.gpsimd.memset(top[n // 2][n % 2][32:48].bitcast(F32), 0.0).then_inc(cleared, 1)
            done(16)
            nc.gpsimd.memset(x_raw[0][0][0:32, 0, 0:1], 0.0).then_inc(zeroed, 1)

            def low_x(t, e, d):
                pool.wait_ge(x_high, 2 * t + d + 1)
                nc.gpsimd.tensor_tensor(rest[d][e][HI:HI + C, :, 1:1 + W], x_raw[d][e][HI:HI + C],
                                        top[d][e][HI:HI + C, :, 1:1 + W], ALU.subtract).then_inc(x_low, 1)

            def low_h(s, k):
                g, e = k % 4, k // 4
                pool.wait_ge(hi_ready, s + 1)
                nc.gpsimd.tensor_tensor(rest[g % 2][1 - e][0:HC, halves(g), 1:1 + W], h_new[g][e][0:HC],
                                        top[g % 2][1 - e][0:HC, halves(g), 1:1 + W],
                                        ALU.subtract).then_inc(lo_ready, 1)

            for d in range(2):
                low_x(0, 0, d)

            def body(i, first, last):
                for k in range(8):
                    s, e = 8 * i + k, k // 4
                    if k > 0:
                        low_h(s - 1, k - 1)
                    elif not first:
                        low_h(s - 1, 7)
                    if k % 4 < 2 and not (last and e == 1):
                        low_x(2 * i + e + 1, 1 - e, k % 4)

            turns(pool, body)
            low_h(4 * STEPS - 1, 7)


def projection(nc, h_rows, w_proj, y, stats):
    ROWS, BUFS = 2, 4
    TURN = ROWS * BUFS
    with ExitStack() as ctx:
        def sem(name):
            return ctx.enter_context(nc.semaphore(name))

        wp = ctx.enter_context(nc.sbuf_tensor("wp", [P, 64], F32))
        h_in = [ctx.enter_context(nc.sbuf_tensor(f"h_in{n}", [P, ROWS, B, W], F32)) for n in range(BUFS)]
        ps = ctx.enter_context(nc.psum_tensor("proj", [P, TURN, 512], F32))
        wp_loaded, gaps_zero = sem("wp_loaded"), sem("gaps_zero")
        h_loaded = [sem(f"h_loaded{n}") for n in range(BUFS)]
        row_summed, row_kept, row_measured = sem("row_summed"), sem("row_kept"), sem("row_measured")
        block = ctx.enter_context(nc.Block())

        @block.sync
        def _(sp):
            sp.dma_start(wp[:], w_proj).then_inc(wp_loaded, 16)
            sp.wait_ge(gaps_zero, BUFS)

            def body(i, first):
                for n in range(BUFS):
                    r = TURN * i + ROWS * n
                    at_least(sp, row_summed, r - TURN + ROWS)
                    for d in range(2):
                        sp.dma_start(h_in[n][64 * d:64 * d + HC],
                                     h_rows[bass.ds(r, ROWS), d].rearrange("r c b w -> c r b w")).then_inc(h_loaded[n], 16)

            body(0, True)
            with sp.Fori(1, H // TURN) as i:
                body(i, False)

        @block.tensor
        def _(pe):
            pe.wait_ge(wp_loaded, 16)

            def body(i, first):
                for k in range(TURN):
                    if k % ROWS == 0:
                        pe.wait_ge(h_loaded[k // ROWS], 32 * i + 32)
                    at_least(pe, row_kept, TURN * (i - 1) + k + 1)
                    for half in range(2):
                        mm = nc.tensor.matmul(ps[64 * half:64 * half + 64, k, 0:NH], wp[:],
                                              h_in[k // ROWS][:, k % ROWS, HB * half:HB * half + HB, :],
                                              start=True, stop=True)
                    mm.then_inc(row_summed, 1)

            body(0, True)
            with pe.Fori(1, H // TURN) as i:
                body(i, False)

        @block.scalar
        def _(act):
            with act.Fori(0, H // TURN) as i:
                for k in range(TURN):
                    act.wait_ge(row_summed, TURN * i + k + 1)
                    nc.scalar.activation(y[:, :, bass.ds(TURN * i + k, 1), :],
                                         ps[:, k, 0:NH].rearrange("p (b r w) -> p b r w", b=HB, r=1),
                                         ACT.Identity).then_inc(row_kept, 1)

        @block.vector
        def _(dve):
            for n in range(BUFS):
                nc.vector.memset(h_in[n][:], 0.0).then_inc(gaps_zero, 1)
            with dve.Fori(0, H // TURN) as i:
                for k in range(TURN):
                    dve.wait_ge(row_kept, TURN * i + k + 1)
                    nc.vector.bn_stats(stats[:, bass.ds((TURN * i + k) * 6, 6)],
                                       y[:, :, bass.ds(TURN * i + k, 1), :]).then_inc(row_measured, 1)
            dve.wait_ge(row_measured, H)


def residual(nc, y, stats, consts, norms, x_lanes, x1_lanes, sums, folded):
    PART = 16 * W
    PARTS = HB * PX // PART
    BUFS = 3
    with ExitStack() as ctx:
        def sb(name, shape, dt=F32):
            return ctx.enter_context(nc.sbuf_tensor(name, shape, dt))

        def sem(name):
            return ctx.enter_context(nc.semaphore(name))

        pairing = sb("pairing", [P, P])
        nv = sb("nv", [P, 4, 8])
        half_stat = sb("half_stat", [P, 2])
        moments = sb("moments", [P, 2])
        root = sb("root", [P, 8])
        ratio = sb("ratio", [P, 8])
        tmp = sb("tmp", [P, 8])
        x_in = [sb(f"x_in{n}", [P, PART]) for n in range(BUFS)]
        part_sums = sb("part_sums", [P, PARTS])
        ps = ctx.enter_context(nc.psum_tensor("moment_ps", [P, 2], F32))
        pairing_loaded, nv_loaded, x_gaps = sem("pairing_loaded"), sem("nv_loaded"), sem("x_gaps")
        x_loaded = [sem(f"x2_loaded{n}") for n in range(BUFS)]
        x1_stored = [sem(f"x1_stored{n}") for n in range(BUFS)]
        step, averaged, rooted, relued, added = (sem(n) for n in ("step", "averaged", "rooted", "relued", "added"))
        block = ctx.enter_context(nc.Block())

        @block.sync
        def _(sp):
            sp.dma_start(pairing[:], consts[:, 0:P]).then_inc(pairing_loaded, 16)
            sp.dma_start(nv[:], norms).then_inc(nv_loaded, 16)
            sp.wait_ge(x_gaps, BUFS)

            def load(i, n):
                for half in range(2):
                    sp.dma_start(x_in[n][64 * half:64 * half + C],
                                 x_lanes[half, :, bass.ds((BUFS * i + n) * PART, PART)]).then_inc(x_loaded[n], 16)

            def store(i, n):
                sp.wait_ge(added, BUFS * i + n + 1)
                sp.dma_start(x1_lanes[:, bass.ds((BUFS * i + n) * PART, PART)], x_in[n][:]).then_inc(x1_stored[n], 16)

            for n in range(BUFS):
                load(0, n)
            with sp.Fori(0, PARTS // BUFS - 1) as i:
                for n in range(BUFS):
                    store(i, n)
                for n in range(BUFS):
                    sp.wait_ge(x1_stored[n], 16 * i + 16)
                    load(i + 1, n)
            for n in range(BUFS):
                store(PARTS // BUFS - 1, n)
            for n in range(BUFS):
                sp.wait_ge(x1_stored[n], 16 * (PARTS // BUFS))

        @block.tensor
        def _(pe):
            pe.wait_ge(pairing_loaded, 16)
            pe.wait_ge(step, 3)
            nc.tensor.matmul(ps[:], pairing[:], moments[:], start=True, stop=True).then_inc(averaged, 1)

        @block.scalar
        def _(act):
            act.wait_ge(step, 6)
            nc.scalar.activation(root[:], tmp[:], ACT.Sqrt).then_inc(rooted, 1)
            act.wait_ge(step, 13)
            with act.Fori(0, PARTS // BUFS) as i:
                for n in range(BUFS):
                    at = y[:].rearrange("p b r w -> p (b r w)")[:, bass.ds((BUFS * i + n) * PART, PART)]
                    nc.scalar.activation(at, at, ACT.Relu, bias=folded[:, 1, 7:8],
                                         scale=folded[:, 0, 7:8]).then_inc(relued, 1)

        @block.vector
        def _(dve):
            for n in range(BUFS):
                nc.vector.memset(x_in[n][:], 0.0).then_inc(x_gaps, 1)
            count = [0]

            def then(ins):
                count[0] += 1
                ins.then_inc(step, 1)
                dve.wait_ge(step, count[0])

            then(nc.vector.bn_aggr(half_stat[:], stats[:]))
            then(nc.vector.tensor_copy(moments[:, 0:1], half_stat[:, 0:1]))
            then(nc.vector.scalar_tensor_tensor(moments[:, 1:2], half_stat[:, 0:1], half_stat[:, 0:1],
                                                half_stat[:, 1:2], ALU.mult, ALU.add))
            dve.wait_ge(averaged, 1)
            dve.wait_ge(nv_loaded, 16)
            then(nc.vector.tensor_copy(half_stat[:], ps[:]))
            nc.vector.tensor_copy(nv[:, 3, 7:8], half_stat[:, 0:1]).then_inc(x_gaps, 1)
            dve.wait_ge(x_gaps, BUFS + 1)
            nc.vector.tensor_scalar(ratio[:, 0:1], half_stat[:, 0:1], half_stat[:, 0:1], -1.0, ALU.mult,
                                    ALU.mult).then_inc(x_gaps, 1)
            dve.wait_ge(x_gaps, BUFS + 2)
            then(nc.vector.tensor_tensor(nv[:, 0, 7:8], ratio[:, 0:1], half_stat[:, 1:2], ALU.add))
            then(nc.vector.tensor_scalar(tmp[:], nv[:, 0, :], EPS, None, ALU.add))
            dve.wait_ge(rooted, 1)
            then(nc.vector.reciprocal(ratio[:], root[:]))
            then(nc.vector.tensor_tensor(ratio[:], ratio[:], tmp[:], ALU.mult))
            then(nc.vector.tensor_tensor(ratio[:], ratio[:], root[:], ALU.add))
            then(nc.vector.tensor_scalar(root[:], ratio[:], 0.5, None, ALU.mult))
            then(nc.vector.reciprocal(ratio[:], root[:]))
            then(nc.vector.tensor_tensor(folded[:, 0, :], ratio[:], nv[:, 1, :], ALU.mult))
            nc.vector.tensor_tensor(tmp[:], folded[:, 0, :], nv[:, 3, :], ALU.mult).then_inc(x_gaps, 1)
            dve.wait_ge(x_gaps, BUFS + 3)
            then(nc.vector.tensor_tensor(folded[:, 1, :], nv[:, 2, :], tmp[:], ALU.subtract))
            with dve.Fori(0, PARTS // BUFS) as i:
                for n in range(BUFS):
                    dve.wait_ge(relued, BUFS * i + n + 1)
                    dve.wait_ge(x_loaded[n], 32 * i + 32)
                    at = y[:].rearrange("p b r w -> p (b r w)")[:, bass.ds((BUFS * i + n) * PART, PART)]
                    nc.vector.scalar_tensor_tensor(x_in[n][:], at, 1.0, x_in[n][:], ALU.mult, ALU.add,
                                                   accum_out=part_sums[:, bass.ds(BUFS * i + n, 1)]).then_inc(added, 1)
            dve.wait_ge(added, PARTS)
            then(nc.vector.tensor_reduce(sums[:], part_sums[:].rearrange("p (b n) -> p b n", b=HB), AX.X, ALU.add))


def selection(nc, consts, w_sal, b_sal, hid, w_pw1, sums, folded, packs_r, packs_f, passes):
    PASSES = 2
    NU = PASSES * UNITS
    with ExitStack() as ctx:
        def sb(name, shape, dt=F32):
            return ctx.enter_context(nc.sbuf_tensor(name, shape, dt))

        def sem(name):
            return ctx.enter_context(nc.semaphore(name))

        cst = sb("cst", [P, 3 * P + HG + NU * UC])
        ident, ones = cst[:, P:2 * P], cst[:, 2 * P:3 * P]
        before = cst[:, 3 * P:3 * P + HG]
        places = cst[:, 3 * P + HG:]
        ws = sb("ws", [P, 2, NG, HG])
        bs = sb("bs", [HG, NG])
        par = sb("par", [HG, NG, NPAR])
        w1 = sb("w1", [HG, NG, 64])
        sal = sb("sal", [HG, NG, B])
        spread = sb("spread", [HG, NG, HG])
        above = sb("above", [HG, NG, B])
        chosen = sb("chosen", [HG, NG, B])
        place = sb("place", [HG, NG, B])
        scratch = sb("scratch", [HG, HID])
        onehot = [sb(f"onehot{n}", [HG, NG, NU * UC]) for n in range(2)]
        pack_r = sb("pack_r", [P, PKR], F32R)
        pack_f = sb("pack_f", [P, PKF])
        most = sb("most", [HG, 1])
        ps_s = ctx.enter_context(nc.psum_tensor("ps_s", [P, NG, B], F32))
        ps_b = ctx.enter_context(nc.psum_tensor("ps_b", [P, 512], F32))
        ps_p = ctx.enter_context(nc.psum_tensor("ps_p", [P, NG, B], F32))
        ps_t = ctx.enter_context(nc.psum_tensor("ps_t", [P, B], F32))
        ps_w = ctx.enter_context(nc.psum_tensor("ps_w", [P, 512], F32))
        ps_q = ctx.enter_context(nc.psum_tensor("ps_q", [P, 512], F32))
        loaded, dve_did, pe_did, act_did, stored = (sem(n) for n in ("s_loaded", "dve_did", "pe_did", "act_did", "pk_stored"))
        block = ctx.enter_context(nc.Block())
        d, t = [0], [0]
        marks = {}

        def n_stored(pair, q):
            return PASSES * pair + q

        @block.sync
        def _(sp):
            sp.dma_start(cst[:], consts).then_inc(loaded, 16)
            sp.dma_start(ws[:], w_sal).then_inc(loaded, 16)
            sp.dma_start(bs[:], b_sal).then_inc(loaded, 16)
            sp.dma_start(par[:], hid).then_inc(loaded, 16)
            sp.dma_start(w1[:], w_pw1).then_inc(loaded, 16)

        @block.vector
        def _(dve):
            def do(ins, wait=True):
                d[0] += 1
                ins.then_inc(dve_did, 1)
                if wait:
                    dve.wait_ge(dve_did, d[0])

            dve.wait_ge(loaded, 80)
            for g in range(NG):
                do(nc.vector.tensor_copy(par[:, g, S1:T1 + 1], folded[0:HG, :, g]), False)
                do(nc.vector.tensor_copy(par[:, g, SD:TD + 1], folded[0:HG, :, NG + g]), False)
            dve.wait_ge(act_did, NG)
            for b in range(B):
                if b:
                    dve.wait_ge(pe_did, marks_pe("spread", b - 1))
                for g in range(NG):
                    do(nc.vector.tensor_scalar(spread[:, g, :], ident[0:HG, 0:HG], sal[:, g, b:b + 1], None, ALU.mult),
                       g == NG - 1)
                marks["spread", b] = d[0]
                dve.wait_ge(pe_did, marks_pe("spread", b))
                for g in range(NG):
                    do(nc.vector.tensor_scalar(scratch[:], ps_b[0:HG, 0:HID], sal[:, g, b:b + 1], 0.0, ALU.is_gt,
                                               ALU.add, accum_out=above[:, g, b:b + 1]))
                marks["counted", b] = d[0]
            do(nc.vector.tensor_scalar(chosen[:], above[:], float(TOPK), None, ALU.is_lt))
            marks["chosen"] = d[0]
            dve.wait_ge(pe_did, marks_pe("places", 0))
            do(nc.vector.scalar_tensor_tensor(place[:], ps_p[0:HG], 1.0, chosen[:], ALU.add, ALU.mult))
            do(nc.vector.tensor_scalar(place[:], place[:], -1.0, None, ALU.add))
            do(nc.vector.tensor_reduce(most[:], ps_t[0:HG], AX.X, ALU.max))
            do(nc.vector.tensor_scalar(passes[0:1, 0:1], most[0:1], float(TOPK), 1.0, ALU.is_gt, ALU.add))
            do(nc.vector.memset(pack_r[:].bitcast(F32), 0.0))
            do(nc.vector.memset(pack_f[:], 0.0))
            for pair in range(HB):
                for half in range(2):
                    b = HB * half + pair
                    for g in range(NG):
                        do(nc.vector.tensor_scalar(onehot[half][:, g, :], places[0:HG], place[:, g, b:b + 1], None,
                                                   ALU.is_equal), False)
                marks["onehot", pair] = d[0]
                for q in range(PASSES):
                    n = HB * q + pair
                    dve.wait_ge(pe_did, marks_pe("pack", n))
                    at_least(dve, stored, 32 * n_stored(pair, q))
                    for half in range(2):
                        lanes = slice(64 * half, 64 * half + 64)
                        cols = slice(64 * half, 64 * half + 64)
                        src = ps_w[lanes, 0:NU * UC].rearrange("p (u r) -> p u r", u=NU)[:, UNITS * q:UNITS * q + UNITS, :]
                        r = pack_r[:].rearrange("p (k u m) -> p k u m", k=2, u=UNITS)
                        do(nc.vector.tensor_copy(r[lanes, 0, :, cols], src))
                        do(nc.vector.tensor_tensor(r[lanes, 1, :, cols], src, r[lanes, 0, :, cols], ALU.subtract))
                        got = ps_q[lanes, 0:UNITS * NPAR].rearrange("p (u m) -> p u m", u=UNITS)
                        f = pack_f[:, 0:UNITS * P].rearrange("p (u m) -> p u m", u=UNITS)
                        do(nc.vector.tensor_copy(f[lanes, :, 64 * half:64 * half + HC], got[:, :, W2:W2 + HC]))
                    got = ps_q[:, 0:UNITS * NPAR].rearrange("p (u m) -> p u m", u=UNITS)
                    do(nc.vector.tensor_copy(pack_f[:, PK_PAR:PK_S2].rearrange("p (u m) -> p u m", u=UNITS), got[:, :, 0:W2]))
                    for u in range(UNITS):
                        for k, tap in enumerate(PE_TAPS):
                            at = PK_DIAG + (u * len(PE_TAPS) + k) * P
                            col = PK_PAR + u * 13 + TAP + tap
                            do(nc.vector.tensor_scalar(pack_f[:, at:at + P], ident, pack_f[:, col:col + 1], None, ALU.mult))
                    do(nc.vector.tensor_copy(pack_f[:, PK_S2:PK_S2 + 1], folded[:, 0, 6:7]))
                    if q == 0:
                        do(nc.vector.tensor_copy(pack_f[:, PK_S2 + 1:PK_S2 + 2], folded[:, 1, 6:7]))
                    else:
                        do(nc.vector.memset(pack_f[:, PK_S2 + 1:PK_S2 + 2], 0.0))
                    marks["packed", n] = d[0]

        @block.scalar
        def _(act):
            act.wait_ge(pe_did, 1)
            for g in range(NG):
                nc.scalar.activation(sal[:, g, :], ps_s[0:HG, g, :], ACT.Sigmoid, bias=bs[:, g:g + 1],
                                     scale=1.0 / PX).then_inc(act_did, 1)

        @block.tensor
        def _(pe):
            def did(mm, name):
                mm.then_inc(pe_did, 1)
                t[0] += 1
                assert t[0] == marks_pe(*name), name

            pe.wait_ge(loaded, 80)
            for g in range(NG):
                for half in range(2):
                    mm = nc.tensor.matmul(ps_s[0:HG, g, HB * half:HB * half + HB], ws[:, half, g, :], sums[:],
                                          start=(g == 0 and half == 0), stop=(g == NG - 1 and half == 1),
                                          skip_group_check=True)
            did(mm, ("sal", 0))
            for b in range(B):
                pe.wait_ge(dve_did, marks["spread", b])
                did(nc.tensor.matmul(ps_b[0:HG, 0:HID], ones[0:HG, 0:HG], spread[:], start=True, stop=True), ("spread", b))
            pe.wait_ge(dve_did, marks["chosen"])
            first = True
            for g in range(NG):
                for k in range(g + 1):
                    nc.tensor.matmul(ps_p[0:HG, g, :], (before if k == g else ones)[0:HG, 0:HG], chosen[:, k, :],
                                     start=first, stop=(g == NG - 1 and k == g), skip_group_check=True)
                    first = False
            for g in range(NG):
                mm = nc.tensor.matmul(ps_t[0:HG, :], ones[0:HG, 0:HG], chosen[:, g, :], start=(g == 0), stop=(g == NG - 1))
            did(mm, ("places", 0))
            for pair in range(HB):
                pe.wait_ge(dve_did, marks["onehot", pair])
                for q in range(PASSES):
                    n = HB * q + pair
                    for half in range(2):
                        lanes = slice(64 * half, 64 * half + 64)
                        if q == 0:
                            for g in range(NG):
                                nc.tensor.matmul(ps_w[lanes, 0:NU * UC], w1[:, g, :], onehot[half][:, g, :],
                                                 start=(g == 0), stop=(g == NG - 1))
                        else:
                            pe.wait_ge(dve_did, marks["packed", pair])
                        for u in range(UNITS):
                            for g in range(NG):
                                at = (UNITS * q + u) * UC
                                mm = nc.tensor.matmul(ps_q[lanes, u * NPAR:(u + 1) * NPAR], onehot[half][:, g, at:at + UC],
                                                      par[:, g, :], start=(g == 0), stop=(g == NG - 1),
                                                      skip_group_check=True)
                    did(mm, ("pack", n))

        @block.gpsimd
        def _(pool):
            for pair in range(HB):
                for q in range(PASSES):
                    n = HB * q + pair
                    pool.wait_ge(dve_did, marks["packed", n])
                    pool.dma_start(packs_r[n], pack_r[:].bitcast(F32)).then_inc(stored, 16)
                    pool.dma_start(packs_f[n], pack_f[:]).then_inc(stored, 16)
            pool.dma_start(packs_r[2 * HB], pack_r[:].bitcast(F32)).then_inc(stored, 16)
            pool.dma_start(packs_f[2 * HB], pack_f[:]).then_inc(stored, 16)
            pool.wait_ge(stored, 32 * (2 * HB + 1))


def marks_pe(what, n):
    if what == "sal":
        return 1
    if what == "spread":
        return 2 + n
    if what == "places":
        return 2 + B
    return 3 + B + 2 * (n % HB) + n // HB


def bottleneck(nc, w_mask, b_mask, x1_lanes, out_lanes, packs_r, packs_f, passes):
    AHEAD = 3
    NT = len(DVE_TAPS)
    with ExitStack() as ctx:
        def sb(name, shape, dt=F32):
            return ctx.enter_context(nc.sbuf_tensor(name, shape, dt))

        def sem(name):
            return ctx.enter_context(nc.semaphore(name))

        pk_r = [sb(f"pk_r{n}", [P, PKR], F32R) for n in range(2)]
        pk_f = [sb(f"pk_f{n}", [P, PKF]) for n in range(2)]
        wm_raw, bm = sb("wm_raw", [P, P]), sb("bm", [P, 1])
        wm = [sb("wm_hi", [P, P], F32R), sb("wm_lo", [P, P], F32R)]
        x1 = [sb(f"x1_{n}", [P, CPX]) for n in range(3)]
        xh = [sb(f"xh{n}", [P, CPX], F32R) for n in range(3)]
        xl = [sb(f"xl{n}", [P, CPX], F32R) for n in range(3)]
        base = [sb(f"base{n}", [P, CPX]) for n in range(3)]
        outb = [sb(f"outb{n}", [P, CPX]) for n in range(3)]
        mask = [sb(f"mask{n}", [P, CPX]) for n in range(3)]
        h1 = sb("h1", [P, UNITS, 3, CH + 2, WP])
        acc = [sb(f"acc{n}", [P, CPX]) for n in range(3)]
        prod = [[sb(f"prod{n}{m}", [P, CPX]) for m in range(2)] for n in range(3)]
        full = [sb(f"full{n}", [P, CPX]) for n in range(3)]
        h2 = [sb(f"h2_{n}", [P, CPX]) for n in range(3)]
        zeros = sb("zeros", [P, UNITS, WP])
        z = sb("z", [P, CPX])
        zm = sb("zm", [P, CPX])
        ps1 = [ctx.enter_context(nc.psum_tensor(f"ps1_{n}", [P, 2, 512], F32)) for n in range(2)]
        psd = ctx.enter_context(nc.psum_tensor("psd", [P, 2, 512], F32))
        ps2 = ctx.enter_context(nc.psum_tensor("ps2", [P, 2, 512], F32))

        mask_loaded, wm_split, borders = sem("mask_loaded"), sem("wm_split"), sem("borders")
        pack_in = [sem(f"pack_in{n}") for n in range(2)]
        x1_in = [sem(f"x1_in{n}") for n in range(3)]
        base_in = [sem(f"base_in{n}") for n in range(3)]
        out_stored = [sem(f"out_stored{n}") for n in range(3)]
        xh_done, xl_done, mask_done, z_done, zm_done, out_done = (
            sem(n) for n in ("xh_done", "xl_done", "mask_done", "z_done", "zm_done", "out_done"))
        pw1_done = sem("pw1_done")
        relu1_done, taps_done, psd_read, chain, acc_done, prod_done, pair_sum, full_done, relu2_done, pw2_done = (
            sem(n) for n in ("relu1_done", "taps_done", "psd_read", "chain", "acc_done", "prod_done", "pair_sum",
                             "full_done", "relu2_done", "pw2_done"))
        halo_done, halo_top = sem("halo_done"), sem("halo_top")
        HALOS = NCH + 1

        def rows(ap):
            return ap.rearrange("p (m r w) -> p m r w", m=2, w=W)

        def banks(ps):
            return ps[:, :, 0:NH].rearrange("p m (r w) -> p m r w", w=W)

        def window(j, slot, tap):
            dy, dx = divmod(tap, 3)
            return h1[:, j, slot, dy:dy + CH, dx:dx + W].rearrange("p (m r) w -> p m r w", m=2)

        def par(pp, j, col):
            return pk_f[pp][:, PK_PAR + 13 * j + col:PK_PAR + 13 * j + col + 1]

        def pairs(eng, one):
            n = eng.value_load(passes[0:1, 0:1], min_val=1, max_val=2)
            with eng.Fori(0, n * (HB // 2)) as o:
                for pp in range(2):
                    one(2 * o + pp, pp)

        def steps(step):
            def run(eng):
                step(0, 0, 0, None)
                with eng.Fori(0, 3) as m:
                    for e in range(3):
                        step(3 * m + 1 + e, (1 + e) % 3, m + 1, m)
                step(10, 1, None, 3)
                step(11, 2, None, 3)
            return run

        def chunk0(Pi):
            return NCH * Pi + AHEAD

        def nth(Pi, third):
            return 64 * Pi + 16 * third + 16

        def pack_count(Pi, pp):
            return 16 * (Pi - pp) + 32

        block = ctx.enter_context(nc.Block())

        @block.sync
        def _(sp):
            sp.dma_start(wm_raw[:], w_mask).then_inc(mask_loaded, 16)
            sp.dma_start(bm[:], b_mask).then_inc(mask_loaded, 16)
            sp.dma_start(pk_r[0][:].bitcast(F32), packs_r[0]).then_inc(pack_in[0], 16)
            sp.dma_start(pk_f[0][:], packs_f[0]).then_inc(pack_in[0], 16)
            for n in range(3):
                sp.sem_inc(out_stored[n], 16)
            npass = sp.value_load(passes[0:1, 0:1], min_val=1, max_val=2)

            def one_pass(q):
                before = x1_lanes if q == 0 else out_lanes

                def cols(pair, k):
                    return bass.ds((NCH * pair + k) * CPX, CPX)

                def load_x1(pair, Ci, k, n):
                    sp.wait_ge(xl_done, Ci - 2)
                    sp.dma_start(x1[n][:], x1_lanes[:, cols(pair, k)]).then_inc(x1_in[n], 16)

                def load_base(pair, Ci, k, n):
                    sp.wait_ge(out_done, Ci - 2)
                    sp.dma_start(base[n][:], before[:, cols(pair, k)]).then_inc(base_in[n], 16)

                def store(pair, Ci, k, n):
                    sp.wait_ge(out_done, Ci + 1)
                    sp.dma_start(out_lanes[:, cols(pair, k)], outb[n][:]).then_inc(out_stored[n], 16)

                with sp.Fori(0, HB // 2) as o:
                    for pp in range(2):
                        pair = 2 * o + pp
                        Pi = pair + HB * q
                        C0 = chunk0(Pi)
                        sp.wait_ge(z_done, C0)
                        sp.dma_start(pk_r[1 - pp][:].bitcast(F32), packs_r[Pi + 1]).then_inc(pack_in[1 - pp], 16)
                        sp.dma_start(pk_f[1 - pp][:], packs_f[Pi + 1]).then_inc(pack_in[1 - pp], 16)
                        for k in range(3):
                            load_x1(pair, C0 + k, k, k)
                        for k in range(3):
                            load_base(pair, C0 + k, k, k)
                        load_x1(pair, C0 + 3, 3, 0)
                        with sp.Fori(0, 2) as m:
                            for e in range(3):
                                k = 3 * m + 1 + e
                                load_x1(pair, C0 + k + 3, k + 3, (1 + e) % 3)
                                store(pair, C0 + k - 1, k - 1, e)
                                load_base(pair, C0 + k + 2, k + 2, e)
                        for k in range(7, 10):
                            if k < 9:
                                load_x1(pair, C0 + k + 3, k + 3, k % 3)
                            store(pair, C0 + k - 1, k - 1, (k - 1) % 3)
                            load_base(pair, C0 + k + 2, k + 2, (k + 2) % 3)
                        for k in range(9, 12):
                            store(pair, C0 + k, k, k % 3)
                for n in range(3):
                    sp.wait_ge(out_stored[n], nth(HB * (q + 1), 0))

            one_pass(0)
            with sp.If(npass > 1):
                one_pass(1)
            sp.wait_ge(pack_in[0], 32)
            sp.wait_ge(pack_in[1], 32)

        @block.tensor
        def _(pe):
            pe.sem_inc(pw1_done, 4 * AHEAD)
            pe.sem_inc(taps_done, 3 * AHEAD)
            pe.sem_inc(pw2_done, 3 * AHEAD)
            pe.wait_ge(wm_split, 2)
            pe.wait_ge(borders, 2)

            def pw1(Ci, n, pp, u):
                if u == 0:
                    pe.wait_ge(xl_done, Ci + 1)
                    pe.wait_ge(relu1_done, 3 * Ci)
                elif u == 1:
                    pe.wait_ge(mask_done, Ci)
                else:
                    pe.wait_ge(relu1_done, 3 * Ci + u - 1)
                if u < UNITS:
                    hi, lo = pk_r[pp][:, u * P:(u + 1) * P], pk_r[pp][:, (UNITS + u) * P:(UNITS + u + 1) * P]
                else:
                    hi, lo = wm[0][:], wm[1][:]
                for m in range(2):
                    for i, (w, v) in enumerate(((hi, xh[n]), (hi, xl[n]), (lo, xh[n]))):
                        mm = nc.tensor.matmul(ps1[u % 2][:, m, 0:NH], w, v[:, m * NH:(m + 1) * NH],
                                              start=(i == 0), stop=(i == 2))
                mm.then_inc(pw1_done, 1)

            def taps(Pi, Ci, k, slot, pp, j):
                if j == 0:
                    pe.wait_ge(halo_done, HALOS * Pi + k + 2)
                pe.wait_ge(psd_read, 3 * Ci + j)
                for m in range(2):
                    for i, tap in enumerate(PE_TAPS):
                        at = PK_DIAG + (j * len(PE_TAPS) + i) * P
                        mm = nc.tensor.matmul(psd[:, m, 0:NH], pk_f[pp][:, at:at + P], window(j, slot, tap)[:, m],
                                              start=(i == 0), stop=(i == len(PE_TAPS) - 1))
                mm.then_inc(taps_done, 1)

            def pw2(Ci, pp, j):
                pe.wait_ge(relu2_done, 3 * Ci + j + 1)
                if j == 0:
                    pe.wait_ge(z_done, Ci)
                for m in range(2):
                    mm = nc.tensor.matmul(ps2[:, m, 0:NH], pk_f[pp][:, j * P:(j + 1) * P], h2[j][:, m * NH:(m + 1) * NH],
                                          start=(j == 0), stop=(j == UNITS - 1), skip_group_check=True)
                mm.then_inc(pw2_done, 1)

            def one(Pi, pp):
                pe.wait_ge(pack_in[pp], pack_count(Pi, pp))
                C0 = chunk0(Pi)
                for k in range(2):
                    for u in range(UNITS + 1):
                        pw1(C0 + k, k, pp, u)

                def step(k, slot, ahead, behind):
                    Ci, nxt = C0 + k, (slot + 2) % 3
                    taps(Pi, Ci, k, slot, pp, 0)
                    if behind is not None:
                        pw2(Ci - 1, pp, 1)
                    if ahead is not None:
                        pw1(Ci + 2, nxt, pp, 0)
                        pw1(Ci + 2, nxt, pp, 1)
                    taps(Pi, Ci, k, slot, pp, 1)
                    if behind is not None:
                        pw2(Ci - 1, pp, 2)
                    if ahead is not None:
                        pw1(Ci + 2, nxt, pp, 2)
                    taps(Pi, Ci, k, slot, pp, 2)
                    if ahead is not None:
                        pw1(Ci + 2, nxt, pp, UNITS)
                    pw2(Ci, pp, 0)

                steps(step)(pe)
                pw2(C0 + NCH - 1, pp, 1)
                pw2(C0 + NCH - 1, pp, 2)

            pairs(pe, one)

        @block.scalar
        def _(act):
            act.sem_inc(xh_done, AHEAD)
            act.sem_inc(relu1_done, 3 * AHEAD)
            act.sem_inc(prod_done, 6 * AHEAD)
            act.sem_inc(relu2_done, 3 * AHEAD)
            act.sem_inc(z_done, AHEAD)
            act.wait_ge(borders, 2)

            def high(Ci, n, loads):
                act.wait_ge(x1_in[n], loads)
                act.wait_ge(pw1_done, 4 * Ci - 8)
                nc.scalar.activation(xh[n][:], x1[n][:], ACT.Copy).then_inc(xh_done, 1)

            def relu1(Ci, n, pp, j):
                act.wait_ge(pw1_done, 4 * Ci + j + 1)
                act.wait_ge(taps_done, 3 * Ci + j - 8)
                act.wait_ge(acc_done, 3 * Ci + j - 8)
                act.wait_ge(prod_done, 6 * Ci + 2 * j - 16)
                nc.scalar.activation(h1[:, j, n, 1:1 + CH, 1:1 + W].rearrange("p (m r) w -> p m r w", m=2),
                                     banks(ps1[j % 2]), ACT.Relu, bias=par(pp, j, T1),
                                     scale=par(pp, j, S1)).then_inc(relu1_done, 1)

            def prods(Ci, slot, pp, j):
                act.wait_ge(full_done, 3 * Ci + j - 2)
                for i, tap in enumerate(ACT_TAPS):
                    nc.scalar.activation(rows(prod[j][i][:]), window(j, slot, tap), ACT.Copy,
                                         scale=par(pp, j, TAP + tap)).then_inc(prod_done, 1)

            def relu2(Ui, pp, j):
                act.wait_ge(full_done, Ui + 1)
                act.wait_ge(pw2_done, Ui - 2)
                nc.scalar.activation(h2[j][:], full[j][:], ACT.Relu, bias=par(pp, j, TD),
                                     scale=par(pp, j, SD)).then_inc(relu2_done, 1)

            def norm2(Ci, pp):
                act.wait_ge(pw2_done, 3 * Ci + 3)
                act.wait_ge(zm_done, Ci)
                nc.scalar.activation(rows(z[:]), banks(ps2), ACT.Identity, bias=pk_f[pp][:, PK_S2 + 1:PK_S2 + 2],
                                     scale=pk_f[pp][:, PK_S2:PK_S2 + 1]).then_inc(z_done, 1)

            def one(Pi, pp):
                act.wait_ge(pack_in[pp], pack_count(Pi, pp))
                C0 = chunk0(Pi)
                for k in range(2):
                    high(C0 + k, k, nth(Pi, 0))
                    for j in range(UNITS):
                        relu1(C0 + k, k, pp, j)

                def step(k, slot, ahead, behind):
                    Ci, nxt = C0 + k, (slot + 2) % 3
                    if ahead is not None:
                        high(Ci + 2, nxt, nth(Pi, ahead))
                    act.wait_ge(halo_done, HALOS * Pi + k + 2)
                    prods(Ci, slot, pp, 0)
                    if behind is not None:
                        relu2(3 * Ci - 1, pp, 2)
                    if ahead is not None:
                        relu1(Ci + 2, nxt, pp, 0)
                        relu1(Ci + 2, nxt, pp, 1)
                    prods(Ci, slot, pp, 1)
                    relu2(3 * Ci, pp, 0)
                    if ahead is not None:
                        relu1(Ci + 2, nxt, pp, 2)
                    prods(Ci, slot, pp, 2)
                    relu2(3 * Ci + 1, pp, 1)
                    if behind is not None:
                        norm2(Ci - 1, pp)

                steps(step)(act)
                relu2(3 * (C0 + NCH - 1) + 2, pp, 2)
                norm2(C0 + NCH - 1, pp)

            pairs(act, one)

        @block.vector
        def _(dve):
            dve.sem_inc(mask_done, AHEAD)
            dve.sem_inc(psd_read, 3 * AHEAD)
            dve.sem_inc(chain, 3 * AHEAD * (NT - 2))
            dve.sem_inc(acc_done, 3 * AHEAD)
            dve.sem_inc(zm_done, AHEAD)
            dve.wait_ge(mask_loaded, 32)
            nc.vector.tensor_copy(wm[0][:], wm_raw[:]).then_inc(wm_split, 1)
            dve.wait_ge(wm_split, 1)
            nc.vector.tensor_tensor(wm[1][:], wm_raw[:], wm[0][:], ALU.subtract).then_inc(wm_split, 1)

            def make_mask(Ci, n):
                dve.wait_ge(pw1_done, 4 * Ci + 4)
                dve.wait_ge(zm_done, Ci - 2)
                nc.vector.tensor_scalar(rows(mask[n][:]), banks(ps1[1]), bm[:, 0:1], 0.0, ALU.add,
                                        ALU.is_ge).then_inc(mask_done, 1)

            def tap_chain(Ci, slot, pp, j):
                Ui = 3 * Ci + j
                dve.wait_ge(taps_done, Ui + 1)
                dve.wait_ge(full_done, Ui - 2)
                for i, tap in enumerate(DVE_TAPS):
                    if i == 1:
                        dve.wait_ge(psd_read, Ui + 1)
                    elif i > 1:
                        dve.wait_ge(chain, (NT - 2) * Ui + i - 1)
                    ins = nc.vector.scalar_tensor_tensor(rows(acc[j][:]), window(j, slot, tap), par(pp, j, TAP + tap),
                                                         banks(psd) if i == 0 else rows(acc[j][:]), ALU.mult, ALU.add)
                    ins.then_inc(psd_read if i == 0 else acc_done if i == NT - 1 else chain, 1)

            def masked(Ci, n):
                dve.wait_ge(z_done, Ci + 1)
                dve.wait_ge(out_done, Ci)
                nc.vector.tensor_tensor(zm[:], z[:], mask[n][:], ALU.mult).then_inc(zm_done, 1)

            def one(Pi, pp):
                dve.wait_ge(pack_in[pp], pack_count(Pi, pp))
                C0 = chunk0(Pi)
                make_mask(C0, 0)
                make_mask(C0 + 1, 1)

                def step(k, slot, ahead, behind):
                    Ci, nxt = C0 + k, (slot + 2) % 3
                    dve.wait_ge(halo_done, HALOS * Pi + k + 2)
                    for j in range(UNITS):
                        tap_chain(Ci, slot, pp, j)
                    if behind is not None:
                        masked(Ci - 1, nxt)
                    if ahead is not None:
                        make_mask(Ci + 2, nxt)

                steps(step)(dve)
                masked(C0 + NCH - 1, 2)

            pairs(dve, one)

        @block.gpsimd
        def _(pool):
            pool.sem_inc(xl_done, AHEAD)
            pool.sem_inc(pair_sum, 3 * AHEAD)
            pool.sem_inc(full_done, 3 * AHEAD)
            pool.sem_inc(out_done, AHEAD)
            nc.gpsimd.memset(zeros[:], 0.0).then_inc(borders, 1)
            nc.gpsimd.memset(h1[:], 0.0).then_inc(borders, 1)
            pool.wait_ge(borders, 2)

            def low(Ci, n):
                pool.wait_ge(xh_done, Ci + 1)
                nc.gpsimd.tensor_tensor(xl[n][:], x1[n][:], xh[n][:], ALU.subtract).then_inc(xl_done, 1)

            def halo(Ci, n):
                prev = (n + 2) % 3
                pool.wait_ge(relu1_done, 3 * Ci + 3)
                above, below = h1[:, :, prev, CH, 1:1 + W], h1[:, :, n, 1, 1:1 + W]
                nc.gpsimd.tensor_tensor(h1[:, :, n, 0, 1:1 + W], above, zeros[:, :, 0:W], ALU.add).then_inc(halo_top, 1)
                nc.gpsimd.tensor_tensor(h1[:, :, prev, CH + 1, 1:1 + W], below, zeros[:, :, 0:W], ALU.add).then_inc(halo_done, 1)

            def edge(Cj, n, r):
                pool.wait_ge(taps_done, 3 * Cj + 3)
                pool.wait_ge(acc_done, 3 * Cj + 3)
                pool.wait_ge(prod_done, 6 * Cj + 6)
                nc.gpsimd.tensor_tensor(h1[:, :, n, r, :], zeros[:], zeros[:], ALU.add).then_inc(halo_done, 1)

            def gather(Ui, j):
                pool.wait_ge(prod_done, 2 * Ui + 2)
                nc.gpsimd.tensor_tensor(prod[j][0][:], prod[j][0][:], prod[j][1][:], ALU.add).then_inc(pair_sum, 1)
                pool.wait_ge(pair_sum, Ui + 1)
                pool.wait_ge(acc_done, Ui + 1)
                pool.wait_ge(relu2_done, Ui - 2)
                nc.gpsimd.tensor_tensor(full[j][:], acc[j][:], prod[j][0][:], ALU.add).then_inc(full_done, 1)

            def add_base(Ci, n, loads):
                pool.wait_ge(zm_done, Ci + 1)
                pool.wait_ge(base_in[n], loads)
                pool.wait_ge(out_stored[n], loads)
                nc.gpsimd.tensor_tensor(outb[n][:], zm[:], base[n][:], ALU.add).then_inc(out_done, 1)

            def one(Pi, pp):
                C0 = chunk0(Pi)
                edge(C0 - 3, 0, 0)
                low(C0, 0)
                low(C0 + 1, 1)
                halo(C0 + 1, 1)

                def step(k, slot, ahead, behind):
                    Ci, nxt = C0 + k, (slot + 2) % 3
                    if ahead is not None:
                        low(Ci + 2, nxt)
                    gather(3 * Ci, 0)
                    gather(3 * Ci + 1, 1)
                    if ahead is not None:
                        halo(Ci + 2, nxt)
                    elif slot == 1:
                        edge(Ci - 2, 2, CH + 1)
                    gather(3 * Ci + 2, 2)
                    if behind is not None:
                        add_base(Ci - 1, nxt, nth(Pi, behind))

                steps(step)(pool)
                add_base(C0 + NCH - 1, 2, nth(Pi, 3))

            pairs(pool, one)


def build(nc, x_rows, x_lanes, w_gates, w_proj, norms, consts, w_sal, b_sal, hid, w_pw1, w_mask, b_mask, out):
    h_rows = nc.dram_tensor("h_rows", [H, 2, HC, B, W], F32).ap()
    x1_lanes = nc.dram_tensor("x1_lanes", [P, HB * PX], F32).ap()
    packs_r = nc.dram_tensor("packs_r", [2 * HB + 1, P, PKR], F32).ap()
    packs_f = nc.dram_tensor("packs_f", [2 * HB + 1, P, PKF], F32).ap()
    recurrence(nc, x_rows, w_gates, h_rows)
    with ExitStack() as ctx:
        def sb(name, shape, dt=F32):
            return ctx.enter_context(nc.sbuf_tensor(name, shape, dt))

        sums = sb("sums", [P, HB])
        folded = sb("folded", [P, 2, 8])
        passes = sb("passes", [1, 1], I32)
        with ExitStack() as own:
            y = own.enter_context(nc.sbuf_tensor("y", [P, HB, H, W], F32))
            stats = own.enter_context(nc.sbuf_tensor("stats", [P, 6 * H], F32))
            projection(nc, h_rows, w_proj, y, stats)
            residual(nc, y, stats, consts, norms, x_lanes, x1_lanes, sums, folded)
        selection(nc, consts, w_sal, b_sal, hid, w_pw1, sums, folded, packs_r, packs_f, passes)
        bottleneck(nc, w_mask, b_mask, x1_lanes, out, packs_r, packs_f, passes)


def kernel(x, L0_conv_w_f, L0_conv_b_f, L0_conv_w_b, L0_conv_b_b, L0_conv_w_proj, L0_conv_gamma, L0_conv_beta,
           L1_conv_w_pw1, L1_conv_bn1_g, L1_conv_bn1_b, L1_conv_bn1_m, L1_conv_bn1_v, L1_conv_w_dw,
           L1_conv_bnd_g, L1_conv_bnd_b, L1_conv_bnd_m, L1_conv_bnd_v, L1_conv_w_pw2,
           L1_conv_bn2_g, L1_conv_bn2_b, L1_conv_bn2_m, L1_conv_bn2_v, L1_conv_w_mask, L1_conv_b_mask,
           L1_conv_w_sal, L1_conv_b_sal):
    import concourse.bacc as bacc
    from concourse.bass_utils import run_bass_kernel_spmd

    def arr(a):
        return np.ascontiguousarray(a)

    def halves(a):
        out = np.zeros((P,) + a.shape[1:], np.float32)
        out[LO:LO + C] = a
        out[HI:HI + C] = a
        return out

    w_gates = np.zeros((P, 12, P), np.float32)
    for d, (w, b) in enumerate(((L0_conv_w_f, L0_conv_b_f), (L0_conv_w_b, L0_conv_b_b))):
        w, b = arr(w), arr(b)
        for tap in range(3):
            for m in range(2):
                at = (d * 3 + tap) * 2 + m
                for col, gate in ((0, 2 * m), (64, 2 * m + 1)):
                    g = slice(HC * gate, HC * gate + HC)
                    w_gates[0:HC, at, col:col + HC] = w[g, C:, 1, tap].T
                    w_gates[HI:HI + C, at, col:col + HC] = w[g, :C, 1, tap].T
                    if tap == 1:
                        w_gates[HC, at, col:col + HC] = b[g]
    w_proj = np.zeros((P, 64), np.float32)
    w_proj[0:HC, 0:C] = arr(L0_conv_w_proj)[:, :HC].T
    w_proj[HI:HI + HC, 0:C] = arr(L0_conv_w_proj)[:, HC:].T

    norms = np.zeros((P, 4, 8), np.float32)
    for kind, (one, mid, two) in enumerate(((L1_conv_bn1_v, L1_conv_bnd_v, L1_conv_bn2_v),
                                            (L1_conv_bn1_g, L1_conv_bnd_g, L1_conv_bn2_g),
                                            (L1_conv_bn1_b, L1_conv_bnd_b, L1_conv_bn2_b),
                                            (L1_conv_bn1_m, L1_conv_bnd_m, L1_conv_bn2_m))):
        norms[0:HG, kind, 0:NG] = arr(one).reshape(NG, HG).T
        norms[0:HG, kind, NG:2 * NG] = arr(mid).reshape(NG, HG).T
        norms[:, kind, 6] = halves(arr(two))
    norms[:, 1, 7] = halves(arr(L0_conv_gamma))
    norms[:, 2, 7] = halves(arr(L0_conv_beta))

    units = 2 * UNITS
    consts = np.zeros((P, 3 * P + HG + units * UC), np.float32)
    for half in range(2):
        for other in range(2):
            consts[64 * half + np.arange(C), 64 * other + np.arange(C)] = 0.5
    consts[np.arange(P), P + np.arange(P)] = 1.0
    consts[:, 2 * P:3 * P] = 1.0
    consts[0:HG, 3 * P:3 * P + HG] = np.triu(np.ones((HG, HG), np.float32), 1)
    place = np.full((units, UC), -2.0, np.float32)
    place[:, :C] = np.arange(units * C).reshape(units, C)
    consts[:, 3 * P + HG:] = place.reshape(-1)

    w_sal = np.zeros((P, 2, NG, HG), np.float32)
    sal_t = arr(L1_conv_w_sal).T.reshape(C, NG, HG)
    w_sal[LO:LO + C, 0] = sal_t
    w_sal[HI:HI + C, 1] = sal_t
    b_sal = arr(arr(L1_conv_b_sal).reshape(NG, HG).T)
    hid = np.zeros((HG, NG, NPAR), np.float32)
    hid[:, :, TAP:TAP + 9] = arr(L1_conv_w_dw).reshape(NG, HG, 9).transpose(1, 0, 2)
    hid[:, :, W2:W2 + C] = arr(L1_conv_w_pw2).T.reshape(NG, HG, C).transpose(1, 0, 2)
    w_pw1 = np.zeros((HG, NG, 64), np.float32)
    w_pw1[:, :, :C] = arr(L1_conv_w_pw1).reshape(NG, HG, C).transpose(1, 0, 2)
    w_mask = np.zeros((P, P), np.float32)
    w_mask[LO:LO + C, LO:LO + C] = arr(L1_conv_w_mask).reshape(C, 1)
    w_mask[HI:HI + C, HI:HI + C] = arr(L1_conv_w_mask).reshape(C, 1)
    b_mask = np.zeros((P, 1), np.float32)
    b_mask[:] = arr(L1_conv_b_mask)

    x = arr(x)
    ins = {
        "x_rows": arr(x.transpose(2, 1, 0, 3)),
        "x_lanes": arr(x.reshape(2, HB, C, PX).transpose(0, 2, 1, 3).reshape(2, C, HB * PX)),
        "w_gates": w_gates, "w_proj": w_proj, "norms": norms, "consts": consts, "w_sal": w_sal, "b_sal": b_sal,
        "hid": hid, "w_pw1": w_pw1, "w_mask": w_mask, "b_mask": b_mask,
    }
    nc = bacc.Bacc("TRN2", target_bir_lowering=False, num_devices=1)
    args = [nc.dram_tensor(name, a.shape, mybir.dt.from_np(a.dtype), kind="ExternalInput").ap() for name, a in ins.items()]
    args.append(nc.dram_tensor("out", (P, HB * PX), F32, kind="ExternalOutput").ap())
    build(nc, *args)
    r = run_bass_kernel_spmd(nc, [ins], core_ids=[0])
    got = r.results[0]["out"].reshape(2, 64, HB, H, W)[:, :C]
    return np.ascontiguousarray(got.transpose(0, 2, 1, 3, 4).reshape(B, C, H, W))
```

```python
from contextlib import ExitStack

import numpy as np

import concourse.bass as bass
from concourse import mybir

F32 = mybir.dt.float32
F32R = mybir.dt.float32r
I32 = mybir.dt.int32
ACT = mybir.ActivationFunctionType
ALU = mybir.AluOpType
AX = mybir.AxisListType

B, C, H, W = 8, 48, 96, 96
HB = B // 2
HC = 48
HID = 288
P = 128
LO, HI = 0, 64
PX = H * W
NH = HB * W
WP = W + 2
HG = 96
NG = HID // HG
TOPK = 144
EPS = 1e-5
S1, T1, TAP, SD, TD, W2, NPAR = 0, 1, 2, 11, 12, 13, 64
UNITS = 3
UC = 64
PE_TAPS = [0, 1]
ACT_TAPS = [2, 3]
DVE_TAPS = [4, 5, 6, 7, 8]
CH = 8
CPX = CH * W
NCH = H // CH
AGAIN = 6
PKR = 2 * UNITS * P
PKF = UNITS * P + UNITS * len(PE_TAPS) * P + UNITS * 13 + 2
PK_DIAG = UNITS * P
PK_PAR = PK_DIAG + UNITS * len(PE_TAPS) * P
PK_S2 = PK_PAR + UNITS * 13


KINDS = ((0, 1), (1, 4), (4, 7))


def at_least(eng, sem, value):
    if not isinstance(value, int) or value > 0:
        eng.wait_ge(sem, value)


def recurrence(nc, x_steps, w_gates, w_kinds, h_rows):
    STEPS = H
    PASSES = 7
    FULL = B * WP
    AHEAD_X = 2
    with ExitStack() as ctx:
        def sb(name, shape, dt=F32):
            return ctx.enter_context(nc.sbuf_tensor(name, shape, dt))

        def sem(name):
            return ctx.enter_context(nc.semaphore(name))

        kinds = sb("kinds", [P, 2, 2])
        w_raw = sb("w_raw", [P, PASSES, 4, P])
        w_high = sb("w_high", [P, PASSES, 4, P], F32R)
        w_part = sb("w_part", [P, 4, 4, P])
        w_low = sb("w_low", [P, 4, 4, P], F32R)
        spread = [[sb(f"spread{d}{e}", [P, B, WP], F32R) for e in range(2)] for d in range(2)]
        single = [[sb(f"single{d}{e}", [P, B, WP], F32R) for e in range(2)] for d in range(2)]
        double = [[sb(f"double{d}{e}", [P, B, WP], F32R) for e in range(2)] for d in range(2)]
        x_raw = sb("x_raw", [P, 2, B, W])
        x_parts = [sb(f"x_parts{e}", [P, 2, B, WP], F32R) for e in range(2)]
        sig_i, sig_f, tanh_g, sig_o, i_g, f_c, cell, tanh_c = (
            [sb(f"{n}{p}", [P, HB, W]) for p in range(2)]
            for n in ("sig_i", "sig_f", "tanh_g", "sig_o", "i_g", "f_c", "cell", "tanh_c"))
        h_new = [sb(f"h_new{e}", [P, B, W]) for e in range(2)]
        gates = [ctx.enter_context(nc.psum_tensor(f"gates{k}", [P, 2, 512], F32)) for k in range(4)]

        w_loaded = [sem(f"w_loaded{n}") for n in range(3)]
        kinds_loaded, w_high_ready, w_part_ready, w_ready = (
            sem(n) for n in ("kinds_loaded", "w_high_ready", "w_part_ready", "w_ready"))
        raw_in = [sem(f"raw_in{e}") for e in range(2)]
        x_in = [[sem(f"x_in{d}{e}") for e in range(2)] for d in range(2)]
        h_stored = [sem(f"h_stored{e}") for e in range(2)]
        parts_clear, zeroed, odd_zeroed, gates_zero = (
            sem(n) for n in ("parts_clear", "zeroed", "odd_zeroed", "gates_zero"))
        x_high, x_low = sem("x_high"), sem("x_low")
        if_summed, go_summed, if_ready, tg_ready, so_ready = (
            sem(n) for n in ("if_summed", "go_summed", "if_ready", "tg_ready", "so_ready"))
        single_ready, double_ready, lo_ready = (sem(n) for n in ("single_ready", "double_ready", "lo_ready"))
        fc_ready, ig_ready, cell_ready, tc_ready, h_ready = (
            sem(n) for n in ("fc_ready", "ig_ready", "cell_ready", "tc_ready", "h_ready"))

        def halves(p):
            return slice(HB * p, HB * p + HB)

        def lanes(d):
            return slice(HI * d, HI * d + HC)

        def row(d, t):
            return t if d == 0 else t * -1 + (H - 1)

        BOTH = slice(0, HI + HC)
        block = ctx.enter_context(nc.Block())

        def turns(eng, body):
            body(0, True, False)
            with eng.Fori(1, STEPS // 2 - 1) as i:
                body(i, False, False)
            body(STEPS // 2 - 1, False, True)

        @block.sync
        def _(sp):
            def load_raw(t, e):
                sp.dma_start(x_raw[BOTH, e], x_steps[t]).then_inc(raw_in[e], 16)

            def load_x(t, e):
                sp.wait_ge(x_low, t + 1)
                for d in range(2):
                    at_least(sp, go_summed, 4 * t - 5 + d)

                    def flat(a):
                        return a.bitcast(F32).rearrange("p b w -> p (b w)")

                    def parts(c0, c1):
                        return x_parts[e][HI * d + c0:HI * d + c1].bitcast(F32).rearrange("p s b w -> p s (b w)")

                    high = parts(0, 32)
                    taps = bass.AP(tensor=high.tensor, offset=high.offset, ap=[[2 * FULL, 32], [1, 3], [1, FULL - 2]])
                    for to, src in ((flat(spread[d][e][0:96])[:, 0:FULL - 2], taps),
                                    (flat(single[d][e][48:112]), high),
                                    (flat(single[d][e][112:128]), parts(32, 48)[:, 0]),
                                    (flat(double[d][e][48:64]), parts(32, 40)),
                                    (flat(double[d][e][112:128]), parts(40, 48))):
                        sp.dma_start(to, src).then_inc(x_in[d][e], 16)

            def store_h(t, e):
                sp.wait_ge(h_ready, 2 * t + 2)
                for d in range(2):
                    sp.dma_start(h_rows[row(d, t), d], h_new[e][lanes(d)]).then_inc(h_stored[e], 16)

            load_raw(0, 0)
            for n, (a, b) in enumerate(KINDS):
                sp.dma_start(w_raw[:, a:b], w_gates[:, a:b]).then_inc(w_loaded[n], 16)
                if n == 0:
                    sp.dma_start(kinds[:], w_kinds).then_inc(kinds_loaded, 16)
            load_raw(1, 1)
            sp.wait_ge(zeroed, 8)
            load_x(0, 0)
            sp.wait_ge(odd_zeroed, 4)

            def body(i, first, last):
                for e in range(2):
                    t = 2 * i + e
                    if not last:
                        load_raw(t + AHEAD_X, e)
                    if not (last and e == 1):
                        load_x(t + 1, 1 - e)
                    if not (first and e == 0):
                        store_h(t - 1, 1 - e)

            turns(sp, body)
            store_h(STEPS - 1, 1)
            for e in range(2):
                sp.wait_ge(h_stored[e], 32 * STEPS // 2)

        @block.tensor
        def _(pe):
            pe.wait_ge(zeroed, 8)

            def body(i, first, last):
                for k in range(8):
                    e, p, d = k // 4, k % 4 // 2, k % 2
                    t, s = 2 * i + e, 8 * i + k
                    if p == 0:
                        pe.wait_ge(x_in[d][e], 80 * (i + 1))
                    at_least(pe, so_ready, s - 3)
                    for m in range(2):
                        for n in range(PASSES):
                            if first and k == 0 and m == 0 and n in (0, 1):
                                pe.wait_ge(w_ready, n + 1)
                            if first and k == 0 and m == 0 and n == 4:
                                pe.wait_ge(w_high_ready, 3)
                            if m == 0 and n == 1:
                                at_least(pe, single_ready, s - 3)
                            if m == 0 and n == 4:
                                at_least(pe, double_ready, s - 3)
                                at_least(pe, lo_ready, s - 3)
                            moving, tap = ((spread, 0) if n == 0 else (single, n - 1) if n < 4 else (double, n - 4))
                            mm = nc.tensor.matmul(gates[k % 4][:, m, 0:NH], (w_high if n >= 4 else w_low)[:, n, 2 * d + m, :],
                                                  moving[d][e][:, halves(p), tap:tap + W],
                                                  start=(n == 0), stop=(n == PASSES - 1))
                        mm.then_inc(go_summed if m else if_summed, 1)

            turns(pe, body)

        @block.scalar
        def _(act):
            for n, (a, b) in enumerate(KINDS):
                act.wait_ge(w_loaded[n], 16)
                nc.scalar.activation(w_high[:, a:b], w_raw[:, a:b], ACT.Copy).then_inc(w_high_ready, 1)
            act.wait_ge(gates_zero, 1)

            def body(i, first, last):
                for k in range(8):
                    p, d = k % 4 // 2, k % 2
                    s = 8 * i + k
                    g = gates[k % 4]
                    act.wait_ge(if_summed, s + 1)
                    nc.scalar.activation(sig_i[p][lanes(d)], g[0:HC, 0, 0:NH], ACT.Sigmoid)
                    nc.scalar.activation(sig_f[p][lanes(d)], g[HI:HI + HC, 0, 0:NH], ACT.Sigmoid).then_inc(if_ready, 1)
                    act.wait_ge(go_summed, s + 1)
                    nc.scalar.activation(tanh_g[p][lanes(d)], g[0:HC, 1, 0:NH], ACT.Tanh).then_inc(tg_ready, 1)
                    nc.scalar.activation(sig_o[p][lanes(d)], g[HI:HI + HC, 1, 0:NH], ACT.Sigmoid).then_inc(so_ready, 1)
                    if d == 1:
                        q = 4 * i + k // 2
                        act.wait_ge(cell_ready, q + 1)
                        nc.scalar.activation(tanh_c[p][BOTH], cell[p][BOTH], ACT.Tanh).then_inc(tc_ready, 1)

            turns(act, body)

        @block.vector
        def _(dve):
            for e in range(2):
                nc.vector.memset(x_parts[e][:].bitcast(F32), 0.0).then_inc(parts_clear, 1)
            for d in range(2):
                nc.vector.memset(single[d][0][:].bitcast(F32), 0.0).then_inc(zeroed, 1)
                nc.vector.memset(double[d][0][:].bitcast(F32), 0.0).then_inc(zeroed, 1)
            dve.wait_ge(parts_clear, 2)

            def high_x(e, loaded, moved):
                dve.wait_ge(raw_in[e], loaded)
                for d in range(2):
                    at_least(dve, x_in[d][e], moved)
                nc.vector.tensor_copy(x_parts[e][BOTH, 0, :, 1:1 + W], x_raw[BOTH, e]).then_inc(x_high, 1)

            def low_x0(b, e):
                dve.wait_ge(x_high, b + 1)
                nc.vector.tensor_tensor(x_parts[e][BOTH, 1, :, 1:1 + W], x_raw[BOTH, e],
                                        x_parts[e][BOTH, 0, :, 1:1 + W], ALU.subtract).then_inc(x_low, 1)

            for b in range(AHEAD_X):
                high_x(b, 16, 0)
                low_x0(b, b)
            for a in (sig_i, sig_f, tanh_g, sig_o, cell):
                for p in range(2):
                    clear = nc.vector.memset(a[p][:] if a is cell else a[p][32:64], 0.0)
            clear.then_inc(gates_zero, 1)
            dve.wait_ge(kinds_loaded, 16)
            for n, (a, b) in enumerate(KINDS[:2]):
                dve.wait_ge(w_high_ready, n + 1)
                nc.vector.tensor_scalar(w_part[:, a:b], w_high[:, a:b].bitcast(F32), kinds[:, 1, n:n + 1], None,
                                        ALU.mult).then_inc(w_part_ready, 1)
                dve.wait_ge(w_part_ready, n + 1)
                nc.vector.scalar_tensor_tensor(w_low[:, a:b], w_raw[:, a:b], kinds[:, 0, n:n + 1], w_part[:, a:b],
                                               ALU.mult, ALU.add).then_inc(w_ready, 1)
            dve.wait_ge(gates_zero, 1)

            def body(i, first, last):
                for k in range(0, 8, 2):
                    e, p = k // 4, k % 4 // 2
                    t, s, q = 2 * i + e, 8 * i + k, 4 * i + k // 2
                    if p == 0 and not last:
                        high_x(e, 16 * (i + 2), 80 * (i + 1))
                    dve.wait_ge(if_ready, s + 2)
                    at_least(dve, cell_ready, q - 1)
                    nc.vector.tensor_tensor(f_c[p][BOTH], sig_f[p][BOTH], cell[p][BOTH], ALU.mult).then_inc(fc_ready, 1)
                    dve.wait_ge(tg_ready, s + 2)
                    nc.vector.tensor_tensor(i_g[p][BOTH], sig_i[p][BOTH], tanh_g[p][BOTH], ALU.mult).then_inc(ig_ready, 1)
                    dve.wait_ge(fc_ready, q + 1)
                    dve.wait_ge(ig_ready, q + 1)
                    nc.vector.tensor_tensor(cell[p][BOTH], f_c[p][BOTH], i_g[p][BOTH], ALU.add).then_inc(cell_ready, 1)
                    dve.wait_ge(tc_ready, q + 1)
                    dve.wait_ge(so_ready, s + 2)
                    at_least(dve, h_stored[e], 32 * i)
                    at_least(dve, lo_ready, s - 6)
                    nc.vector.tensor_tensor(h_new[e][BOTH, halves(p)], sig_o[p][BOTH], tanh_c[p][BOTH], ALU.mult).then_inc(h_ready, 1)
                    dve.wait_ge(h_ready, q + 1)
                    for d in range(2):
                        nc.vector.tensor_copy(single[d][1 - e][0:HC, halves(p), 1:1 + W],
                                              h_new[e][lanes(d), halves(p)]).then_inc(single_ready, 1)
                        nc.vector.tensor_copy(double[d][1 - e][lanes(d), halves(p), 1:1 + W],
                                              h_new[e][lanes(d), halves(p)]).then_inc(double_ready, 1)

            dve.wait_ge(odd_zeroed, 4)
            turns(dve, body)

        @block.gpsimd
        def _(pool):
            for d in range(2):
                nc.gpsimd.memset(double[d][1][:].bitcast(F32), 0.0).then_inc(odd_zeroed, 1)
                nc.gpsimd.memset(single[d][1][:].bitcast(F32), 0.0).then_inc(odd_zeroed, 1)
            pool.wait_ge(odd_zeroed, 4)
            for d in range(2):
                for e in range(2):
                    nc.gpsimd.memset(spread[d][e][96:128].bitcast(F32), 1.0).then_inc(zeroed, 1)

            pool.wait_ge(zeroed, 8)

            def body(i, first, last):
                for k in range(8):
                    e, p, d = k // 4, k % 4 // 2, k % 2
                    s = 8 * i + k
                    if k % 4 == 0 and not last:
                        b = 2 * i + e + AHEAD_X
                        pool.wait_ge(x_high, b + 1)
                        at_least(pool, lo_ready, s)
                        nc.gpsimd.tensor_tensor(x_parts[e][BOTH, 1, :, 1:1 + W], x_raw[BOTH, e],
                                                x_parts[e][BOTH, 0, :, 1:1 + W], ALU.subtract).then_inc(x_low, 1)
                        pool.wait_ge(x_low, b + 1)
                    pool.wait_ge(double_ready, s + 1)
                    at_least(pool, lo_ready, s)
                    own, other = lanes(d), lanes(1 - d)
                    nc.gpsimd.tensor_tensor(double[d][1 - e][other, halves(p), 1:1 + W], h_new[e][own, halves(p)],
                                            double[d][1 - e][own, halves(p), 1:1 + W], ALU.subtract).then_inc(lo_ready, 1)

            turns(pool, body)


def projection(nc, h_rows, w_proj, y, stats):
    ROWS, BUFS = 2, 4
    TURN = ROWS * BUFS
    with ExitStack() as ctx:
        def sem(name):
            return ctx.enter_context(nc.semaphore(name))

        wp = ctx.enter_context(nc.sbuf_tensor("wp", [P, 64], F32))
        h_in = [ctx.enter_context(nc.sbuf_tensor(f"h_in{n}", [P, ROWS, B, W], F32)) for n in range(BUFS)]
        ps = ctx.enter_context(nc.psum_tensor("proj", [P, TURN, 512], F32))
        wp_loaded, gaps_zero = sem("wp_loaded"), sem("gaps_zero")
        h_loaded = [sem(f"h_loaded{n}") for n in range(BUFS)]
        row_summed, row_kept, row_measured = sem("row_summed"), sem("row_kept"), sem("row_measured")
        block = ctx.enter_context(nc.Block())

        @block.sync
        def _(sp):
            sp.dma_start(wp[:], w_proj).then_inc(wp_loaded, 16)
            sp.wait_ge(gaps_zero, BUFS)

            def body(i, first):
                for n in range(BUFS):
                    r = TURN * i + ROWS * n
                    at_least(sp, row_summed, r - TURN + ROWS)
                    for d in range(2):
                        sp.dma_start(h_in[n][64 * d:64 * d + HC],
                                     h_rows[bass.ds(r, ROWS), d].rearrange("r c b w -> c r b w")).then_inc(h_loaded[n], 16)

            body(0, True)
            with sp.Fori(1, H // TURN) as i:
                body(i, False)

        @block.tensor
        def _(pe):
            pe.wait_ge(wp_loaded, 16)

            def body(i, first):
                for k in range(TURN):
                    if k % ROWS == 0:
                        pe.wait_ge(h_loaded[k // ROWS], 32 * i + 32)
                    at_least(pe, row_kept, TURN * (i - 1) + k + 1)
                    for half in range(2):
                        mm = nc.tensor.matmul(ps[64 * half:64 * half + 64, k, 0:NH], wp[:],
                                              h_in[k // ROWS][:, k % ROWS, HB * half:HB * half + HB, :],
                                              start=True, stop=True)
                    mm.then_inc(row_summed, 1)

            body(0, True)
            with pe.Fori(1, H // TURN) as i:
                body(i, False)

        @block.scalar
        def _(act):
            with act.Fori(0, H // TURN) as i:
                for k in range(TURN):
                    act.wait_ge(row_summed, TURN * i + k + 1)
                    nc.scalar.activation(y[:, :, bass.ds(TURN * i + k, 1), :],
                                         ps[:, k, 0:NH].rearrange("p (b r w) -> p b r w", b=HB, r=1),
                                         ACT.Identity).then_inc(row_kept, 1)

        @block.vector
        def _(dve):
            for n in range(BUFS):
                nc.vector.memset(h_in[n][:], 0.0).then_inc(gaps_zero, 1)
            with dve.Fori(0, H // TURN) as i:
                for k in range(TURN):
                    dve.wait_ge(row_kept, TURN * i + k + 1)
                    nc.vector.bn_stats(stats[:, bass.ds((TURN * i + k) * 6, 6)],
                                       y[:, :, bass.ds(TURN * i + k, 1), :]).then_inc(row_measured, 1)
            dve.wait_ge(row_measured, H)


def residual(nc, y, stats, consts, norms, x_lanes, x1_lanes, sums, folded):
    PART = 16 * W
    PARTS = HB * PX // PART
    BUFS = 4
    REPEATED = AGAIN * CPX // PART
    with ExitStack() as ctx:
        def sb(name, shape, dt=F32):
            return ctx.enter_context(nc.sbuf_tensor(name, shape, dt))

        def sem(name):
            return ctx.enter_context(nc.semaphore(name))

        pairing = sb("pairing", [P, P])
        nv = sb("nv", [P, 4, 8])
        half_stat = sb("half_stat", [P, 2])
        moments = sb("moments", [P, 2])
        root = sb("root", [P, 8])
        ratio = sb("ratio", [P, 8])
        tmp = sb("tmp", [P, 8])
        x_in = [sb(f"x_in{n}", [P, PART]) for n in range(BUFS)]
        part_sums = sb("part_sums", [P, PARTS])
        ps = ctx.enter_context(nc.psum_tensor("moment_ps", [P, 2], F32))
        pairing_loaded, nv_loaded, x_gaps = sem("pairing_loaded"), sem("nv_loaded"), sem("x_gaps")
        x_loaded = [sem(f"x2_loaded{n}") for n in range(BUFS)]
        x1_stored = [sem(f"x1_stored{n}") for n in range(BUFS)]
        step, averaged, rooted, relued, added = (sem(n) for n in ("step", "averaged", "rooted", "relued", "added"))
        block = ctx.enter_context(nc.Block())

        @block.sync
        def _(sp):
            sp.dma_start(pairing[:], consts[:, 0:P]).then_inc(pairing_loaded, 16)
            sp.dma_start(nv[:], norms).then_inc(nv_loaded, 16)
            sp.wait_ge(x_gaps, BUFS)

            def load(i, n):
                for half in range(2):
                    sp.dma_start(x_in[n][64 * half:64 * half + C],
                                 x_lanes[half, :, bass.ds((BUFS * i + n) * PART, PART)]).then_inc(x_loaded[n], 16)

            for n in range(BUFS):
                load(0, n)
            with sp.Fori(1, PARTS // BUFS) as i:
                for n in range(BUFS):
                    sp.wait_ge(x1_stored[n], 16 * i + (16 if n < REPEATED else 0))
                    load(i, n)

        @block.gpsimd
        def _(pool):
            def store(i, n, at):
                pool.wait_ge(added, BUFS * i + n + 1)
                pool.dma_start(x1_lanes[:, bass.ds(at * PART, PART)], x_in[n][:]).then_inc(x1_stored[n], 16)

            for n in range(BUFS):
                store(0, n, n)
                if n < REPEATED:
                    store(0, n, PARTS + n)
            with pool.Fori(1, PARTS // BUFS) as i:
                for n in range(BUFS):
                    store(i, n, BUFS * i + n)
            for n in range(BUFS):
                pool.wait_ge(x1_stored[n], 16 * (PARTS // BUFS) + (16 if n < REPEATED else 0))

        @block.tensor
        def _(pe):
            pe.wait_ge(pairing_loaded, 16)
            pe.wait_ge(step, 3)
            nc.tensor.matmul(ps[:], pairing[:], moments[:], start=True, stop=True).then_inc(averaged, 1)

        @block.scalar
        def _(act):
            act.wait_ge(step, 6)
            nc.scalar.activation(root[:], tmp[:], ACT.Sqrt).then_inc(rooted, 1)
            act.wait_ge(step, 13)
            with act.Fori(0, PARTS // BUFS) as i:
                for n in range(BUFS):
                    at = y[:].rearrange("p b r w -> p (b r w)")[:, bass.ds((BUFS * i + n) * PART, PART)]
                    nc.scalar.activation(at, at, ACT.Relu, bias=folded[:, 1, 7:8],
                                         scale=folded[:, 0, 7:8]).then_inc(relued, 1)

        @block.vector
        def _(dve):
            for n in range(BUFS):
                nc.vector.memset(x_in[n][:], 0.0).then_inc(x_gaps, 1)
            count = [0]

            def then(ins):
                count[0] += 1
                ins.then_inc(step, 1)
                dve.wait_ge(step, count[0])

            then(nc.vector.bn_aggr(half_stat[:], stats[:]))
            then(nc.vector.tensor_copy(moments[:, 0:1], half_stat[:, 0:1]))
            then(nc.vector.scalar_tensor_tensor(moments[:, 1:2], half_stat[:, 0:1], half_stat[:, 0:1],
                                                half_stat[:, 1:2], ALU.mult, ALU.add))
            dve.wait_ge(averaged, 1)
            dve.wait_ge(nv_loaded, 16)
            then(nc.vector.tensor_copy(half_stat[:], ps[:]))
            nc.vector.tensor_copy(nv[:, 3, 7:8], half_stat[:, 0:1]).then_inc(x_gaps, 1)
            dve.wait_ge(x_gaps, BUFS + 1)
            nc.vector.tensor_scalar(ratio[:, 0:1], half_stat[:, 0:1], half_stat[:, 0:1], -1.0, ALU.mult,
                                    ALU.mult).then_inc(x_gaps, 1)
            dve.wait_ge(x_gaps, BUFS + 2)
            then(nc.vector.tensor_tensor(nv[:, 0, 7:8], ratio[:, 0:1], half_stat[:, 1:2], ALU.add))
            then(nc.vector.tensor_scalar(tmp[:], nv[:, 0, :], EPS, None, ALU.add))
            dve.wait_ge(rooted, 1)
            then(nc.vector.reciprocal(ratio[:], root[:]))
            then(nc.vector.tensor_tensor(ratio[:], ratio[:], tmp[:], ALU.mult))
            then(nc.vector.tensor_tensor(ratio[:], ratio[:], root[:], ALU.add))
            then(nc.vector.tensor_scalar(root[:], ratio[:], 0.5, None, ALU.mult))
            then(nc.vector.reciprocal(ratio[:], root[:]))
            then(nc.vector.tensor_tensor(folded[:, 0, :], ratio[:], nv[:, 1, :], ALU.mult))
            nc.vector.tensor_tensor(tmp[:], folded[:, 0, :], nv[:, 3, :], ALU.mult).then_inc(x_gaps, 1)
            dve.wait_ge(x_gaps, BUFS + 3)
            then(nc.vector.tensor_tensor(folded[:, 1, :], nv[:, 2, :], tmp[:], ALU.subtract))
            with dve.Fori(0, PARTS // BUFS) as i:
                for n in range(BUFS):
                    dve.wait_ge(relued, BUFS * i + n + 1)
                    dve.wait_ge(x_loaded[n], 32 * i + 32)
                    at = y[:].rearrange("p b r w -> p (b r w)")[:, bass.ds((BUFS * i + n) * PART, PART)]
                    nc.vector.scalar_tensor_tensor(x_in[n][:], at, 1.0, x_in[n][:], ALU.mult, ALU.add,
                                                   accum_out=part_sums[:, bass.ds(BUFS * i + n, 1)]).then_inc(added, 1)
            dve.wait_ge(added, PARTS)
            then(nc.vector.tensor_reduce(sums[:], part_sums[:].rearrange("p (b n) -> p b n", b=HB), AX.X, ALU.add))


def selection(nc, consts, w_sal, b_sal, hid, w_pw1, sums, folded, packs_r, packs_f, passes):
    PASSES = 2
    NU = PASSES * UNITS
    with ExitStack() as ctx:
        def sb(name, shape, dt=F32):
            return ctx.enter_context(nc.sbuf_tensor(name, shape, dt))

        def sem(name):
            return ctx.enter_context(nc.semaphore(name))

        cst = sb("cst", [P, 3 * P + HG + NU * UC])
        ident, ones = cst[:, P:2 * P], cst[:, 2 * P:3 * P]
        before = cst[:, 3 * P:3 * P + HG]
        places = cst[:, 3 * P + HG:]
        ws = sb("ws", [P, 2, NG, HG])
        bs = sb("bs", [HG, NG])
        par = sb("par", [HG, NG, NPAR])
        w1 = sb("w1", [HG, NG, 64])
        sal = sb("sal", [HG, NG, B])
        spread = [sb(f"spread{n}", [HG, NG, HG]) for n in range(2)]
        above = sb("above", [HG, NG, B])
        chosen = sb("chosen", [HG, NG, B])
        place = sb("place", [HG, NG, B])
        scratch = sb("scratch", [HG, NG, HID])
        onehot = [sb(f"onehot{n}", [HG, NG, NU * UC]) for n in range(2)]
        pack_r = [sb(f"pack_r{n}", [P, PKR], F32R) for n in range(2)]
        pack_f = [sb(f"pack_f{n}", [P, PKF]) for n in range(2)]
        most = sb("most", [HG, 1])
        ps_s = ctx.enter_context(nc.psum_tensor("ps_s", [P, NG, B], F32))
        ps_b = [ctx.enter_context(nc.psum_tensor(f"ps_b{n}", [P, 512], F32)) for n in range(2)]
        ps_p = ctx.enter_context(nc.psum_tensor("ps_p", [P, NG, B], F32))
        ps_t = ctx.enter_context(nc.psum_tensor("ps_t", [P, B], F32))
        ps_w = ctx.enter_context(nc.psum_tensor("ps_w", [P, 512], F32))
        ps_q = ctx.enter_context(nc.psum_tensor("ps_q", [P, 512], F32))
        loaded, dve_did, pe_did, act_did = (sem(n) for n in ("s_loaded", "dve_did", "pe_did", "act_did"))
        stored = [sem(f"pk_stored{n}") for n in range(2)]
        block = ctx.enter_context(nc.Block())
        d, t = [0], [0]
        marks = {}

        @block.sync
        def _(sp):
            sp.dma_start(cst[:], consts).then_inc(loaded, 16)
            sp.dma_start(ws[:], w_sal).then_inc(loaded, 16)
            sp.dma_start(bs[:], b_sal).then_inc(loaded, 16)
            sp.dma_start(par[:], hid).then_inc(loaded, 16)
            sp.dma_start(w1[:], w_pw1).then_inc(loaded, 16)

        @block.vector
        def _(dve):
            def do(ins, wait=True):
                d[0] += 1
                ins.then_inc(dve_did, 1)
                if wait:
                    dve.wait_ge(dve_did, d[0])

            dve.wait_ge(loaded, 80)
            for g in range(NG):
                do(nc.vector.tensor_copy(par[:, g, S1:T1 + 1], folded[0:HG, :, g]), False)
                do(nc.vector.tensor_copy(par[:, g, SD:TD + 1], folded[0:HG, :, NG + g]), False)
            dve.wait_ge(act_did, NG)
            def spread_out(b):
                for g in range(NG):
                    do(nc.vector.tensor_scalar(spread[b % 2][:, g, :], ident[0:HG, 0:HG], sal[:, g, b:b + 1], None,
                                               ALU.mult), False)
                marks["spread", b] = d[0]

            spread_out(0)
            for b in range(B):
                if b + 1 < B:
                    spread_out(b + 1)
                dve.wait_ge(pe_did, marks_pe("spread", b))
                if b:
                    dve.wait_ge(dve_did, marks["counted", b - 1])
                for g in range(NG):
                    do(nc.vector.tensor_scalar(scratch[:, g, :], ps_b[b % 2][0:HG, 0:HID], sal[:, g, b:b + 1], 0.0,
                                               ALU.is_gt, ALU.add, accum_out=above[:, g, b:b + 1]), False)
                marks["counted", b] = d[0]
            dve.wait_ge(dve_did, d[0])
            do(nc.vector.tensor_scalar(chosen[:], above[:], float(TOPK), None, ALU.is_lt))
            marks["chosen"] = d[0]
            dve.wait_ge(pe_did, marks_pe("places", 0))
            do(nc.vector.scalar_tensor_tensor(place[:], ps_p[0:HG], 1.0, chosen[:], ALU.add, ALU.mult))
            do(nc.vector.tensor_scalar(place[:], place[:], -1.0, None, ALU.add))
            do(nc.vector.tensor_reduce(most[:], ps_t[0:HG], AX.X, ALU.max))
            do(nc.vector.tensor_scalar(passes[0:1, 0:1], most[0:1], float(TOPK), 1.0, ALU.is_gt, ALU.add))
            for n in range(2):
                do(nc.vector.memset(pack_r[n][:].bitcast(F32), 0.0), False)
                do(nc.vector.memset(pack_f[n][:], 0.0), n == 1)
            for pair in range(HB):
                for half in range(2):
                    b = HB * half + pair
                    for g in range(NG):
                        do(nc.vector.tensor_scalar(onehot[half][:, g, :], places[0:HG], place[:, g, b:b + 1], None,
                                                   ALU.is_equal), False)
                marks["onehot", pair] = d[0]
                for q in range(PASSES):
                    n = HB * q + pair
                    dve.wait_ge(pe_did, marks_pe("pack", n))
                    at_least(dve, stored[q], 32 * pair)
                    r = pack_r[q][:].rearrange("p (k u m) -> p k u m", k=2, u=UNITS)
                    f = pack_f[q][:, 0:UNITS * P].rearrange("p (u m) -> p u m", u=UNITS)
                    for half in range(2):
                        lanes = slice(64 * half, 64 * half + 64)
                        src = ps_w[lanes, 0:NU * UC].rearrange("p (u r) -> p u r", u=NU)[:, UNITS * q:UNITS * q + UNITS, :]
                        got = ps_q[lanes, 0:UNITS * NPAR].rearrange("p (u m) -> p u m", u=UNITS)
                        do(nc.vector.tensor_copy(r[lanes, 0, :, lanes], src), False)
                        do(nc.vector.tensor_copy(f[lanes, :, 64 * half:64 * half + HC], got[:, :, W2:W2 + HC]), False)
                    got = ps_q[:, 0:UNITS * NPAR].rearrange("p (u m) -> p u m", u=UNITS)
                    do(nc.vector.tensor_copy(pack_f[q][:, PK_PAR:PK_S2].rearrange("p (u m) -> p u m", u=UNITS),
                                             got[:, :, 0:W2]))
                    for half in range(2):
                        lanes = slice(64 * half, 64 * half + 64)
                        src = ps_w[lanes, 0:NU * UC].rearrange("p (u r) -> p u r", u=NU)[:, UNITS * q:UNITS * q + UNITS, :]
                        do(nc.vector.tensor_tensor(r[lanes, 1, :, lanes], src, r[lanes, 0, :, lanes], ALU.subtract), False)
                    for u in range(UNITS):
                        for k, tap in enumerate(PE_TAPS):
                            at = PK_DIAG + (u * len(PE_TAPS) + k) * P
                            col = PK_PAR + u * 13 + TAP + tap
                            do(nc.vector.tensor_scalar(pack_f[q][:, at:at + P], ident, pack_f[q][:, col:col + 1], None,
                                                       ALU.mult), False)
                    if pair == 0:
                        do(nc.vector.tensor_copy(pack_f[q][:, PK_S2:PK_S2 + 1], folded[:, 0, 6:7]), False)
                        if q == 0:
                            do(nc.vector.tensor_copy(pack_f[q][:, PK_S2 + 1:PK_S2 + 2], folded[:, 1, 6:7]), False)
                    marks["packed", n] = d[0]

        @block.scalar
        def _(act):
            act.wait_ge(pe_did, 1)
            for g in range(NG):
                nc.scalar.activation(sal[:, g, :], ps_s[0:HG, g, :], ACT.Sigmoid, bias=bs[:, g:g + 1],
                                     scale=1.0 / PX).then_inc(act_did, 1)

        @block.tensor
        def _(pe):
            def did(mm, name):
                mm.then_inc(pe_did, 1)
                t[0] += 1
                assert t[0] == marks_pe(*name), name

            pe.wait_ge(loaded, 80)
            for g in range(NG):
                for half in range(2):
                    mm = nc.tensor.matmul(ps_s[0:HG, g, HB * half:HB * half + HB], ws[:, half, g, :], sums[:],
                                          start=(g == 0 and half == 0), stop=(g == NG - 1 and half == 1),
                                          skip_group_check=True)
            did(mm, ("sal", 0))
            for b in range(B):
                pe.wait_ge(dve_did, marks["spread", b])
                if b >= 2:
                    pe.wait_ge(dve_did, marks["counted", b - 2])
                did(nc.tensor.matmul(ps_b[b % 2][0:HG, 0:HID], ones[0:HG, 0:HG], spread[b % 2][:], start=True, stop=True),
                    ("spread", b))
            pe.wait_ge(dve_did, marks["chosen"])
            first = True
            for g in range(NG):
                for k in range(g + 1):
                    nc.tensor.matmul(ps_p[0:HG, g, :], (before if k == g else ones)[0:HG, 0:HG], chosen[:, k, :],
                                     start=first, stop=(g == NG - 1 and k == g), skip_group_check=True)
                    first = False
            for g in range(NG):
                mm = nc.tensor.matmul(ps_t[0:HG, :], ones[0:HG, 0:HG], chosen[:, g, :], start=(g == 0), stop=(g == NG - 1))
            did(mm, ("places", 0))
            for pair in range(HB):
                pe.wait_ge(dve_did, marks["onehot", pair])
                for q in range(PASSES):
                    n = HB * q + pair
                    for half in range(2):
                        lanes = slice(64 * half, 64 * half + 64)
                        if q == 0:
                            for g in range(NG):
                                nc.tensor.matmul(ps_w[lanes, 0:NU * UC], w1[:, g, :], onehot[half][:, g, :],
                                                 start=(g == 0), stop=(g == NG - 1))
                        else:
                            pe.wait_ge(dve_did, marks["packed", pair])
                        for u in range(UNITS):
                            for g in range(NG):
                                at = (UNITS * q + u) * UC
                                mm = nc.tensor.matmul(ps_q[lanes, u * NPAR:(u + 1) * NPAR], onehot[half][:, g, at:at + UC],
                                                      par[:, g, :], start=(g == 0), stop=(g == NG - 1),
                                                      skip_group_check=True)
                    did(mm, ("pack", n))

        @block.gpsimd
        def _(pool):
            for pair in range(HB):
                for q in range(PASSES):
                    n = HB * q + pair
                    pool.wait_ge(dve_did, marks["packed", n])
                    pool.dma_start(packs_r[n], pack_r[q][:].bitcast(F32)).then_inc(stored[q], 16)
                    pool.dma_start(packs_f[n], pack_f[q][:]).then_inc(stored[q], 16)
            pool.dma_start(packs_r[2 * HB], pack_r[1][:].bitcast(F32)).then_inc(stored[1], 16)
            pool.dma_start(packs_f[2 * HB], pack_f[1][:]).then_inc(stored[1], 16)
            pool.wait_ge(stored[0], 32 * HB)
            pool.wait_ge(stored[1], 32 * (HB + 1))


def marks_pe(what, n):
    if what == "sal":
        return 1
    if what == "spread":
        return 2 + n
    if what == "places":
        return 2 + B
    return 3 + B + 2 * (n % HB) + n // HB


def bottleneck(nc, w_mask, b_mask, x1_lanes, out_lanes, packs_r, packs_f, passes):
    AHEAD = 3
    NT = len(DVE_TAPS)
    with ExitStack() as ctx:
        def sb(name, shape, dt=F32):
            return ctx.enter_context(nc.sbuf_tensor(name, shape, dt))

        def sem(name):
            return ctx.enter_context(nc.semaphore(name))

        pk_r = [sb(f"pk_r{n}", [P, PKR], F32R) for n in range(2)]
        pk_f = [sb(f"pk_f{n}", [P, PKF]) for n in range(2)]
        wm_raw, bm = sb("wm_raw", [P, P]), sb("bm", [P, 1])
        wm = [sb("wm_hi", [P, P], F32R), sb("wm_lo", [P, P], F32R)]
        x1 = [sb(f"x1_{n}", [P, CPX]) for n in range(3)]
        xh = [sb(f"xh{n}", [P, CPX], F32R) for n in range(3)]
        xl = [sb(f"xl{n}", [P, CPX], F32R) for n in range(3)]
        base = [sb(f"base{n}", [P, CPX]) for n in range(3)]
        outb = [sb(f"outb{n}", [P, CPX]) for n in range(3)]
        mask = [sb(f"mask{n}", [P, CPX]) for n in range(3)]
        h1 = sb("h1", [P, UNITS, 3, CH + 2, WP])
        acc = [sb(f"acc{n}", [P, CPX]) for n in range(3)]
        prod = [[sb(f"prod{n}{m}", [P, CPX]) for m in range(2)] for n in range(3)]
        full = [sb(f"full{n}", [P, CPX]) for n in range(3)]
        h2 = [sb(f"h2_{n}", [P, CPX]) for n in range(3)]
        zeros = sb("zeros", [P, UNITS, WP])
        z = sb("z", [P, CPX])
        zm = sb("zm", [P, CPX])
        ps1 = [ctx.enter_context(nc.psum_tensor(f"ps1_{n}", [P, 2, 512], F32)) for n in range(2)]
        psd = ctx.enter_context(nc.psum_tensor("psd", [P, 2, 512], F32))
        ps2 = ctx.enter_context(nc.psum_tensor("ps2", [P, 2, 512], F32))

        mask_loaded, wm_split, borders = sem("mask_loaded"), sem("wm_split"), sem("borders")
        pack_in = [sem(f"pack_in{n}") for n in range(2)]
        x1_in = [sem(f"x1_in{n}") for n in range(3)]
        base_in = [sem(f"base_in{n}") for n in range(3)]
        out_stored = [sem(f"out_stored{n}") for n in range(3)]
        xh_done, xl_done, mask_done, z_done, zm_done, out_done = (
            sem(n) for n in ("xh_done", "xl_done", "mask_done", "z_done", "zm_done", "out_done"))
        pw1_done = sem("pw1_done")
        relu1_done, taps_done, psd_read, chain, acc_done, prod_done, pair_sum, full_done, relu2_done, pw2_done = (
            sem(n) for n in ("relu1_done", "taps_done", "psd_read", "chain", "acc_done", "prod_done", "pair_sum",
                             "full_done", "relu2_done", "pw2_done"))
        above_done, below_done = sem("above_done"), sem("below_done")

        def rows(ap):
            return ap.rearrange("p (m r w) -> p m r w", m=2, w=W)

        def banks(ps):
            return ps[:, :, 0:NH].rearrange("p m (r w) -> p m r w", w=W)

        def window(j, slot, tap):
            dy, dx = divmod(tap, 3)
            return h1[:, j, slot, dy:dy + CH, dx:dx + W].rearrange("p (m r) w -> p m r w", m=2)

        def par(pp, j, col):
            return pk_f[pp][:, PK_PAR + 13 * j + col:PK_PAR + 13 * j + col + 1]

        def run(eng, step):
            step(0, 0, lambda k: 0, 0, 0)
            n = eng.value_load(passes[0:1, 0:1], min_val=1, max_val=2)
            with eng.Fori(0, n * (HB // 2)) as o:
                for pp in range(2):
                    def pack(k):
                        return 1 - pp if isinstance(k, int) and k >= NCH else pp

                    for k in (1, 2):
                        step(2 * o + pp, k, pack, k, 0)
                    with eng.Fori(1, 3) as m:
                        for e in range(3):
                            step(2 * o + pp, 3 * m + e, lambda k: pp, e, m)
                    for k in range(9, NCH + 1):
                        step(2 * o + pp, k, pack, k % 3, k // 3)

        def chunk0(Pi):
            return NCH * Pi + AHEAD

        def nth(Pi, third):
            return 64 * Pi + 16 * third + 16

        def pack_count(Pi, pp):
            return 16 * (Pi - pp) + 32

        block = ctx.enter_context(nc.Block())

        @block.sync
        def _(sp):
            sp.dma_start(wm_raw[:], w_mask).then_inc(mask_loaded, 16)
            sp.dma_start(bm[:], b_mask).then_inc(mask_loaded, 16)
            sp.dma_start(pk_r[0][:].bitcast(F32), packs_r[0]).then_inc(pack_in[0], 16)
            sp.dma_start(pk_f[0][:], packs_f[0]).then_inc(pack_in[0], 16)
            for n in range(3):
                sp.sem_inc(out_stored[n], 16)
            for k in range(5):
                if k >= 3:
                    sp.wait_ge(xl_done, AHEAD + k - 2)
                sp.dma_start(x1[k % 3][:], x1_lanes[:, k * CPX:(k + 1) * CPX]).then_inc(x1_in[k % 3], 16)
            npass = sp.value_load(passes[0:1, 0:1], min_val=1, max_val=2)

            def one_pass(q):
                before = x1_lanes if q == 0 else out_lanes

                def cols(pair, k):
                    return bass.ds((NCH * pair + k) * CPX, CPX)

                def load_x1(pair, Ci, k, n):
                    sp.wait_ge(xl_done, Ci - 2)
                    sp.dma_start(x1[n][:], x1_lanes[:, cols(pair, k)]).then_inc(x1_in[n], 16)

                def load_base(pair, Ci, k, n):
                    sp.wait_ge(out_done, Ci - 2)
                    sp.dma_start(base[n][:], before[:, cols(pair, k)]).then_inc(base_in[n], 16)

                def store(pair, Ci, k, n):
                    sp.wait_ge(out_done, Ci + 1)
                    sp.dma_start(out_lanes[:, cols(pair, k)], outb[n][:]).then_inc(out_stored[n], 16)

                with sp.Fori(0, HB // 2) as o:
                    for pp in range(2):
                        pair = 2 * o + pp
                        Pi = pair + HB * q
                        C0 = chunk0(Pi)
                        sp.wait_ge(z_done, C0)
                        sp.dma_start(pk_r[1 - pp][:].bitcast(F32), packs_r[Pi + 1]).then_inc(pack_in[1 - pp], 16)
                        sp.dma_start(pk_f[1 - pp][:], packs_f[Pi + 1]).then_inc(pack_in[1 - pp], 16)
                        for k in range(3):
                            load_base(pair, C0 + k, k, k)
                        with sp.Fori(0, 3) as m:
                            for e in range(3):
                                k = 3 * m + e
                                load_x1(pair, C0 + k + 5, k + 5, (e + 2) % 3)
                                store(pair, C0 + k, k, e)
                                load_base(pair, C0 + k + 3, k + 3, e)
                        for k in range(9, NCH):
                            load_x1(pair, C0 + k + 5, k + 5, (k + 5) % 3)
                            store(pair, C0 + k, k, k % 3)
                for n in range(3):
                    sp.wait_ge(out_stored[n], nth(HB * (q + 1), 0))
                    sp.wait_ge(x1_in[n], nth(HB * (q + 1), 1 if n < 2 else 0))

            one_pass(0)
            with sp.If(npass > 1):
                one_pass(1)
            sp.wait_ge(pack_in[0], 32)
            sp.wait_ge(pack_in[1], 32)

        @block.tensor
        def _(pe):
            pe.sem_inc(pw1_done, 4 * AHEAD)
            pe.sem_inc(taps_done, 3 * AHEAD)
            pe.sem_inc(pw2_done, 3 * AHEAD)
            pe.wait_ge(wm_split, 2)
            pe.wait_ge(borders, 2)

            def pw1(Ci, n, pp, u):
                if u == 0:
                    pe.wait_ge(xl_done, Ci + 1)
                    pe.wait_ge(relu1_done, 3 * Ci)
                elif u == 1:
                    pe.wait_ge(mask_done, Ci)
                else:
                    pe.wait_ge(relu1_done, 3 * Ci + u - 1)
                if u < UNITS:
                    hi, lo = pk_r[pp][:, u * P:(u + 1) * P], pk_r[pp][:, (UNITS + u) * P:(UNITS + u + 1) * P]
                else:
                    hi, lo = wm[0][:], wm[1][:]
                for m in range(2):
                    for i, (w, v) in enumerate(((hi, xh[n]), (hi, xl[n]), (lo, xh[n]))):
                        mm = nc.tensor.matmul(ps1[u % 2][:, m, 0:NH], w, v[:, m * NH:(m + 1) * NH],
                                              start=(i == 0), stop=(i == 2))
                mm.then_inc(pw1_done, 1)

            def taps(Ci, slot, pp, j):
                if j == 0:
                    pe.wait_ge(above_done, Ci + 1)
                pe.wait_ge(psd_read, 3 * Ci + j)
                for m in range(2):
                    for i, tap in enumerate(PE_TAPS):
                        at = PK_DIAG + (j * len(PE_TAPS) + i) * P
                        mm = nc.tensor.matmul(psd[:, m, 0:NH], pk_f[pp][:, at:at + P], window(j, slot, tap)[:, m],
                                              start=(i == 0), stop=(i == len(PE_TAPS) - 1))
                mm.then_inc(taps_done, 1)

            def pw2(Ci, pp, j):
                pe.wait_ge(relu2_done, 3 * Ci + j + 1)
                if j == 0:
                    pe.wait_ge(z_done, Ci)
                for m in range(2):
                    mm = nc.tensor.matmul(ps2[:, m, 0:NH], pk_f[pp][:, j * P:(j + 1) * P], h2[j][:, m * NH:(m + 1) * NH],
                                          start=(j == 0), stop=(j == UNITS - 1), skip_group_check=True)
                mm.then_inc(pw2_done, 1)

            def step(Pi, k, pack, slot, third):
                Ci, nxt = chunk0(Pi) + k, (slot + 2) % 3
                before, now, then, ahead = (pack(k + n) for n in (-1, 0, 1, 2))
                inside = not (isinstance(k, int) and k == 0)
                if isinstance(k, int) and k == NCH - 2:
                    pe.wait_ge(pack_in[ahead], pack_count(Pi + 1, ahead))
                pw1(Ci + 2, nxt, ahead, 0)
                taps(Ci, slot, now, 1)
                if inside:
                    pw2(Ci - 1, before, 1)
                pw1(Ci + 2, nxt, ahead, 1)
                taps(Ci, slot, now, 2)
                if inside:
                    pw2(Ci - 1, before, 2)
                pw1(Ci + 2, nxt, ahead, 2)
                pw1(Ci + 2, nxt, ahead, UNITS)
                taps(Ci + 1, (slot + 1) % 3, then, 0)
                pw2(Ci, now, 0)

            pe.wait_ge(pack_in[0], 32)
            for k in range(2):
                for u in range(UNITS + 1):
                    pw1(AHEAD + k, k, 0, u)
            taps(AHEAD, 0, 0, 0)
            run(pe, step)

        @block.scalar
        def _(act):
            act.sem_inc(xh_done, AHEAD)
            act.sem_inc(relu1_done, 3 * AHEAD)
            act.sem_inc(prod_done, 6 * AHEAD)
            act.sem_inc(relu2_done, 3 * AHEAD)
            act.sem_inc(z_done, AHEAD)
            act.wait_ge(borders, 2)

            def high(Ci, n, loads):
                act.wait_ge(x1_in[n], loads)
                act.wait_ge(pw1_done, 4 * Ci - 8)
                nc.scalar.activation(xh[n][:], x1[n][:], ACT.Copy).then_inc(xh_done, 1)

            def relu1(Ci, n, pp, j):
                act.wait_ge(pw1_done, 4 * Ci + j + 1)
                act.wait_ge(taps_done, 3 * Ci + j - 8)
                act.wait_ge(acc_done, 3 * Ci + j - 8)
                act.wait_ge(prod_done, 6 * Ci + 2 * j - 16)
                nc.scalar.activation(h1[:, j, n, 1:1 + CH, 1:1 + W].rearrange("p (m r) w -> p m r w", m=2),
                                     banks(ps1[j % 2]), ACT.Relu, bias=par(pp, j, T1),
                                     scale=par(pp, j, S1)).then_inc(relu1_done, 1)

            def prods(Ci, slot, pp, j):
                if j == 0:
                    act.wait_ge(above_done, Ci + 1)
                act.wait_ge(full_done, 3 * Ci + j - 2)
                for i, tap in enumerate(ACT_TAPS):
                    nc.scalar.activation(rows(prod[j][i][:]), window(j, slot, tap), ACT.Copy,
                                         scale=par(pp, j, TAP + tap)).then_inc(prod_done, 1)

            def relu2(Ui, pp, j):
                act.wait_ge(full_done, Ui + 1)
                act.wait_ge(pw2_done, Ui - 2)
                nc.scalar.activation(h2[j][:], full[j][:], ACT.Relu, bias=par(pp, j, TD),
                                     scale=par(pp, j, SD)).then_inc(relu2_done, 1)

            def norm2(Ci, pp):
                act.wait_ge(pw2_done, 3 * Ci + 3)
                act.wait_ge(zm_done, Ci)
                nc.scalar.activation(rows(z[:]), banks(ps2), ACT.Identity, bias=pk_f[pp][:, PK_S2 + 1:PK_S2 + 2],
                                     scale=pk_f[pp][:, PK_S2:PK_S2 + 1]).then_inc(z_done, 1)

            def step(Pi, k, pack, slot, third):
                Ci, nxt = chunk0(Pi) + k, (slot + 2) % 3
                before, now, then, ahead = (pack(k + n) for n in (-1, 0, 1, 2))
                inside = not (isinstance(k, int) and k == 0)
                if isinstance(k, int) and k == NCH - 2:
                    act.wait_ge(pack_in[ahead], pack_count(Pi + 1, ahead))
                if inside:
                    relu2(3 * Ci - 2, before, 1)
                prods(Ci, slot, now, 1)
                relu1(Ci + 2, nxt, ahead, 0)
                high(Ci + 3, slot, nth(Pi, third + 1))
                if inside:
                    relu2(3 * Ci - 1, before, 2)
                relu1(Ci + 2, nxt, ahead, 1)
                prods(Ci, slot, now, 2)
                if inside:
                    norm2(Ci - 1, before)
                relu2(3 * Ci, now, 0)
                relu1(Ci + 2, nxt, ahead, 2)
                prods(Ci + 1, (slot + 1) % 3, then, 0)

            act.wait_ge(pack_in[0], 32)
            for k in range(3):
                high(AHEAD + k, k, 16)
            for k in range(2):
                for j in range(UNITS):
                    relu1(AHEAD + k, k, 0, j)
            prods(AHEAD, 0, 0, 0)
            run(act, step)

        @block.vector
        def _(dve):
            dve.sem_inc(mask_done, AHEAD)
            dve.sem_inc(psd_read, 3 * AHEAD)
            dve.sem_inc(chain, 3 * AHEAD * (NT - 2))
            dve.sem_inc(acc_done, 3 * AHEAD)
            dve.sem_inc(zm_done, AHEAD)
            dve.wait_ge(mask_loaded, 32)
            nc.vector.tensor_copy(wm[0][:], wm_raw[:]).then_inc(wm_split, 1)
            dve.wait_ge(wm_split, 1)
            nc.vector.tensor_tensor(wm[1][:], wm_raw[:], wm[0][:], ALU.subtract).then_inc(wm_split, 1)

            def make_mask(Ci, n):
                dve.wait_ge(pw1_done, 4 * Ci + 4)
                dve.wait_ge(zm_done, Ci - 2)
                nc.vector.tensor_scalar(rows(mask[n][:]), banks(ps1[1]), bm[:, 0:1], 0.0, ALU.add,
                                        ALU.is_ge).then_inc(mask_done, 1)

            def add_tap(Ci, slot, pp, j, i):
                Ui = 3 * Ci + j
                if i == 2 and j == 0:
                    dve.wait_ge(below_done, Ci + 1)
                if i == 0:
                    dve.wait_ge(taps_done, Ui + 1)
                    dve.wait_ge(full_done, Ui - 2)
                elif i == 1:
                    dve.wait_ge(psd_read, Ui + 1)
                else:
                    dve.wait_ge(chain, (NT - 2) * Ui + i - 1)
                ins = nc.vector.scalar_tensor_tensor(rows(acc[j][:]), window(j, slot, DVE_TAPS[i]),
                                                     par(pp, j, TAP + DVE_TAPS[i]),
                                                     banks(psd) if i == 0 else rows(acc[j][:]), ALU.mult, ALU.add)
                ins.then_inc(psd_read if i == 0 else acc_done if i == NT - 1 else chain, 1)

            def masked(Ci, n):
                dve.wait_ge(z_done, Ci + 1)
                dve.wait_ge(out_done, Ci)
                nc.vector.tensor_tensor(zm[:], z[:], mask[n][:], ALU.mult).then_inc(zm_done, 1)

            def step(Pi, k, pack, slot, third):
                Ci, nxt = chunk0(Pi) + k, (slot + 2) % 3
                before, now = pack(k - 1), pack(k)
                inside = not (isinstance(k, int) and k == 0)
                for j in range(UNITS):
                    for i in range(NT - 2):
                        add_tap(Ci, slot, now, j, i)
                        if i < 2 and j > 0:
                            add_tap(Ci, slot, now, j - 1, NT - 2 + i)
                        elif i < 2 and inside:
                            add_tap(Ci - 1, nxt, before, UNITS - 1, NT - 2 + i)
                if inside:
                    masked(Ci - 1, nxt)
                make_mask(Ci + 2, nxt)

            dve.wait_ge(pack_in[0], 32)
            make_mask(AHEAD, 0)
            make_mask(AHEAD + 1, 1)
            run(dve, step)

        @block.gpsimd
        def _(pool):
            pool.sem_inc(xl_done, AHEAD)
            pool.sem_inc(pair_sum, 3 * AHEAD)
            pool.sem_inc(full_done, 3 * AHEAD)
            pool.sem_inc(out_done, AHEAD)
            pool.sem_inc(above_done, AHEAD)
            pool.sem_inc(below_done, AHEAD)
            nc.gpsimd.memset(zeros[:], 0.0).then_inc(borders, 1)
            nc.gpsimd.memset(h1[:], 0.0).then_inc(borders, 1)
            pool.wait_ge(borders, 2)

            def low(Ci, n):
                pool.wait_ge(xh_done, Ci + 1)
                nc.gpsimd.tensor_tensor(xl[n][:], x1[n][:], xh[n][:], ALU.subtract).then_inc(xl_done, 1)

            def halo(Ci, n):
                prev = (n + 2) % 3
                pool.wait_ge(relu1_done, 3 * Ci + 3)
                last, first = h1[:, :, prev, CH, 1:1 + W], h1[:, :, n, 1, 1:1 + W]
                nc.gpsimd.tensor_tensor(h1[:, :, prev, CH + 1, 1:1 + W], first, zeros[:, :, 0:W], ALU.add).then_inc(below_done, 1)
                nc.gpsimd.tensor_tensor(h1[:, :, n, 0, 1:1 + W], last, zeros[:, :, 0:W], ALU.add).then_inc(above_done, 1)

            def edge(Ci, n):
                prev = (n + 2) % 3
                pool.wait_ge(relu1_done, 3 * Ci + 3)
                nc.gpsimd.tensor_tensor(h1[:, :, prev, CH + 1, :], zeros[:], zeros[:], ALU.add).then_inc(below_done, 1)
                nc.gpsimd.tensor_tensor(h1[:, :, n, 0, :], zeros[:], zeros[:], ALU.add).then_inc(above_done, 1)

            def add_pair(Ui, j):
                pool.wait_ge(prod_done, 2 * Ui + 2)
                nc.gpsimd.tensor_tensor(prod[j][0][:], prod[j][0][:], prod[j][1][:], ALU.add).then_inc(pair_sum, 1)

            def gather(Ui, j):
                pool.wait_ge(pair_sum, Ui + 1)
                pool.wait_ge(acc_done, Ui + 1)
                pool.wait_ge(relu2_done, Ui - 2)
                nc.gpsimd.tensor_tensor(full[j][:], acc[j][:], prod[j][0][:], ALU.add).then_inc(full_done, 1)

            def add_base(Ci, n, loads):
                pool.wait_ge(zm_done, Ci + 1)
                pool.wait_ge(base_in[n], loads)
                pool.wait_ge(out_stored[n], loads)
                nc.gpsimd.tensor_tensor(outb[n][:], zm[:], base[n][:], ALU.add).then_inc(out_done, 1)

            def step(Pi, k, pack, slot, third):
                Ci, nxt = chunk0(Pi) + k, (slot + 2) % 3
                inside = not (isinstance(k, int) and k == 0)
                add_pair(3 * Ci, 0)
                if inside:
                    gather(3 * Ci - 1, 2)
                add_pair(3 * Ci + 1, 1)
                low(Ci + 3, slot)
                gather(3 * Ci, 0)
                add_pair(3 * Ci + 2, 2)
                if isinstance(k, int) and k == NCH - 2:
                    edge(Ci + 2, nxt)
                else:
                    halo(Ci + 2, nxt)
                gather(3 * Ci + 1, 1)
                if inside:
                    add_base(Ci - 1, nxt, nth(Pi, third if slot else third - 1))

            for k in range(3):
                low(AHEAD + k, k)
            pool.sem_inc(above_done, 1)
            halo(AHEAD + 1, 1)
            run(pool, step)


def build(nc, x_steps, x_lanes, w_gates, w_kinds, w_proj, norms, consts, w_sal, b_sal, hid, w_pw1, w_mask, b_mask, out):
    h_rows = nc.dram_tensor("h_rows", [H, 2, HC, B, W], F32).ap()
    x1_lanes = nc.dram_tensor("x1_lanes", [P, HB * PX + AGAIN * CPX], F32).ap()
    packs_r = nc.dram_tensor("packs_r", [2 * HB + 1, P, PKR], F32).ap()
    packs_f = nc.dram_tensor("packs_f", [2 * HB + 1, P, PKF], F32).ap()
    recurrence(nc, x_steps, w_gates, w_kinds, h_rows)
    with ExitStack() as ctx:
        def sb(name, shape, dt=F32):
            return ctx.enter_context(nc.sbuf_tensor(name, shape, dt))

        sums = sb("sums", [P, HB])
        folded = sb("folded", [P, 2, 8])
        passes = sb("passes", [1, 1], I32)
        with ExitStack() as own:
            y = own.enter_context(nc.sbuf_tensor("y", [P, HB, H, W], F32))
            stats = own.enter_context(nc.sbuf_tensor("stats", [P, 6 * H], F32))
            projection(nc, h_rows, w_proj, y, stats)
            residual(nc, y, stats, consts, norms, x_lanes, x1_lanes, sums, folded)
        selection(nc, consts, w_sal, b_sal, hid, w_pw1, sums, folded, packs_r, packs_f, passes)
        bottleneck(nc, w_mask, b_mask, x1_lanes, out, packs_r, packs_f, passes)


def kernel(x, L0_conv_w_f, L0_conv_b_f, L0_conv_w_b, L0_conv_b_b, L0_conv_w_proj, L0_conv_gamma, L0_conv_beta,
           L1_conv_w_pw1, L1_conv_bn1_g, L1_conv_bn1_b, L1_conv_bn1_m, L1_conv_bn1_v, L1_conv_w_dw,
           L1_conv_bnd_g, L1_conv_bnd_b, L1_conv_bnd_m, L1_conv_bnd_v, L1_conv_w_pw2,
           L1_conv_bn2_g, L1_conv_bn2_b, L1_conv_bn2_m, L1_conv_bn2_v, L1_conv_w_mask, L1_conv_b_mask,
           L1_conv_w_sal, L1_conv_b_sal):
    import concourse.bacc as bacc
    from concourse.bass_utils import run_bass_kernel_spmd

    def arr(a):
        return np.ascontiguousarray(a)

    def halves(a):
        out = np.zeros((P,) + a.shape[1:], np.float32)
        out[LO:LO + C] = a
        out[HI:HI + C] = a
        return out

    w_gates = np.zeros((P, 7, 2, 2, P), np.float32)
    for d, (w, b) in enumerate(((L0_conv_w_f, L0_conv_b_f), (L0_conv_w_b, L0_conv_b_b))):
        w, b = arr(w)[:, :, 1], arr(b)
        for m in range(2):
            for col, gate in ((0, 2 * m), (64, 2 * m + 1)):
                g = slice(HC * gate, HC * gate + HC)
                cols = slice(col, col + HC)
                for tap in range(3):
                    wx, wh = w[g, :C, tap].T, w[g, C:, tap].T
                    w_gates[tap:96:3, 0, d, m, cols] = wx[0:32]
                    w_gates[0:HC, 1 + tap, d, m, cols] = wh
                    w_gates[48:112, 1 + tap, d, m, cols] = np.repeat(wx[0:32], 2, axis=0)
                    w_gates[112:128, 1 + tap, d, m, cols] = wx[32:48]
                    w_gates[0:HC, 4 + tap, d, m, cols] = wh
                    w_gates[HI:HI + HC, 4 + tap, d, m, cols] = wh
                    w_gates[48:64, 4 + tap, d, m, cols] = np.repeat(wx[32:40], 2, axis=0)
                    w_gates[112:128, 4 + tap, d, m, cols] = np.repeat(wx[40:48], 2, axis=0)
                w_gates[96:98, 0, d, m, cols] = b[g]
    w_gates = w_gates.reshape(P, 7, 4, P)
    w_kinds = np.zeros((P, 2, 2), np.float32)
    w_kinds[0:96, 0, 0] = 1.0
    w_kinds[97, 0, 0] = 1.0
    w_kinds[0:HC, 0, 1] = 1.0
    w_kinds[112:128, 0, 1] = 1.0
    w_kinds[:, 1] = 1.0 - 2.0 * w_kinds[:, 0]
    w_proj = np.zeros((P, 64), np.float32)
    w_proj[0:HC, 0:C] = arr(L0_conv_w_proj)[:, :HC].T
    w_proj[HI:HI + HC, 0:C] = arr(L0_conv_w_proj)[:, HC:].T

    norms = np.zeros((P, 4, 8), np.float32)
    for kind, (one, mid, two) in enumerate(((L1_conv_bn1_v, L1_conv_bnd_v, L1_conv_bn2_v),
                                            (L1_conv_bn1_g, L1_conv_bnd_g, L1_conv_bn2_g),
                                            (L1_conv_bn1_b, L1_conv_bnd_b, L1_conv_bn2_b),
                                            (L1_conv_bn1_m, L1_conv_bnd_m, L1_conv_bn2_m))):
        norms[0:HG, kind, 0:NG] = arr(one).reshape(NG, HG).T
        norms[0:HG, kind, NG:2 * NG] = arr(mid).reshape(NG, HG).T
        norms[:, kind, 6] = halves(arr(two))
    norms[:, 1, 7] = halves(arr(L0_conv_gamma))
    norms[:, 2, 7] = halves(arr(L0_conv_beta))

    units = 2 * UNITS
    consts = np.zeros((P, 3 * P + HG + units * UC), np.float32)
    for half in range(2):
        for other in range(2):
            consts[64 * half + np.arange(C), 64 * other + np.arange(C)] = 0.5
    consts[np.arange(P), P + np.arange(P)] = 1.0
    consts[:, 2 * P:3 * P] = 1.0
    consts[0:HG, 3 * P:3 * P + HG] = np.triu(np.ones((HG, HG), np.float32), 1)
    place = np.full((units, UC), -2.0, np.float32)
    place[:, :C] = np.arange(units * C).reshape(units, C)
    consts[:, 3 * P + HG:] = place.reshape(-1)

    w_sal = np.zeros((P, 2, NG, HG), np.float32)
    sal_t = arr(L1_conv_w_sal).T.reshape(C, NG, HG)
    w_sal[LO:LO + C, 0] = sal_t
    w_sal[HI:HI + C, 1] = sal_t
    b_sal = arr(arr(L1_conv_b_sal).reshape(NG, HG).T)
    hid = np.zeros((HG, NG, NPAR), np.float32)
    hid[:, :, TAP:TAP + 9] = arr(L1_conv_w_dw).reshape(NG, HG, 9).transpose(1, 0, 2)
    hid[:, :, W2:W2 + C] = arr(L1_conv_w_pw2).T.reshape(NG, HG, C).transpose(1, 0, 2)
    w_pw1 = np.zeros((HG, NG, 64), np.float32)
    w_pw1[:, :, :C] = arr(L1_conv_w_pw1).reshape(NG, HG, C).transpose(1, 0, 2)
    w_mask = np.zeros((P, P), np.float32)
    w_mask[LO:LO + C, LO:LO + C] = arr(L1_conv_w_mask).reshape(C, 1)
    w_mask[HI:HI + C, HI:HI + C] = arr(L1_conv_w_mask).reshape(C, 1)
    b_mask = np.zeros((P, 1), np.float32)
    b_mask[:] = arr(L1_conv_b_mask)

    x = arr(x)
    x_steps = np.zeros((H, HI + C, B, W), np.float32)
    x_steps[:, LO:LO + C] = x.transpose(2, 1, 0, 3)
    x_steps[:, HI:HI + C] = x.transpose(2, 1, 0, 3)[::-1]
    ins = {
        "x_steps": x_steps,
        "x_lanes": arr(x.reshape(2, HB, C, PX).transpose(0, 2, 1, 3).reshape(2, C, HB * PX)),
        "w_gates": w_gates, "w_kinds": w_kinds, "w_proj": w_proj, "norms": norms, "consts": consts, "w_sal": w_sal, "b_sal": b_sal,
        "hid": hid, "w_pw1": w_pw1, "w_mask": w_mask, "b_mask": b_mask,
    }
    nc = bacc.Bacc("TRN2", target_bir_lowering=False, num_devices=1)
    args = [nc.dram_tensor(name, a.shape, mybir.dt.from_np(a.dtype), kind="ExternalInput").ap() for name, a in ins.items()]
    args.append(nc.dram_tensor("out", (P, HB * PX), F32, kind="ExternalOutput").ap())
    build(nc, *args)
    r = run_bass_kernel_spmd(nc, [ins], core_ids=[0])
    got = r.results[0]["out"].reshape(2, 64, HB, H, W)[:, :C]
    return np.ascontiguousarray(got.transpose(0, 2, 1, 3, 4).reshape(B, C, H, W))
```

```python
from contextlib import ExitStack

import numpy as np

import concourse.bass as bass
from concourse import mybir

F32 = mybir.dt.float32
F32R = mybir.dt.float32r
I32 = mybir.dt.int32
ACT = mybir.ActivationFunctionType
ALU = mybir.AluOpType
AX = mybir.AxisListType

B, C, H, W = 8, 48, 96, 96
HB = B // 2
HC = 48
HID = 288
P = 128
LO, HI = 0, 64
PX = H * W
NH = HB * W
WP = W + 2
HG = 96
NG = HID // HG
TOPK = 144
EPS = 1e-5
S1, T1, TAP, SD, TD, W2, NPAR = 0, 1, 2, 11, 12, 13, 64
UNITS = 3
UC = 64
PE_TAPS = [0, 1]
ACT_TAPS = [2, 3]
DVE_TAPS = [4, 5, 6, 7, 8]
CH = 8
CPX = CH * W
NCH = H // CH
AGAIN = 6
X1_PART = 16 * W
CONSTS = 3 * P + HG + 2 * UNITS * UC
PKR = 2 * UNITS * P
PKF = UNITS * P + UNITS * len(PE_TAPS) * P + UNITS * 13 + 2
PK_DIAG = UNITS * P
PK_PAR = PK_DIAG + UNITS * len(PE_TAPS) * P
PK_S2 = PK_PAR + UNITS * 13


KINDS = ((0, 1), (1, 4), (4, 7))


def at_least(eng, sem, value):
    if not isinstance(value, int) or value > 0:
        eng.wait_ge(sem, value)


def recurrence(nc, x_steps, w_gates, w_kinds, h_rows):
    STEPS = H
    PASSES = 7
    FULL = B * WP
    AHEAD_X = 2
    with ExitStack() as ctx:
        def sb(name, shape, dt=F32):
            return ctx.enter_context(nc.sbuf_tensor(name, shape, dt))

        def sem(name):
            return ctx.enter_context(nc.semaphore(name))

        kinds = sb("kinds", [P, 2, 2])
        w_raw = sb("w_raw", [P, PASSES, 4, P])
        w_high = sb("w_high", [P, PASSES, 4, P], F32R)
        w_part = sb("w_part", [P, 4, 4, P])
        w_low = sb("w_low", [P, 4, 4, P], F32R)
        spread = [[sb(f"spread{d}{e}", [P, B, WP], F32R) for e in range(2)] for d in range(2)]
        single = [[sb(f"single{d}{e}", [P, B, WP], F32R) for e in range(2)] for d in range(2)]
        double = [[sb(f"double{d}{e}", [P, B, WP], F32R) for e in range(2)] for d in range(2)]
        x_raw = sb("x_raw", [P, 2, B, W])
        x_parts = [sb(f"x_parts{e}", [P, 2, B, WP], F32R) for e in range(2)]
        sig_i, sig_f, tanh_g, sig_o, i_g, f_c, cell, tanh_c = (
            [sb(f"{n}{p}", [P, HB, W]) for p in range(2)]
            for n in ("sig_i", "sig_f", "tanh_g", "sig_o", "i_g", "f_c", "cell", "tanh_c"))
        h_new = [sb(f"h_new{e}", [P, B, W]) for e in range(2)]
        gates = [ctx.enter_context(nc.psum_tensor(f"gates{k}", [P, 2, 512], F32)) for k in range(4)]

        w_loaded = [sem(f"w_loaded{n}") for n in range(3)]
        kinds_loaded, w_high_ready, w_part_ready, w_ready = (
            sem(n) for n in ("kinds_loaded", "w_high_ready", "w_part_ready", "w_ready"))
        raw_in = [sem(f"raw_in{e}") for e in range(2)]
        x_in = [[sem(f"x_in{d}{e}") for e in range(2)] for d in range(2)]
        h_stored = [sem(f"h_stored{e}") for e in range(2)]
        parts_clear, zeroed, odd_zeroed, gates_zero = (
            sem(n) for n in ("parts_clear", "zeroed", "odd_zeroed", "gates_zero"))
        x_high, x_low = sem("x_high"), sem("x_low")
        if_summed, go_summed, if_ready, tg_ready, so_ready = (
            sem(n) for n in ("if_summed", "go_summed", "if_ready", "tg_ready", "so_ready"))
        single_ready, double_ready, lo_ready = (sem(n) for n in ("single_ready", "double_ready", "lo_ready"))
        fc_ready, ig_ready, cell_ready, tc_ready, h_ready = (
            sem(n) for n in ("fc_ready", "ig_ready", "cell_ready", "tc_ready", "h_ready"))

        def halves(p):
            return slice(HB * p, HB * p + HB)

        def lanes(d):
            return slice(HI * d, HI * d + HC)

        BOTH = slice(0, HI + HC)
        block = ctx.enter_context(nc.Block())

        def turns(eng, body):
            body(0, True, False)
            with eng.Fori(1, STEPS // 2 - 1) as i:
                body(i, False, False)
            body(STEPS // 2 - 1, False, True)

        @block.sync
        def _(sp):
            def load_raw(t, e):
                sp.dma_start(x_raw[BOTH, e], x_steps[t]).then_inc(raw_in[e], 16)

            def load_x(t, e):
                sp.wait_ge(x_low, t + 1)
                for d in range(2):
                    at_least(sp, go_summed, 4 * t - 5 + d)

                    def flat(a):
                        return a.bitcast(F32).rearrange("p b w -> p (b w)")

                    def parts(c0, c1):
                        return x_parts[e][HI * d + c0:HI * d + c1].bitcast(F32).rearrange("p s b w -> p s (b w)")

                    high = parts(0, 32)
                    taps = bass.AP(tensor=high.tensor, offset=high.offset, ap=[[2 * FULL, 32], [1, 3], [1, FULL - 2]])
                    for to, src in ((flat(spread[d][e][0:96])[:, 0:FULL - 2], taps),
                                    (flat(single[d][e][48:112]), high),
                                    (flat(single[d][e][112:128]), parts(32, 48)[:, 0]),
                                    (flat(double[d][e][48:64]), parts(32, 40)),
                                    (flat(double[d][e][112:128]), parts(40, 48))):
                        sp.dma_start(to, src).then_inc(x_in[d][e], 16)

            def store_h(i, e):
                sp.wait_ge(h_ready, 4 * i + 2 * e + 2)
                for d in range(2):
                    two = i if d == 0 else i * -1 + (H // 2 - 1)
                    sp.dma_start(h_rows[two, d, :, e if d == 0 else 1 - e], h_new[e][lanes(d)]).then_inc(h_stored[e], 16)

            load_raw(0, 0)
            for n, (a, b) in enumerate(KINDS):
                sp.dma_start(w_raw[:, a:b], w_gates[:, a:b]).then_inc(w_loaded[n], 16)
                if n == 0:
                    sp.dma_start(kinds[:], w_kinds).then_inc(kinds_loaded, 16)
            load_raw(1, 1)
            sp.wait_ge(zeroed, 8)
            load_x(0, 0)
            sp.wait_ge(odd_zeroed, 4)

            def body(i, first, last):
                for e in range(2):
                    t = 2 * i + e
                    if not last:
                        load_raw(t + AHEAD_X, e)
                    if not (last and e == 1):
                        load_x(t + 1, 1 - e)
                    if e == 1:
                        store_h(i, 0)
                    elif not first:
                        store_h(i - 1, 1)

            turns(sp, body)
            store_h(STEPS // 2 - 1, 1)
            for e in range(2):
                sp.wait_ge(h_stored[e], 32 * STEPS // 2)

        @block.tensor
        def _(pe):
            pe.wait_ge(zeroed, 8)

            def body(i, first, last):
                for k in range(8):
                    e, p, d = k // 4, k % 4 // 2, k % 2
                    t, s = 2 * i + e, 8 * i + k
                    if p == 0:
                        pe.wait_ge(x_in[d][e], 80 * (i + 1))
                    at_least(pe, so_ready, s - 3)
                    for m in range(2):
                        for n in range(PASSES):
                            if first and k == 0 and m == 0 and n in (0, 1):
                                pe.wait_ge(w_ready, n + 1)
                            if first and k == 0 and m == 0 and n == 4:
                                pe.wait_ge(w_high_ready, 3)
                            if m == 0 and n == 1:
                                at_least(pe, single_ready, s - 3)
                            if m == 0 and n == 4:
                                at_least(pe, double_ready, s - 3)
                                at_least(pe, lo_ready, s - 3)
                            moving, tap = ((spread, 0) if n == 0 else (single, n - 1) if n < 4 else (double, n - 4))
                            mm = nc.tensor.matmul(gates[k % 4][:, m, 0:NH], (w_high if n >= 4 else w_low)[:, n, 2 * d + m, :],
                                                  moving[d][e][:, halves(p), tap:tap + W],
                                                  start=(n == 0), stop=(n == PASSES - 1))
                        mm.then_inc(go_summed if m else if_summed, 1)

            turns(pe, body)

        @block.scalar
        def _(act):
            for n, (a, b) in enumerate(KINDS):
                act.wait_ge(w_loaded[n], 16)
                nc.scalar.activation(w_high[:, a:b], w_raw[:, a:b], ACT.Copy).then_inc(w_high_ready, 1)
            act.wait_ge(gates_zero, 10)

            def body(i, first, last):
                for k in range(8):
                    p, d = k % 4 // 2, k % 2
                    s = 8 * i + k
                    g = gates[k % 4]
                    act.wait_ge(if_summed, s + 1)
                    nc.scalar.activation(sig_i[p][lanes(d)], g[0:HC, 0, 0:NH], ACT.Sigmoid)
                    nc.scalar.activation(sig_f[p][lanes(d)], g[HI:HI + HC, 0, 0:NH], ACT.Sigmoid).then_inc(if_ready, 1)
                    act.wait_ge(go_summed, s + 1)
                    nc.scalar.activation(tanh_g[p][lanes(d)], g[0:HC, 1, 0:NH], ACT.Tanh).then_inc(tg_ready, 1)
                    nc.scalar.activation(sig_o[p][lanes(d)], g[HI:HI + HC, 1, 0:NH], ACT.Sigmoid).then_inc(so_ready, 1)
                    if d == 1:
                        q = 4 * i + k // 2
                        act.wait_ge(cell_ready, q + 1)
                        nc.scalar.activation(tanh_c[p][BOTH], cell[p][BOTH], ACT.Tanh).then_inc(tc_ready, 1)

            turns(act, body)

        @block.vector
        def _(dve):
            for e in range(2):
                nc.vector.memset(x_parts[e][:, :, :, 0:1].bitcast(F32), 0.0).then_inc(parts_clear, 1)
                nc.vector.memset(x_parts[e][:, :, :, 1 + W:WP].bitcast(F32), 0.0).then_inc(parts_clear, 1)
            for d in range(2):
                nc.vector.memset(single[d][0][:].bitcast(F32), 0.0).then_inc(zeroed, 1)
                nc.vector.memset(double[d][0][:].bitcast(F32), 0.0).then_inc(zeroed, 1)
            dve.wait_ge(parts_clear, 4)

            def high_x(e, loaded, moved):
                dve.wait_ge(raw_in[e], loaded)
                for d in range(2):
                    at_least(dve, x_in[d][e], moved)
                nc.vector.tensor_copy(x_parts[e][BOTH, 0, :, 1:1 + W], x_raw[BOTH, e]).then_inc(x_high, 1)

            def low_first_x(e):
                dve.wait_ge(x_high, e + 1)
                nc.vector.tensor_tensor(x_parts[e][BOTH, 1, :, 1:1 + W], x_raw[BOTH, e],
                                        x_parts[e][BOTH, 0, :, 1:1 + W], ALU.subtract).then_inc(x_low, 1)

            high_x(0, 16, 0)
            low_first_x(0)
            dve.wait_ge(kinds_loaded, 16)
            for n, (a, b) in enumerate(KINDS[:2]):
                dve.wait_ge(w_high_ready, n + 1)
                nc.vector.tensor_scalar(w_part[:, a:b], w_high[:, a:b].bitcast(F32), kinds[:, 1, n:n + 1], None,
                                        ALU.mult).then_inc(w_part_ready, 1)
                dve.wait_ge(w_part_ready, n + 1)
                nc.vector.scalar_tensor_tensor(w_low[:, a:b], w_raw[:, a:b], kinds[:, 0, n:n + 1], w_part[:, a:b],
                                               ALU.mult, ALU.add).then_inc(w_ready, 1)
            dve.wait_ge(gates_zero, 10)

            def body(i, first, last):
                for k in range(0, 8, 2):
                    e, p = k // 4, k % 4 // 2
                    t, s, q = 2 * i + e, 8 * i + k, 4 * i + k // 2
                    if p == 0 and not last:
                        high_x(e, 16 * (i + 2), 80 * (i + 1))
                    dve.wait_ge(if_ready, s + 2)
                    at_least(dve, cell_ready, q - 1)
                    nc.vector.tensor_tensor(f_c[p][BOTH], sig_f[p][BOTH], cell[p][BOTH], ALU.mult).then_inc(fc_ready, 1)
                    dve.wait_ge(tg_ready, s + 2)
                    nc.vector.tensor_tensor(i_g[p][BOTH], sig_i[p][BOTH], tanh_g[p][BOTH], ALU.mult).then_inc(ig_ready, 1)
                    dve.wait_ge(fc_ready, q + 1)
                    dve.wait_ge(ig_ready, q + 1)
                    nc.vector.tensor_tensor(cell[p][BOTH], f_c[p][BOTH], i_g[p][BOTH], ALU.add).then_inc(cell_ready, 1)
                    dve.wait_ge(tc_ready, q + 1)
                    dve.wait_ge(so_ready, s + 2)
                    at_least(dve, h_stored[e], 32 * i)
                    at_least(dve, lo_ready, s - 6)
                    nc.vector.tensor_tensor(h_new[e][BOTH, halves(p)], sig_o[p][BOTH], tanh_c[p][BOTH], ALU.mult).then_inc(h_ready, 1)
                    dve.wait_ge(h_ready, q + 1)
                    for d in range(2):
                        nc.vector.tensor_copy(single[d][1 - e][0:HC, halves(p), 1:1 + W],
                                              h_new[e][lanes(d), halves(p)]).then_inc(single_ready, 1)
                        nc.vector.tensor_copy(double[d][1 - e][lanes(d), halves(p), 1:1 + W],
                                              h_new[e][lanes(d), halves(p)]).then_inc(double_ready, 1)

            high_x(1, 16, 0)
            low_first_x(1)
            dve.wait_ge(odd_zeroed, 4)
            turns(dve, body)

        @block.gpsimd
        def _(pool):
            for d in range(2):
                nc.gpsimd.memset(double[d][1][:].bitcast(F32), 0.0).then_inc(odd_zeroed, 1)
                nc.gpsimd.memset(single[d][1][:].bitcast(F32), 0.0).then_inc(odd_zeroed, 1)
            pool.wait_ge(odd_zeroed, 4)
            for d in range(2):
                for e in range(2):
                    nc.gpsimd.memset(spread[d][e][96:128].bitcast(F32), 1.0).then_inc(zeroed, 1)

            pool.wait_ge(zeroed, 8)
            for p in range(2):
                nc.gpsimd.memset(cell[p][:], 0.0).then_inc(gates_zero, 1)
            pool.wait_ge(gates_zero, 2)
            for a in (sig_i, sig_f, tanh_g, sig_o):
                for p in range(2):
                    nc.gpsimd.memset(a[p][32:64], 0.0).then_inc(gates_zero, 1)
            pool.wait_ge(gates_zero, 10)

            def body(i, first, last):
                for k in range(8):
                    e, p, d = k // 4, k % 4 // 2, k % 2
                    s = 8 * i + k
                    if k % 4 == 0 and not last:
                        b = 2 * i + e + AHEAD_X
                        pool.wait_ge(x_high, b + 1)
                        at_least(pool, lo_ready, s)
                        nc.gpsimd.tensor_tensor(x_parts[e][BOTH, 1, :, 1:1 + W], x_raw[BOTH, e],
                                                x_parts[e][BOTH, 0, :, 1:1 + W], ALU.subtract).then_inc(x_low, 1)
                        pool.wait_ge(x_low, b + 1)
                    pool.wait_ge(double_ready, s + 1)
                    at_least(pool, lo_ready, s)
                    own, other = lanes(d), lanes(1 - d)
                    nc.gpsimd.tensor_tensor(double[d][1 - e][other, halves(p), 1:1 + W], h_new[e][own, halves(p)],
                                            double[d][1 - e][own, halves(p), 1:1 + W], ALU.subtract).then_inc(lo_ready, 1)

            turns(pool, body)


def projection(nc, h_rows, w_proj, y, stats):
    ROWS, BUFS = 2, 4
    TURN = ROWS * BUFS
    with ExitStack() as ctx:
        def sem(name):
            return ctx.enter_context(nc.semaphore(name))

        wp = ctx.enter_context(nc.sbuf_tensor("wp", [P, 64], F32))
        h_in = [ctx.enter_context(nc.sbuf_tensor(f"h_in{n}", [P, ROWS, B, W], F32)) for n in range(BUFS)]
        ps = ctx.enter_context(nc.psum_tensor("proj", [P, TURN, 512], F32))
        wp_loaded, gaps_zero = sem("wp_loaded"), sem("gaps_zero")
        h_loaded = [sem(f"h_loaded{n}") for n in range(BUFS)]
        row_summed, row_kept, row_measured = sem("row_summed"), sem("row_kept"), sem("row_measured")
        block = ctx.enter_context(nc.Block())

        @block.sync
        def _(sp):
            sp.dma_start(wp[:], w_proj).then_inc(wp_loaded, 16)

            def body(i, first):
                for n in range(BUFS):
                    if first:
                        sp.wait_ge(gaps_zero, n + 1)
                    r = TURN * i + ROWS * n
                    at_least(sp, row_summed, r - TURN + ROWS)
                    for d in range(2):
                        sp.dma_start(h_in[n][64 * d:64 * d + HC], h_rows[BUFS * i + n, d]).then_inc(h_loaded[n], 16)

            body(0, True)
            with sp.Fori(1, H // TURN) as i:
                body(i, False)

        @block.tensor
        def _(pe):
            pe.wait_ge(wp_loaded, 16)

            def body(i, first):
                for k in range(TURN):
                    if k % ROWS == 0:
                        pe.wait_ge(h_loaded[k // ROWS], 32 * i + 32)
                    at_least(pe, row_kept, TURN * (i - 1) + k + 1)
                    for half in range(2):
                        mm = nc.tensor.matmul(ps[64 * half:64 * half + 64, k, 0:NH], wp[:],
                                              h_in[k // ROWS][:, k % ROWS, HB * half:HB * half + HB, :],
                                              start=True, stop=True)
                    mm.then_inc(row_summed, 1)

            body(0, True)
            with pe.Fori(1, H // TURN) as i:
                body(i, False)

        @block.scalar
        def _(act):
            with act.Fori(0, H // TURN) as i:
                for k in range(TURN):
                    act.wait_ge(row_summed, TURN * i + k + 1)
                    nc.scalar.activation(y[:, :, bass.ds(TURN * i + k, 1), :],
                                         ps[:, k, 0:NH].rearrange("p (b r w) -> p b r w", b=HB, r=1),
                                         ACT.Identity).then_inc(row_kept, 1)

        @block.vector
        def _(dve):
            for n in range(BUFS):
                nc.vector.memset(h_in[n][:], 0.0).then_inc(gaps_zero, 1)
            with dve.Fori(0, H // TURN) as i:
                for k in range(TURN):
                    dve.wait_ge(row_kept, TURN * i + k + 1)
                    nc.vector.bn_stats(stats[:, bass.ds((TURN * i + k) * 6, 6)],
                                       y[:, :, bass.ds(TURN * i + k, 1), :]).then_inc(row_measured, 1)
            dve.wait_ge(row_measured, H)


PACKS_STORED = (32 * (HB // 2), 32 * (HB // 2 + 1))


STORES = (8, 12, 7)
assert sum(STORES) * X1_PART == HB * PX + AGAIN * CPX


def store_x1(sp, y, x1_lanes, x1_stored, i):
    part = i % (HB * PX // X1_PART)
    sp.dma_start(x1_lanes[:, i * X1_PART:(i + 1) * X1_PART],
                 y[0:HI + C].rearrange("p b r w -> p (b r w)")[:, part * X1_PART:(part + 1) * X1_PART]
                 ).then_inc(x1_stored, 16)


def residual(nc, y, stats, consts, norms, x_lanes, x1_lanes, sums, folded, x1_stored, prefetch):
    PART = X1_PART
    PARTS = HB * PX // PART
    BUFS = 3
    with ExitStack() as ctx:
        def sb(name, shape, dt=F32):
            return ctx.enter_context(nc.sbuf_tensor(name, shape, dt))

        def sem(name):
            return ctx.enter_context(nc.semaphore(name))

        pairing = sb("pairing", [P, P])
        nv = sb("nv", [P, 4, 8])
        half_stat = sb("half_stat", [P, 2])
        moments = sb("moments", [P, 2])
        root = sb("root", [P, 8])
        ratio = sb("ratio", [P, 8])
        tmp = sb("tmp", [P, 8])
        x_in = [sb(f"x_in{n}", [P, PART]) for n in range(BUFS)]
        part_sums = sb("part_sums", [P, PARTS])
        ps = ctx.enter_context(nc.psum_tensor("moment_ps", [P, 2], F32))
        pairing_loaded, nv_loaded, x_gaps = sem("pairing_loaded"), sem("nv_loaded"), sem("x_gaps")
        x_loaded = [sem(f"x2_loaded{n}") for n in range(BUFS)]
        step, averaged, rooted, relued, added = (sem(n) for n in ("step", "averaged", "rooted", "relued", "added"))
        block = ctx.enter_context(nc.Block())

        @block.sync
        def _(sp):
            sp.dma_start(pairing[:], consts[:, 0:P]).then_inc(pairing_loaded, 16)
            sp.dma_start(nv[:], norms).then_inc(nv_loaded, 16)

            def load(i, n):
                for half in range(2):
                    sp.dma_start(x_in[n][64 * half:64 * half + C],
                                 x_lanes[half, :, bass.ds((BUFS * i + n) * PART, PART)]).then_inc(x_loaded[n], 16)

            for n in range(BUFS):
                sp.wait_ge(x_gaps, n + 1)
                load(0, n)
            with sp.Fori(1, PARTS // BUFS) as i:
                for n in range(BUFS):
                    sp.wait_ge(added, BUFS * (i - 1) + n + 1)
                    load(i, n)

            prefetch(sp)
            for i in range(STORES[0]):
                sp.wait_ge(added, i + 1)
                store_x1(sp, y, x1_lanes, x1_stored, i)

        @block.tensor
        def _(pe):
            pe.wait_ge(pairing_loaded, 16)
            pe.wait_ge(step, 3)
            nc.tensor.matmul(ps[:], pairing[:], moments[:], start=True, stop=True).then_inc(averaged, 1)

        @block.scalar
        def _(act):
            act.wait_ge(step, 6)
            nc.scalar.activation(root[:], tmp[:], ACT.Sqrt).then_inc(rooted, 1)
            act.wait_ge(step, 13)
            with act.Fori(0, PARTS // BUFS) as i:
                for n in range(BUFS):
                    at = y[:].rearrange("p b r w -> p (b r w)")[:, bass.ds((BUFS * i + n) * PART, PART)]
                    nc.scalar.activation(at, at, ACT.Relu, bias=folded[:, 1, 7:8],
                                         scale=folded[:, 0, 7:8]).then_inc(relued, 1)

        @block.vector
        def _(dve):
            for n in range(BUFS):
                nc.vector.memset(x_in[n][:], 0.0).then_inc(x_gaps, 1)
            count = [0]

            def then(ins):
                count[0] += 1
                ins.then_inc(step, 1)
                dve.wait_ge(step, count[0])

            then(nc.vector.bn_aggr(half_stat[:], stats[:]))
            then(nc.vector.tensor_copy(moments[:, 0:1], half_stat[:, 0:1]))
            then(nc.vector.scalar_tensor_tensor(moments[:, 1:2], half_stat[:, 0:1], half_stat[:, 0:1],
                                                half_stat[:, 1:2], ALU.mult, ALU.add))
            dve.wait_ge(averaged, 1)
            dve.wait_ge(nv_loaded, 16)
            then(nc.vector.tensor_copy(half_stat[:], ps[:]))
            nc.vector.tensor_copy(nv[:, 3, 7:8], half_stat[:, 0:1]).then_inc(x_gaps, 1)
            dve.wait_ge(x_gaps, BUFS + 1)
            nc.vector.tensor_scalar(ratio[:, 0:1], half_stat[:, 0:1], half_stat[:, 0:1], -1.0, ALU.mult,
                                    ALU.mult).then_inc(x_gaps, 1)
            dve.wait_ge(x_gaps, BUFS + 2)
            then(nc.vector.tensor_tensor(nv[:, 0, 7:8], ratio[:, 0:1], half_stat[:, 1:2], ALU.add))
            then(nc.vector.tensor_scalar(tmp[:], nv[:, 0, :], EPS, None, ALU.add))
            dve.wait_ge(rooted, 1)
            then(nc.vector.reciprocal(ratio[:], root[:]))
            then(nc.vector.tensor_tensor(ratio[:], ratio[:], tmp[:], ALU.mult))
            then(nc.vector.tensor_tensor(ratio[:], ratio[:], root[:], ALU.add))
            then(nc.vector.tensor_scalar(root[:], ratio[:], 0.5, None, ALU.mult))
            then(nc.vector.reciprocal(ratio[:], root[:]))
            then(nc.vector.tensor_tensor(folded[:, 0, :], ratio[:], nv[:, 1, :], ALU.mult))
            nc.vector.tensor_tensor(tmp[:], folded[:, 0, :], nv[:, 3, :], ALU.mult).then_inc(x_gaps, 1)
            dve.wait_ge(x_gaps, BUFS + 3)
            then(nc.vector.tensor_tensor(folded[:, 1, :], nv[:, 2, :], tmp[:], ALU.subtract))
            with dve.Fori(0, PARTS // BUFS) as i:
                for n in range(BUFS):
                    dve.wait_ge(relued, BUFS * i + n + 1)
                    dve.wait_ge(x_loaded[n], 32 * i + 32)
                    at = y[:].rearrange("p b r w -> p (b r w)")[:, bass.ds((BUFS * i + n) * PART, PART)]
                    nc.vector.scalar_tensor_tensor(at, at, 1.0, x_in[n][:], ALU.mult, ALU.add,
                                                   accum_out=part_sums[:, bass.ds(BUFS * i + n, 1)]).then_inc(added, 1)
            dve.wait_ge(added, PARTS)
            then(nc.vector.tensor_reduce(sums[:], part_sums[:].rearrange("p (b n) -> p b n", b=HB), AX.X, ALU.add))


def selection(nc, sums, folded, cst, ws, bs, par, loaded, place, passes, y, x1_lanes, x1_stored):
    with ExitStack() as ctx:
        def sb(name, shape, dt=F32):
            return ctx.enter_context(nc.sbuf_tensor(name, shape, dt))

        def sem(name):
            return ctx.enter_context(nc.semaphore(name))

        ident, ones = cst[:, P:2 * P], cst[:, 2 * P:3 * P]
        before = cst[:, 3 * P:3 * P + HG]
        sal = sb("sal", [HG, NG, B])
        spread = [sb(f"spread{n}", [HG, NG, HG]) for n in range(2)]
        above = sb("above", [HG, NG, B])
        chosen = sb("chosen", [HG, NG, B])
        scratch = sb("scratch", [HG, NG, HID])
        most = sb("most", [HG, 1])
        ps_s = ctx.enter_context(nc.psum_tensor("ps_s", [P, NG, B], F32))
        ps_b = [ctx.enter_context(nc.psum_tensor(f"ps_b{n}", [P, 512], F32)) for n in range(2)]
        ps_p = ctx.enter_context(nc.psum_tensor("ps_p", [P, NG, B], F32))
        ps_t = ctx.enter_context(nc.psum_tensor("ps_t", [P, B], F32))
        dve_did, pe_did, act_did = (sem(n) for n in ("dve_did", "pe_did", "act_did"))
        block = ctx.enter_context(nc.Block())
        d, t = [0], [0]
        marks = {}

        @block.sync
        def _(sp):
            for i in range(STORES[1]):
                store_x1(sp, y, x1_lanes, x1_stored, STORES[0] + i)

        @block.vector
        def _(dve):
            def do(ins, wait=True):
                d[0] += 1
                ins.then_inc(dve_did, 1)
                if wait:
                    dve.wait_ge(dve_did, d[0])

            dve.wait_ge(loaded, 80)
            for g in range(NG):
                do(nc.vector.tensor_copy(par[:, g, S1:T1 + 1], folded[0:HG, :, g]), False)
                do(nc.vector.tensor_copy(par[:, g, SD:TD + 1], folded[0:HG, :, NG + g]), False)
            dve.wait_ge(act_did, NG)

            def spread_out(b):
                for g in range(NG):
                    do(nc.vector.tensor_scalar(spread[b % 2][:, g, :], ident[0:HG, 0:HG], sal[:, g, b:b + 1], None,
                                               ALU.mult), False)
                marks["spread", b] = d[0]

            spread_out(0)
            for b in range(B):
                if b + 1 < B:
                    spread_out(b + 1)
                dve.wait_ge(pe_did, marks_pe("spread", b))
                if b:
                    dve.wait_ge(dve_did, marks["counted", b - 1])
                for g in range(NG):
                    do(nc.vector.tensor_scalar(scratch[:, g, :], ps_b[b % 2][0:HG, 0:HID], sal[:, g, b:b + 1], 0.0,
                                               ALU.is_gt, ALU.add, accum_out=above[:, g, b:b + 1]), False)
                marks["counted", b] = d[0]
            dve.wait_ge(dve_did, d[0])
            do(nc.vector.tensor_scalar(chosen[:], above[:], float(TOPK), None, ALU.is_lt))
            marks["chosen"] = d[0]
            dve.wait_ge(pe_did, marks_pe("places", 0))
            do(nc.vector.scalar_tensor_tensor(place[:], ps_p[0:HG], 1.0, chosen[:], ALU.add, ALU.mult))
            do(nc.vector.tensor_scalar(place[:], place[:], -1.0, None, ALU.add))
            do(nc.vector.tensor_reduce(most[:], ps_t[0:HG], AX.X, ALU.max))
            do(nc.vector.tensor_scalar(passes[0:1, 0:1], most[0:1], float(TOPK), 1.0, ALU.is_gt, ALU.add))

        @block.scalar
        def _(act):
            act.wait_ge(pe_did, 1)
            for g in range(NG):
                nc.scalar.activation(sal[:, g, :], ps_s[0:HG, g, :], ACT.Sigmoid, bias=bs[:, g:g + 1],
                                     scale=1.0 / PX).then_inc(act_did, 1)

        @block.tensor
        def _(pe):
            def did(mm, name):
                mm.then_inc(pe_did, 1)
                t[0] += 1
                assert t[0] == marks_pe(*name), name

            pe.wait_ge(loaded, 80)
            for g in range(NG):
                for half in range(2):
                    mm = nc.tensor.matmul(ps_s[0:HG, g, HB * half:HB * half + HB], ws[:, half, g, :], sums[:],
                                          start=(g == 0 and half == 0), stop=(g == NG - 1 and half == 1),
                                          skip_group_check=True)
            did(mm, ("sal", 0))
            for b in range(B):
                pe.wait_ge(dve_did, marks["spread", b])
                if b >= 2:
                    pe.wait_ge(dve_did, marks["counted", b - 2])
                did(nc.tensor.matmul(ps_b[b % 2][0:HG, 0:HID], ones[0:HG, 0:HG], spread[b % 2][:], start=True, stop=True),
                    ("spread", b))
            pe.wait_ge(dve_did, marks["chosen"])
            first = True
            for g in range(NG):
                for k in range(g + 1):
                    nc.tensor.matmul(ps_p[0:HG, g, :], (before if k == g else ones)[0:HG, 0:HG], chosen[:, k, :],
                                     start=first, stop=(g == NG - 1 and k == g), skip_group_check=True)
                    first = False
            for g in range(NG):
                mm = nc.tensor.matmul(ps_t[0:HG, :], ones[0:HG, 0:HG], chosen[:, g, :], start=(g == 0), stop=(g == NG - 1))
            did(mm, ("places", 0))


def marks_pe(what, n):
    if what == "sal":
        return 1
    if what == "spread":
        return 2 + n
    if what == "places":
        return 2 + B


def gather(nc, q, cst, par, w1, place, folded, pack_r, pack_f, packs_r, packs_f, stored, passes, y, x1_lanes,
           x1_stored):
    with ExitStack() as ctx:
        def sem(name):
            return ctx.enter_context(nc.semaphore(f"{name}_{q}"))

        ident = cst[:, P:2 * P]
        places = cst[0:HG, 3 * P + HG + q * UNITS * UC:3 * P + HG + (q + 1) * UNITS * UC]
        onehot = [[ctx.enter_context(nc.sbuf_tensor(f"onehot{q}{n}{h}", [HG, NG, UNITS * UC], F32)) for h in range(2)]
                  for n in range(2)]
        ps_w = [ctx.enter_context(nc.psum_tensor(f"ps_w{q}{n}", [P, 512], F32)) for n in range(2)]
        ps_q = [ctx.enter_context(nc.psum_tensor(f"ps_q{q}{n}", [P, 512], F32)) for n in range(2)]
        cleared, onehot_ready, gathered, copied, low_ready, packed = (
            sem(n) for n in ("cleared", "onehot_ready", "gathered", "copied", "low_ready", "packed"))
        before = [q * PACKS_STORED[n] for n in range(2)]
        block = ctx.enter_context(nc.Block())

        def guarded(eng, program):
            if q == 0:
                program()
            else:
                n = eng.value_load(passes[0:1, 0:1], min_val=1, max_val=2)
                with eng.If(n > 1):
                    program()

        @block.sync
        def _(sp):
            def program():
                def store(at, n):
                    sp.dma_start(packs_r[at], pack_r[n][:].bitcast(F32)).then_inc(stored[n], 16)
                    sp.dma_start(packs_f[at], pack_f[n][:]).then_inc(stored[n], 16)

                for pair in range(HB):
                    if q == 0:
                        for i in range(pair, STORES[2], HB):
                            store_x1(sp, y, x1_lanes, x1_stored, STORES[0] + STORES[1] + i)
                    sp.wait_ge(packed, pair + 1)
                    sp.wait_ge(low_ready, pair + 1)
                    store(HB * q + pair, pair % 2)
                store(HB * (q + 1), 1)
                if q == 1:
                    for n in range(2):
                        sp.wait_ge(stored[n], before[n] + PACKS_STORED[n])

            guarded(sp, program)
            if q == 1:
                sp.wait_ge(x1_stored, 16 * sum(STORES))

        @block.tensor
        def _(pe):
            def program():
                for pair in range(HB):
                    n = pair % 2
                    pe.wait_ge(onehot_ready, pair + 1)
                    at_least(pe, low_ready, pair - 1)
                    for half in range(2):
                        lanes = slice(64 * half, 64 * half + 64)
                        for g in range(NG):
                            nc.tensor.matmul(ps_w[n][lanes, 0:UNITS * UC], w1[:, g, :], onehot[n][half][:, g, :],
                                             start=(g == 0), stop=(g == NG - 1))
                        for u in range(UNITS):
                            for g in range(NG):
                                mm = nc.tensor.matmul(ps_q[n][lanes, u * NPAR:(u + 1) * NPAR],
                                                      onehot[n][half][:, g, u * UC:(u + 1) * UC], par[:, g, :],
                                                      start=(g == 0), stop=(g == NG - 1), skip_group_check=True)
                    mm.then_inc(gathered, 1)

            guarded(pe, program)

        @block.scalar
        def _(act):
            def program():
                for pair in range(HB):
                    n = pair % 2
                    act.wait_ge(copied, pair + 1)
                    for u in range(UNITS):
                        for k, tap in enumerate(PE_TAPS):
                            at = PK_DIAG + (u * len(PE_TAPS) + k) * P
                            col = PK_PAR + u * 13 + TAP + tap
                            diag = nc.scalar.activation(pack_f[n][:, at:at + P], ident, ACT.Copy,
                                                        scale=pack_f[n][:, col:col + 1])
                    diag.then_inc(packed, 1)

            guarded(act, program)

        @block.vector
        def _(dve):
            def program():
                for n in range(2):
                    if q == 0:
                        nc.vector.memset(pack_r[n][:].bitcast(F32), 0.0)
                        clear = nc.vector.memset(pack_f[n][:], 0.0)
                    else:
                        dve.wait_ge(stored[n], before[n])
                        clear = nc.vector.memset(pack_f[n][:, PK_S2 + 1:PK_S2 + 2], 0.0)
                clear.then_inc(cleared, 1)
                dve.wait_ge(cleared, 1)
                if q == 0:
                    for n in range(2):
                        nc.vector.tensor_copy(pack_f[n][:, PK_S2:PK_S2 + 2], folded[:, :, 6])

                def mark(pair):
                    at_least(dve, gathered, pair - 1)
                    for half in range(2):
                        b = HB * half + pair
                        for g in range(NG):
                            one = nc.vector.tensor_scalar(onehot[pair % 2][half][:, g, :], places, place[:, g, b:b + 1],
                                                          None, ALU.is_equal)
                    one.then_inc(onehot_ready, 1)

                mark(0)
                for pair in range(HB):
                    n = pair % 2
                    if pair + 1 < HB:
                        mark(pair + 1)
                    dve.wait_ge(gathered, pair + 1)
                    at_least(dve, stored[n], before[n] + 32 * (pair // 2))
                    r = pack_r[n][:].rearrange("p (k u m) -> p k u m", k=2, u=UNITS)
                    f = pack_f[n][:, 0:UNITS * P].rearrange("p (u m) -> p u m", u=UNITS)
                    src = ps_w[n][:, 0:UNITS * UC].rearrange("p (u r) -> p u r", u=UNITS)
                    got = ps_q[n][:, 0:UNITS * NPAR].rearrange("p (u m) -> p u m", u=UNITS)
                    for half in range(2):
                        lanes = slice(64 * half, 64 * half + 64)
                        nc.vector.tensor_copy(r[lanes, 0, :, lanes], src[lanes])
                        nc.vector.tensor_copy(f[lanes, :, 64 * half:64 * half + HC], got[lanes, :, W2:W2 + HC])
                    nc.vector.tensor_copy(pack_f[n][:, PK_PAR:PK_S2].rearrange("p (u m) -> p u m", u=UNITS),
                                          got[:, :, 0:W2]).then_inc(copied, 1)
                    dve.wait_ge(copied, pair + 1)
                    for half in range(2):
                        lanes = slice(64 * half, 64 * half + 64)
                        low = nc.vector.tensor_tensor(r[lanes, 1, :, lanes], src[lanes], r[lanes, 0, :, lanes],
                                                      ALU.subtract)
                    low.then_inc(low_ready, 1)

            guarded(dve, program)


def bottleneck(nc, w_mask, b_mask, x1_lanes, out_lanes, packs_r, packs_f, passes, packs_stored):
    AHEAD = 3
    NT = len(DVE_TAPS)
    with ExitStack() as ctx:
        def sb(name, shape, dt=F32):
            return ctx.enter_context(nc.sbuf_tensor(name, shape, dt))

        def sem(name):
            return ctx.enter_context(nc.semaphore(name))

        pk_r = [sb(f"pk_r{n}", [P, PKR], F32R) for n in range(2)]
        pk_f = [sb(f"pk_f{n}", [P, PKF]) for n in range(2)]
        wm_raw, bm = sb("wm_raw", [P, P]), sb("bm", [P, 1])
        wm = [sb("wm_hi", [P, P], F32R), sb("wm_lo", [P, P], F32R)]
        x1 = [sb(f"x1_{n}", [P, CPX]) for n in range(3)]
        xh = [sb(f"xh{n}", [P, CPX], F32R) for n in range(3)]
        xl = [sb(f"xl{n}", [P, CPX], F32R) for n in range(3)]
        base = [sb(f"base{n}", [P, CPX]) for n in range(3)]
        outb = [sb(f"outb{n}", [P, CPX]) for n in range(3)]
        logits = [sb(f"logits{n}", [P, CPX]) for n in range(3)]
        h1 = sb("h1", [P, UNITS, 3, CH + 2, WP])
        acc = [sb(f"acc{n}", [P, CPX]) for n in range(3)]
        prod = [[sb(f"prod{n}{m}", [P, CPX]) for m in range(2)] for n in range(3)]
        full = [sb(f"full{n}", [P, CPX]) for n in range(3)]
        h2 = [sb(f"h2_{n}", [P, CPX]) for n in range(3)]
        zeros = sb("zeros", [P, UNITS, WP])
        z = sb("z", [P, CPX])
        zm = sb("zm", [P, CPX])
        ps1 = [ctx.enter_context(nc.psum_tensor(f"ps1_{n}", [P, 2, 512], F32)) for n in range(2)]
        psd = ctx.enter_context(nc.psum_tensor("psd", [P, 2, 512], F32))
        ps2 = ctx.enter_context(nc.psum_tensor("ps2", [P, 2, 512], F32))

        gaps_clear = sem("gaps_clear")
        mask_loaded, wm_split, borders = sem("mask_loaded"), sem("wm_split"), sem("borders")
        pack_in = [sem(f"pack_in{n}") for n in range(2)]
        x1_in = [sem(f"x1_in{n}") for n in range(3)]
        base_in = [sem(f"base_in{n}") for n in range(3)]
        out_stored = [sem(f"out_stored{n}") for n in range(3)]
        xh_done, xl_done, logits_done, z_done, zm_done, out_done = (
            sem(n) for n in ("xh_done", "xl_done", "logits_done", "z_done", "zm_done", "out_done"))
        pw1_done = sem("pw1_done")
        relu1_done, taps_done, psd_read, chain, acc_done, prod_done, pair_sum, full_done, relu2_done, pw2_done = (
            sem(n) for n in ("relu1_done", "taps_done", "psd_read", "chain", "acc_done", "prod_done", "pair_sum",
                             "full_done", "relu2_done", "pw2_done"))
        above_done, below_done = sem("above_done"), sem("below_done")

        def rows(ap):
            return ap.rearrange("p (m r w) -> p m r w", m=2, w=W)

        def banks(ps):
            return ps[:, :, 0:NH].rearrange("p m (r w) -> p m r w", w=W)

        def window(j, slot, tap):
            dy, dx = divmod(tap, 3)
            return h1[:, j, slot, dy:dy + CH, dx:dx + W].rearrange("p (m r) w -> p m r w", m=2)

        def par(pp, j, col):
            return pk_f[pp][:, PK_PAR + 13 * j + col:PK_PAR + 13 * j + col + 1]


        def run(eng, step):
            step(0, 0, lambda k: 0, 0, 0)
            n = eng.value_load(passes[0:1, 0:1], min_val=1, max_val=2)
            with eng.Fori(0, n * (HB // 2)) as o:
                for pp in range(2):
                    def pack(k):
                        return 1 - pp if isinstance(k, int) and k >= NCH else pp

                    for k in (1, 2):
                        step(2 * o + pp, k, pack, k, 0)
                    with eng.Fori(1, 3) as m:
                        for e in range(3):
                            step(2 * o + pp, 3 * m + e, lambda k: pp, e, m)
                    for k in range(9, NCH + 1):
                        step(2 * o + pp, k, pack, k % 3, k // 3)

        def chunk0(Pi):
            return NCH * Pi + AHEAD

        def nth(Pi, third):
            return 64 * Pi + 16 * third + 16

        def pack_count(Pi, pp):
            return 16 * (Pi - pp) + 32

        block = ctx.enter_context(nc.Block())

        @block.sync
        def _(sp):
            for n in range(3):
                sp.sem_inc(out_stored[n], 16)
            for k in range(5):
                if k < 3:
                    sp.wait_ge(gaps_clear, k + 1)
                else:
                    sp.wait_ge(xl_done, AHEAD + k - 2)
                if k == 1:
                    sp.dma_start(wm_raw[:], w_mask).then_inc(mask_loaded, 16)
                    sp.dma_start(bm[:], b_mask).then_inc(mask_loaded, 16)
                if k == 2:
                    for n in range(2):
                        sp.wait_ge(packs_stored[n], PACKS_STORED[n])
                    sp.dma_start(pk_r[0][:].bitcast(F32), packs_r[0]).then_inc(pack_in[0], 16)
                    sp.dma_start(pk_f[0][:], packs_f[0]).then_inc(pack_in[0], 16)
                sp.dma_start(x1[k % 3][0:HI + C], x1_lanes[:, k * CPX:(k + 1) * CPX]).then_inc(x1_in[k % 3], 16)
            sp.wait_ge(gaps_clear, 6)
            npass = sp.value_load(passes[0:1, 0:1], min_val=1, max_val=2)

            def one_pass(q):
                before = x1_lanes if q == 0 else out_lanes

                def cols(pair, k):
                    return bass.ds((NCH * pair + k) * CPX, CPX)

                def load_x1(pair, Ci, k, n):
                    sp.wait_ge(xl_done, Ci - 2)
                    sp.dma_start(x1[n][0:HI + C], x1_lanes[:, cols(pair, k)]).then_inc(x1_in[n], 16)

                def load_base(pair, Ci, k, n):
                    sp.wait_ge(out_done, Ci - 2)
                    sp.dma_start(base[n][0:HI + C], before[:, cols(pair, k)]).then_inc(base_in[n], 16)

                def store(pair, Ci, k, n):
                    sp.wait_ge(out_done, Ci + 1)
                    sp.dma_start(out_lanes[:, cols(pair, k)], outb[n][0:HI + C]).then_inc(out_stored[n], 16)

                with sp.Fori(0, HB // 2) as o:
                    for pp in range(2):
                        pair = 2 * o + pp
                        Pi = pair + HB * q
                        C0 = chunk0(Pi)
                        sp.wait_ge(z_done, C0)
                        sp.dma_start(pk_r[1 - pp][:].bitcast(F32), packs_r[Pi + 1]).then_inc(pack_in[1 - pp], 16)
                        sp.dma_start(pk_f[1 - pp][:], packs_f[Pi + 1]).then_inc(pack_in[1 - pp], 16)
                        for k in range(3):
                            load_base(pair, C0 + k, k, k)
                        with sp.Fori(0, 3) as m:
                            for e in range(3):
                                k = 3 * m + e
                                load_x1(pair, C0 + k + 5, k + 5, (e + 2) % 3)
                                store(pair, C0 + k, k, e)
                                load_base(pair, C0 + k + 3, k + 3, e)
                        for k in range(9, NCH):
                            load_x1(pair, C0 + k + 5, k + 5, (k + 5) % 3)
                            store(pair, C0 + k, k, k % 3)
                for n in range(3):
                    sp.wait_ge(out_stored[n], nth(HB * (q + 1), 0))
                    sp.wait_ge(x1_in[n], nth(HB * (q + 1), 1 if n < 2 else 0))

            one_pass(0)
            with sp.If(npass > 1):
                one_pass(1)
            sp.wait_ge(pack_in[0], 32)
            sp.wait_ge(pack_in[1], 32)

        @block.tensor
        def _(pe):
            pe.sem_inc(pw1_done, 4 * AHEAD)
            pe.sem_inc(taps_done, 3 * AHEAD)
            pe.sem_inc(pw2_done, 3 * AHEAD)
            pe.wait_ge(wm_split, 2)
            pe.wait_ge(borders, 2)

            def pw1(Ci, n, pp, u):
                if u == 0:
                    pe.wait_ge(xl_done, Ci + 1)
                    pe.wait_ge(relu1_done, 3 * Ci)
                elif u == 1:
                    pe.wait_ge(logits_done, Ci)
                else:
                    pe.wait_ge(relu1_done, 3 * Ci + u - 1)
                if u < UNITS:
                    hi, lo = pk_r[pp][:, u * P:(u + 1) * P], pk_r[pp][:, (UNITS + u) * P:(UNITS + u + 1) * P]
                else:
                    hi, lo = wm[0][:], wm[1][:]
                for m in range(2):
                    for i, (w, v) in enumerate(((hi, xh[n]), (hi, xl[n]), (lo, xh[n]))):
                        mm = nc.tensor.matmul(ps1[u % 2][:, m, 0:NH], w, v[:, m * NH:(m + 1) * NH],
                                              start=(i == 0), stop=(i == 2))
                mm.then_inc(pw1_done, 1)

            def taps(Ci, slot, pp, j):
                if j == 0:
                    pe.wait_ge(above_done, Ci + 1)
                pe.wait_ge(psd_read, 3 * Ci + j)
                for m in range(2):
                    for i, tap in enumerate(PE_TAPS):
                        at = PK_DIAG + (j * len(PE_TAPS) + i) * P
                        mm = nc.tensor.matmul(psd[:, m, 0:NH], pk_f[pp][:, at:at + P], window(j, slot, tap)[:, m],
                                              start=(i == 0), stop=(i == len(PE_TAPS) - 1))
                mm.then_inc(taps_done, 1)

            def pw2(Ci, pp, j):
                pe.wait_ge(relu2_done, 3 * Ci + j + 1)
                if j == 0:
                    pe.wait_ge(z_done, Ci)
                for m in range(2):
                    mm = nc.tensor.matmul(ps2[:, m, 0:NH], pk_f[pp][:, j * P:(j + 1) * P], h2[j][:, m * NH:(m + 1) * NH],
                                          start=(j == 0), stop=(j == UNITS - 1), skip_group_check=True)
                mm.then_inc(pw2_done, 1)

            def step(Pi, k, pack, slot, third):
                Ci, nxt = chunk0(Pi) + k, (slot + 2) % 3
                before, now, then, ahead = (pack(k + n) for n in (-1, 0, 1, 2))
                inside = not (isinstance(k, int) and k == 0)
                if isinstance(k, int) and k == NCH - 2:
                    pe.wait_ge(pack_in[ahead], pack_count(Pi + 1, ahead))
                pw1(Ci + 2, nxt, ahead, 0)
                taps(Ci, slot, now, 1)
                if inside:
                    pw2(Ci - 1, before, 1)
                pw1(Ci + 2, nxt, ahead, 1)
                taps(Ci, slot, now, 2)
                if inside:
                    pw2(Ci - 1, before, 2)
                pw1(Ci + 2, nxt, ahead, 2)
                pw1(Ci + 2, nxt, ahead, UNITS)
                taps(Ci + 1, (slot + 1) % 3, then, 0)
                pw2(Ci, now, 0)

            pe.wait_ge(pack_in[0], 32)
            for k in range(2):
                for u in range(UNITS + 1):
                    pw1(AHEAD + k, k, 0, u)
                if k == 0:
                    taps(AHEAD, 0, 0, 0)
            run(pe, step)

        @block.scalar
        def _(act):
            act.sem_inc(xh_done, AHEAD)
            act.sem_inc(relu1_done, 3 * AHEAD)
            act.sem_inc(prod_done, 6 * AHEAD)
            act.sem_inc(relu2_done, 3 * AHEAD)
            act.sem_inc(z_done, AHEAD)
            act.sem_inc(logits_done, AHEAD)
            act.sem_inc(above_done, AHEAD)
            act.sem_inc(below_done, AHEAD)
            act.wait_ge(borders, 2)

            def high(Ci, n, loads):
                act.wait_ge(x1_in[n], loads)
                act.wait_ge(pw1_done, 4 * Ci - 8)
                nc.scalar.activation(xh[n][:], x1[n][:], ACT.Copy).then_inc(xh_done, 1)

            def relu1(Ci, n, pp, j):
                act.wait_ge(pw1_done, 4 * Ci + j + 1)
                act.wait_ge(taps_done, 3 * Ci + j - 8)
                act.wait_ge(acc_done, 3 * Ci + j - 8)
                act.wait_ge(prod_done, 6 * Ci + 2 * j - 16)
                nc.scalar.activation(h1[:, j, n, 1:1 + CH, 1:1 + W].rearrange("p (m r) w -> p m r w", m=2),
                                     banks(ps1[j % 2]), ACT.Relu, bias=par(pp, j, T1),
                                     scale=par(pp, j, S1)).then_inc(relu1_done, 1)

            def logit(Ci, n):
                act.wait_ge(pw1_done, 4 * Ci + 4)
                act.wait_ge(zm_done, Ci - 2)
                nc.scalar.activation(rows(logits[n][:]), banks(ps1[1]), ACT.Identity, bias=bm[:, 0:1]).then_inc(logits_done, 1)

            def halo(Ci, n, edge=False):
                prev = (n + 2) % 3
                act.wait_ge(relu1_done, 3 * Ci + 3)
                last, first = h1[:, :, prev, CH, 1:1 + W], h1[:, :, n, 1, 1:1 + W]
                if edge:
                    last = first = zeros[:, :, 0:W]
                nc.scalar.activation(h1[:, :, prev, CH + 1, 1:1 + W], first, ACT.Copy).then_inc(below_done, 1)
                nc.scalar.activation(h1[:, :, n, 0, 1:1 + W], last, ACT.Copy).then_inc(above_done, 1)

            def prods(Ci, slot, pp, j):
                if j == 0:
                    act.wait_ge(above_done, Ci + 1)
                act.wait_ge(full_done, 3 * Ci + j - 2)
                for i, tap in enumerate(ACT_TAPS):
                    nc.scalar.activation(rows(prod[j][i][:]), window(j, slot, tap), ACT.Copy,
                                         scale=par(pp, j, TAP + tap)).then_inc(prod_done, 1)

            def relu2(Ui, pp, j):
                act.wait_ge(full_done, Ui + 1)
                act.wait_ge(pw2_done, Ui - 2)
                nc.scalar.activation(h2[j][:], full[j][:], ACT.Relu, bias=par(pp, j, TD),
                                     scale=par(pp, j, SD)).then_inc(relu2_done, 1)

            def norm2(Ci, pp):
                act.wait_ge(pw2_done, 3 * Ci + 3)
                act.wait_ge(zm_done, Ci)
                nc.scalar.activation(rows(z[:]), banks(ps2), ACT.Identity, bias=pk_f[pp][:, PK_S2 + 1:PK_S2 + 2],
                                     scale=pk_f[pp][:, PK_S2:PK_S2 + 1]).then_inc(z_done, 1)

            def step(Pi, k, pack, slot, third):
                Ci, nxt = chunk0(Pi) + k, (slot + 2) % 3
                before, now, then, ahead = (pack(k + n) for n in (-1, 0, 1, 2))
                inside = not (isinstance(k, int) and k == 0)
                if isinstance(k, int) and k == NCH - 2:
                    act.wait_ge(pack_in[ahead], pack_count(Pi + 1, ahead))
                if inside:
                    relu2(3 * Ci - 2, before, 1)
                prods(Ci, slot, now, 1)
                relu1(Ci + 2, nxt, ahead, 0)
                high(Ci + 3, slot, nth(Pi, third + 1))
                if inside:
                    relu2(3 * Ci - 1, before, 2)
                relu1(Ci + 2, nxt, ahead, 1)
                prods(Ci, slot, now, 2)
                if inside:
                    norm2(Ci - 1, before)
                relu2(3 * Ci, now, 0)
                relu1(Ci + 2, nxt, ahead, 2)
                halo(Ci + 2, nxt, isinstance(k, int) and k == NCH - 2)
                logit(Ci + 2, nxt)
                prods(Ci + 1, (slot + 1) % 3, then, 0)

            act.wait_ge(pack_in[0], 32)
            for k in range(3):
                high(AHEAD + k, k, 16)
            for k in range(2):
                for j in range(UNITS):
                    relu1(AHEAD + k, k, 0, j)
                logit(AHEAD + k, k)
                if k == 0:
                    act.wait_ge(relu1_done, 3 * AHEAD + 3)
                    act.sem_inc(above_done, 1)
                    prods(AHEAD, 0, 0, 0)
            halo(AHEAD + 1, 1)
            run(act, step)

        @block.vector
        def _(dve):
            dve.sem_inc(psd_read, 3 * AHEAD)
            dve.sem_inc(chain, 3 * AHEAD * (NT - 2))
            dve.sem_inc(acc_done, 3 * AHEAD)
            dve.sem_inc(zm_done, AHEAD)
            for buf in x1 + base:
                nc.vector.memset(buf[96:128], 0.0).then_inc(gaps_clear, 1)
            dve.wait_ge(mask_loaded, 32)
            nc.vector.tensor_copy(wm[0][:], wm_raw[:]).then_inc(wm_split, 1)
            dve.wait_ge(wm_split, 1)
            nc.vector.tensor_tensor(wm[1][:], wm_raw[:], wm[0][:], ALU.subtract).then_inc(wm_split, 1)

            def add_tap(Ci, slot, pp, j, i):
                Ui = 3 * Ci + j
                if i == 2 and j == 0:
                    dve.wait_ge(below_done, Ci + 1)
                if i == 0:
                    dve.wait_ge(taps_done, Ui + 1)
                    dve.wait_ge(full_done, Ui - 2)
                elif i == 1:
                    dve.wait_ge(psd_read, Ui + 1)
                else:
                    dve.wait_ge(chain, (NT - 2) * Ui + i - 1)
                ins = nc.vector.scalar_tensor_tensor(rows(acc[j][:]), window(j, slot, DVE_TAPS[i]),
                                                     par(pp, j, TAP + DVE_TAPS[i]),
                                                     banks(psd) if i == 0 else rows(acc[j][:]), ALU.mult, ALU.add)
                ins.then_inc(psd_read if i == 0 else acc_done if i == NT - 1 else chain, 1)

            def masked(Ci, n):
                dve.wait_ge(z_done, Ci + 1)
                dve.wait_ge(out_done, Ci)
                nc.vector.scalar_tensor_tensor(zm[:], logits[n][:], 0.0, z[:], ALU.is_ge, ALU.mult).then_inc(zm_done, 1)

            def step(Pi, k, pack, slot, third):
                Ci, nxt = chunk0(Pi) + k, (slot + 2) % 3
                before, now = pack(k - 1), pack(k)
                inside = not (isinstance(k, int) and k == 0)
                for j in range(UNITS):
                    for i in range(NT - 2):
                        add_tap(Ci, slot, now, j, i)
                        if i < 2 and j > 0:
                            add_tap(Ci, slot, now, j - 1, NT - 2 + i)
                        elif i < 2 and inside:
                            add_tap(Ci - 1, nxt, before, UNITS - 1, NT - 2 + i)
                if inside:
                    masked(Ci - 1, nxt)

            dve.wait_ge(pack_in[0], 32)
            run(dve, step)

        @block.gpsimd
        def _(pool):
            pool.sem_inc(xl_done, AHEAD)
            pool.sem_inc(pair_sum, 3 * AHEAD)
            pool.sem_inc(full_done, 3 * AHEAD)
            pool.sem_inc(out_done, AHEAD)
            nc.gpsimd.memset(zeros[:], 0.0).then_inc(borders, 1)
            nc.gpsimd.memset(h1[:, :, :, :, 0:1], 0.0)
            nc.gpsimd.memset(h1[:, :, :, :, 1 + W:WP], 0.0)
            nc.gpsimd.memset(h1[:, :, 0, 0, 1:1 + W], 0.0).then_inc(borders, 1)
            pool.wait_ge(borders, 2)

            def low(Ci, n):
                pool.wait_ge(xh_done, Ci + 1)
                nc.gpsimd.tensor_tensor(xl[n][:], x1[n][:], xh[n][:], ALU.subtract).then_inc(xl_done, 1)

            def add_pair(Ui, j):
                pool.wait_ge(prod_done, 2 * Ui + 2)
                nc.gpsimd.tensor_tensor(prod[j][0][:], prod[j][0][:], prod[j][1][:], ALU.add).then_inc(pair_sum, 1)

            def gather(Ui, j):
                pool.wait_ge(pair_sum, Ui + 1)
                pool.wait_ge(acc_done, Ui + 1)
                pool.wait_ge(relu2_done, Ui - 2)
                nc.gpsimd.tensor_tensor(full[j][:], acc[j][:], prod[j][0][:], ALU.add).then_inc(full_done, 1)

            def add_base(Ci, n, loads):
                pool.wait_ge(zm_done, Ci + 1)
                pool.wait_ge(base_in[n], loads)
                pool.wait_ge(out_stored[n], loads)
                nc.gpsimd.tensor_tensor(outb[n][:], zm[:], base[n][:], ALU.add).then_inc(out_done, 1)

            def step(Pi, k, pack, slot, third):
                Ci, nxt = chunk0(Pi) + k, (slot + 2) % 3
                inside = not (isinstance(k, int) and k == 0)
                add_pair(3 * Ci, 0)
                if inside:
                    gather(3 * Ci - 1, 2)
                add_pair(3 * Ci + 1, 1)
                low(Ci + 3, slot)
                gather(3 * Ci, 0)
                add_pair(3 * Ci + 2, 2)
                gather(3 * Ci + 1, 1)
                if inside:
                    add_base(Ci - 1, nxt, nth(Pi, third if slot else third - 1))

            for k in range(3):
                low(AHEAD + k, k)
            run(pool, step)


def build(nc, x_steps, x_lanes, w_gates, w_kinds, w_proj, norms, consts, w_sal, b_sal, hid, w_pw1, w_mask, b_mask, out):
    h_rows = nc.dram_tensor("h_rows", [H // 2, 2, HC, 2, B, W], F32).ap()
    x1_lanes = nc.dram_tensor("x1_lanes", [HI + C, HB * PX + AGAIN * CPX], F32).ap()
    packs_r = nc.dram_tensor("packs_r", [2 * HB + 1, P, PKR], F32).ap()
    packs_f = nc.dram_tensor("packs_f", [2 * HB + 1, P, PKF], F32).ap()
    recurrence(nc, x_steps, w_gates, w_kinds, h_rows)
    with ExitStack() as ctx:
        def sb(name, shape, dt=F32):
            return ctx.enter_context(nc.sbuf_tensor(name, shape, dt))

        sums = sb("sums", [P, HB])
        folded = sb("folded", [P, 2, 8])
        passes = sb("passes", [1, 1], I32)
        x1_stored = ctx.enter_context(nc.semaphore("x1_stored"))
        packs_stored = [ctx.enter_context(nc.semaphore(f"packs_stored{n}")) for n in range(2)]
        pack_r = [sb(f"pack_r{n}", [P, PKR], F32R) for n in range(2)]
        pack_f = [sb(f"pack_f{n}", [P, PKF]) for n in range(2)]
        with ExitStack() as own:
            y = own.enter_context(nc.sbuf_tensor("y", [P, HB, H, W], F32))
            stats = own.enter_context(nc.sbuf_tensor("stats", [P, 6 * H], F32))
            projection(nc, h_rows, w_proj, y, stats)
            cst = own.enter_context(nc.sbuf_tensor("cst", [P, CONSTS], F32))
            par = own.enter_context(nc.sbuf_tensor("par", [HG, NG, NPAR], F32))
            w1 = own.enter_context(nc.sbuf_tensor("w1", [HG, NG, 64], F32))
            place = own.enter_context(nc.sbuf_tensor("place", [HG, NG, B], F32))
            ws = own.enter_context(nc.sbuf_tensor("ws", [P, 2, NG, HG], F32))
            bs = own.enter_context(nc.sbuf_tensor("bs", [HG, NG], F32))
            loaded = own.enter_context(nc.semaphore("selection_loaded"))

            def prefetch(sp):
                for to, src in ((cst, consts), (ws, w_sal), (bs, b_sal), (par, hid), (w1, w_pw1)):
                    sp.dma_start(to[:], src).then_inc(loaded, 16)

            residual(nc, y, stats, consts, norms, x_lanes, x1_lanes, sums, folded, x1_stored, prefetch)
            selection(nc, sums, folded, cst, ws, bs, par, loaded, place, passes, y, x1_lanes, x1_stored)
            for q in range(2):
                gather(nc, q, cst, par, w1, place, folded, pack_r, pack_f, packs_r, packs_f, packs_stored, passes, y,
                       x1_lanes, x1_stored)
        bottleneck(nc, w_mask, b_mask, x1_lanes, out, packs_r, packs_f, passes, packs_stored)


def kernel(x, L0_conv_w_f, L0_conv_b_f, L0_conv_w_b, L0_conv_b_b, L0_conv_w_proj, L0_conv_gamma, L0_conv_beta,
           L1_conv_w_pw1, L1_conv_bn1_g, L1_conv_bn1_b, L1_conv_bn1_m, L1_conv_bn1_v, L1_conv_w_dw,
           L1_conv_bnd_g, L1_conv_bnd_b, L1_conv_bnd_m, L1_conv_bnd_v, L1_conv_w_pw2,
           L1_conv_bn2_g, L1_conv_bn2_b, L1_conv_bn2_m, L1_conv_bn2_v, L1_conv_w_mask, L1_conv_b_mask,
           L1_conv_w_sal, L1_conv_b_sal):
    import concourse.bacc as bacc
    from concourse.bass_utils import run_bass_kernel_spmd

    def arr(a):
        return np.ascontiguousarray(a)

    def halves(a):
        out = np.zeros((P,) + a.shape[1:], np.float32)
        out[LO:LO + C] = a
        out[HI:HI + C] = a
        return out

    w_gates = np.zeros((P, 7, 2, 2, P), np.float32)
    for d, (w, b) in enumerate(((L0_conv_w_f, L0_conv_b_f), (L0_conv_w_b, L0_conv_b_b))):
        w, b = arr(w)[:, :, 1], arr(b)
        for m in range(2):
            for col, gate in ((0, 2 * m), (64, 2 * m + 1)):
                g = slice(HC * gate, HC * gate + HC)
                cols = slice(col, col + HC)
                for tap in range(3):
                    wx, wh = w[g, :C, tap].T, w[g, C:, tap].T
                    w_gates[tap:96:3, 0, d, m, cols] = wx[0:32]
                    w_gates[0:HC, 1 + tap, d, m, cols] = wh
                    w_gates[48:112, 1 + tap, d, m, cols] = np.repeat(wx[0:32], 2, axis=0)
                    w_gates[112:128, 1 + tap, d, m, cols] = wx[32:48]
                    w_gates[0:HC, 4 + tap, d, m, cols] = wh
                    w_gates[HI:HI + HC, 4 + tap, d, m, cols] = wh
                    w_gates[48:64, 4 + tap, d, m, cols] = np.repeat(wx[32:40], 2, axis=0)
                    w_gates[112:128, 4 + tap, d, m, cols] = np.repeat(wx[40:48], 2, axis=0)
                w_gates[96:98, 0, d, m, cols] = b[g]
    w_gates = w_gates.reshape(P, 7, 4, P)
    w_kinds = np.zeros((P, 2, 2), np.float32)
    w_kinds[0:96, 0, 0] = 1.0
    w_kinds[97, 0, 0] = 1.0
    w_kinds[0:HC, 0, 1] = 1.0
    w_kinds[112:128, 0, 1] = 1.0
    w_kinds[:, 1] = 1.0 - 2.0 * w_kinds[:, 0]
    w_proj = np.zeros((P, 64), np.float32)
    w_proj[0:HC, 0:C] = arr(L0_conv_w_proj)[:, :HC].T
    w_proj[HI:HI + HC, 0:C] = arr(L0_conv_w_proj)[:, HC:].T

    norms = np.zeros((P, 4, 8), np.float32)
    for kind, (one, mid, two) in enumerate(((L1_conv_bn1_v, L1_conv_bnd_v, L1_conv_bn2_v),
                                            (L1_conv_bn1_g, L1_conv_bnd_g, L1_conv_bn2_g),
                                            (L1_conv_bn1_b, L1_conv_bnd_b, L1_conv_bn2_b),
                                            (L1_conv_bn1_m, L1_conv_bnd_m, L1_conv_bn2_m))):
        norms[0:HG, kind, 0:NG] = arr(one).reshape(NG, HG).T
        norms[0:HG, kind, NG:2 * NG] = arr(mid).reshape(NG, HG).T
        norms[:, kind, 6] = halves(arr(two))
    norms[:, 1, 7] = halves(arr(L0_conv_gamma))
    norms[:, 2, 7] = halves(arr(L0_conv_beta))

    units = 2 * UNITS
    consts = np.zeros((P, 3 * P + HG + units * UC), np.float32)
    for half in range(2):
        for other in range(2):
            consts[64 * half + np.arange(C), 64 * other + np.arange(C)] = 0.5
    consts[np.arange(P), P + np.arange(P)] = 1.0
    consts[:, 2 * P:3 * P] = 1.0
    consts[0:HG, 3 * P:3 * P + HG] = np.triu(np.ones((HG, HG), np.float32), 1)
    place = np.full((units, UC), -2.0, np.float32)
    place[:, :C] = np.arange(units * C).reshape(units, C)
    consts[:, 3 * P + HG:] = place.reshape(-1)

    w_sal = np.zeros((P, 2, NG, HG), np.float32)
    sal_t = arr(L1_conv_w_sal).T.reshape(C, NG, HG)
    w_sal[LO:LO + C, 0] = sal_t
    w_sal[HI:HI + C, 1] = sal_t
    b_sal = arr(arr(L1_conv_b_sal).reshape(NG, HG).T)
    hid = np.zeros((HG, NG, NPAR), np.float32)
    hid[:, :, TAP:TAP + 9] = arr(L1_conv_w_dw).reshape(NG, HG, 9).transpose(1, 0, 2)
    hid[:, :, W2:W2 + C] = arr(L1_conv_w_pw2).T.reshape(NG, HG, C).transpose(1, 0, 2)
    w_pw1 = np.zeros((HG, NG, 64), np.float32)
    w_pw1[:, :, :C] = arr(L1_conv_w_pw1).reshape(NG, HG, C).transpose(1, 0, 2)
    w_mask = np.zeros((P, P), np.float32)
    w_mask[LO:LO + C, LO:LO + C] = arr(L1_conv_w_mask).reshape(C, 1)
    w_mask[HI:HI + C, HI:HI + C] = arr(L1_conv_w_mask).reshape(C, 1)
    b_mask = np.zeros((P, 1), np.float32)
    b_mask[:] = arr(L1_conv_b_mask)

    x = arr(x)
    x_steps = np.zeros((H, HI + C, B, W), np.float32)
    x_steps[:, LO:LO + C] = x.transpose(2, 1, 0, 3)
    x_steps[:, HI:HI + C] = x.transpose(2, 1, 0, 3)[::-1]
    ins = {
        "x_steps": x_steps,
        "x_lanes": arr(x.reshape(2, HB, C, PX).transpose(0, 2, 1, 3).reshape(2, C, HB * PX)),
        "w_gates": w_gates, "w_kinds": w_kinds, "w_proj": w_proj, "norms": norms, "consts": consts, "w_sal": w_sal, "b_sal": b_sal,
        "hid": hid, "w_pw1": w_pw1, "w_mask": w_mask, "b_mask": b_mask,
    }
    nc = bacc.Bacc("TRN2", target_bir_lowering=False, num_devices=1)
    args = [nc.dram_tensor(name, a.shape, mybir.dt.from_np(a.dtype), kind="ExternalInput").ap() for name, a in ins.items()]
    args.append(nc.dram_tensor("out", (HI + C, HB * PX), F32, kind="ExternalOutput").ap())
    build(nc, *args)
    r = run_bass_kernel_spmd(nc, [ins], core_ids=[0])
    got = r.results[0]["out"].reshape(HI + C, HB, H, W)
    return np.concatenate([got[first:first + C].transpose(1, 0, 2, 3) for first in (LO, HI)])
```
